# Optimizing a Trainium2 kernel written in Bass

```python
import numpy as np
import jax
import jax.numpy as jnp

def _softmax(x, axis=-1):
    return jax.nn.softmax(x, axis=axis)

def _gelu(x):
    return jax.nn.gelu(x, approximate=True)

def _silu(x):
    return jax.nn.silu(x)

def _sigmoid(x):
    return jax.nn.sigmoid(x)

def _layernorm(x, axis=-1, eps=1e-05):
    m = jnp.mean(x, axis=axis, keepdims=True)
    v = jnp.var(x, axis=axis, keepdims=True)
    return (x - m) / jnp.sqrt(v + eps)

def _scatter_add(tgt, idx, src, axis=0):
    return tgt.at[idx].add(src)

def _segment_sum(src, seg, n):
    return jax.ops.segment_sum(src, seg, n)
kernel_name = 'mk_gnn_ffn_d4_gnn_r32_202eb6'

def setup_inputs(seed: int=0):
    np.random.seed(seed)
    _w = jnp.asarray

    def _rec_inputs():
        import jax
        import jax.numpy as jnp
        _gk = jax.random.key(seed)
        x = -0.0003713 + 1 * jax.random.normal(jax.random.fold_in(_gk, 1), (3125, 256), jnp.float32)
        src = jax.random.randint(jax.random.fold_in(_gk, 2), (50000,), 0, 3125, jnp.int32)
        dst = jax.random.randint(jax.random.fold_in(_gk, 3), (50000,), 0, 3125, jnp.int32)
        _o = jnp.argsort(dst, stable=True)
        src = src[_o]
        dst = dst[_o]
        return (x, src, dst)
    x, src, dst = _rec_inputs()

    def _L0_gnn_setup():
        import jax, jax.numpy as jnp
        import numpy as np
        N_NODES = 50000
        N_EDGES = 25000
        F_IN = 256
        HEADS = 4
        C_OUT = 64
        NEG_SLOPE = 0.2
        key = jax.random.key(seed)
        k0, k1, k2, k3, k4, k5 = jax.random.split(key, 6)
        x = jax.random.normal(k0, (N_NODES, F_IN), dtype=jnp.float32)
        edge_index = jax.random.randint(k1, (2, N_EDGES), 0, N_NODES, dtype=jnp.int64)
        s = 1.0 / np.sqrt(F_IN)
        W = jax.random.uniform(k2, (HEADS * C_OUT, F_IN), minval=-s, maxval=s, dtype=jnp.float32)
        att_src = jax.random.normal(k3, (HEADS, C_OUT), dtype=jnp.float32) * 0.1
        att_dst = jax.random.normal(k4, (HEADS, C_OUT), dtype=jnp.float32) * 0.1
        bias = jnp.zeros((HEADS * C_OUT,), dtype=jnp.float32)
        return {'x': x, 'edge_index': edge_index, 'W': W, 'att_src': att_src, 'att_dst': att_dst, 'bias': bias}
    _L0_gnn_all = _L0_gnn_setup()
    _L0_gnn_in = {k: v for k, v in _L0_gnn_all.items() if k in ('W', 'att_src', 'att_dst', 'bias')}
    del _L0_gnn_all

    def _L0_ffn_setup():
        import jax, jax.numpy as jnp
        import numpy as np
        NUM_EXPERTS = 8
        TOP_K = 2
        B, S, D = (8, 256, 256)

        def _moe(tokens, router_w, w1, b1, w2, b2):
            N = tokens.shape[0]
            E = router_w.shape[0]
            logits = tokens.astype(jnp.float32) @ router_w.astype(jnp.float32).T
            probs = jax.nn.softmax(logits, axis=-1)
            rw, re = jax.lax.top_k(probs, TOP_K)
            if TOP_K > 1:
                rw = rw / jnp.maximum(rw.sum(-1, keepdims=True), 1e-12)
            rw = rw.astype(tokens.dtype)
            combine = jnp.zeros((N, E), tokens.dtype).at[jnp.arange(N)[:, None], re].set(rw)
            out = tokens
            for e in range(E):
                h = jax.nn.gelu(tokens @ w1[e] + b1[e], approximate=False)
                y = h @ w2[e] + b2[e]
                out = out + combine[:, e:e + 1] * y
            return out
        key = jax.random.key(seed)
        ks = jax.random.split(key, 4)
        scale = 1.0 / np.sqrt(D).astype(np.float32)
        return {'input_embeddings': jax.random.normal(ks[0], (B, S, D), jnp.float32), 'router_w': jax.random.normal(ks[1], (NUM_EXPERTS, D), jnp.float32) * scale, 'w1': jax.random.normal(ks[2], (NUM_EXPERTS, D, D), jnp.float32) * scale, 'b1': jnp.zeros((NUM_EXPERTS, D), jnp.float32), 'w2': jax.random.normal(ks[3], (NUM_EXPERTS, D, D), jnp.float32) * scale, 'b2': jnp.zeros((NUM_EXPERTS, D), jnp.float32)}
    _L0_ffn_all = _L0_ffn_setup()
    _L0_ffn_in = {k: v for k, v in _L0_ffn_all.items() if k in ('router_w', 'w1', 'b1', 'w2', 'b2')}
    del _L0_ffn_all

    def _L1_gnn_setup():
        import jax, jax.numpy as jnp
        import numpy as np
        N = 50000
        E_RAND = 25000
        IN, HID, H, OUT = (256, 64, 4, 256)
        NEG_SLOPE = 0.2

        def gat_layer(h, W, a_src, a_dst, src, dst, concat):
            n = h.shape[0]
            nh, nf = a_src.shape
            hp = (h @ W.T).reshape(n, nh, nf)
            e = (hp[src] * a_src).sum(-1) + (hp[dst] * a_dst).sum(-1)
            e = jnp.where(e > 0, e, NEG_SLOPE * e)
            e_max = jax.ops.segment_max(e, dst, num_segments=n)
            ex = jnp.exp(e - e_max[dst])
            e_sum = jax.ops.segment_sum(ex, dst, num_segments=n)
            alpha = ex / (e_sum[dst] + 1e-16)
            out = jax.ops.segment_sum(hp[src] * alpha[..., None], dst, num_segments=n)
            return out.reshape(n, nh * nf) if concat else out.mean(axis=1)
        key = jax.random.key(seed)
        ks = jax.random.split(key, 8)
        x = jax.random.normal(ks[0], (N, IN), dtype=jnp.float32)
        er = jax.random.randint(ks[1], (2, E_RAND), 0, N, dtype=jnp.int32)
        loops = jnp.arange(N, dtype=jnp.int32)
        edge_index = jnp.concatenate([er, jnp.stack([loops, loops])], axis=1)
        W1 = jax.random.normal(ks[2], (H * HID, IN), jnp.float32) * (2.0 / (IN + H * HID)) ** 0.5
        a1_src = jax.random.normal(ks[3], (H, HID), jnp.float32) * 0.1
        a1_dst = jax.random.normal(ks[4], (H, HID), jnp.float32) * 0.1
        W2 = jax.random.normal(ks[5], (OUT, H * HID), jnp.float32) * (2.0 / (H * HID + OUT)) ** 0.5
        a2_src = jax.random.normal(ks[6], (1, OUT), jnp.float32) * 0.1
        a2_dst = jax.random.normal(ks[7], (1, OUT), jnp.float32) * 0.1
        return {'x': x, 'edge_index': edge_index, 'W1': W1, 'a1_src': a1_src, 'a1_dst': a1_dst, 'W2': W2, 'a2_src': a2_src, 'a2_dst': a2_dst}
    _L1_gnn_all = _L1_gnn_setup()
    _L1_gnn_in = {k: v for k, v in _L1_gnn_all.items() if k in ('W1', 'a1_src', 'a1_dst', 'W2', 'a2_src', 'a2_dst')}
    del _L1_gnn_all

    def _L1_ffn_setup():
        import jax, jax.numpy as jnp
        import numpy as np
        from jax import lax
        key = jax.random.key(seed)
        B, T, I, H = (64, 64, 256, 256)
        ks = jax.random.split(key, 13)
        s = 1.0 / np.sqrt(H)

        def w(k, shape):
            return jax.random.uniform(k, shape, jnp.float32, -s, s)
        return {'x': jax.random.normal(ks[0], (B, T, I), jnp.float32), 'U_i': w(ks[1], (I, H)), 'V_i': w(ks[2], (H, H)), 'b_i': w(ks[3], (H,)), 'U_f': w(ks[4], (I, H)), 'V_f': w(ks[5], (H, H)), 'b_f': w(ks[6], (H,)), 'U_c': w(ks[7], (I, H)), 'V_c': w(ks[8], (H, H)), 'b_c': w(ks[9], (H,)), 'U_o': w(ks[10], (I, H)), 'V_o': w(ks[11], (H, H)), 'b_o': w(ks[12], (H,))}
    _L1_ffn_all = _L1_ffn_setup()
    _L1_ffn_in = {k: v for k, v in _L1_ffn_all.items() if k in ('U_i', 'V_i', 'b_i', 'U_f', 'V_f', 'b_f', 'U_c', 'V_c', 'b_c', 'U_o', 'V_o', 'b_o')}
    del _L1_ffn_all

    def _L2_gnn_setup():
        import jax, jax.numpy as jnp
        import numpy as np

        def gcn_layer(h, src, dst, norm, n, W, b):
            h = h @ W
            msg = h[src] * norm[:, None]
            agg = jax.ops.segment_sum(msg, dst, num_segments=n)
            return agg + b
        key = jax.random.key(seed)
        ks = jax.random.split(key, 8)
        N, E, D, H = (50000, 25000, 256, 256)
        x = jax.random.normal(ks[0], (N, D), dtype=jnp.float32)
        edge_index = jax.random.randint(ks[1], (2, E), 0, N, dtype=jnp.int32)
        batch = jnp.zeros((N,), dtype=jnp.int32)
        s = 1.0 / np.sqrt(D)
        W1 = jax.random.normal(ks[2], (D, H), dtype=jnp.float32) * s
        b1 = jnp.zeros((H,), dtype=jnp.float32)
        W2 = jax.random.normal(ks[3], (H, H), dtype=jnp.float32) * s
        b2 = jnp.zeros((H,), dtype=jnp.float32)
        W3 = jax.random.normal(ks[4], (H, H), dtype=jnp.float32) * s
        b3 = jnp.zeros((H,), dtype=jnp.float32)
        return {'x': x, 'edge_index': edge_index, 'batch': batch, 'W1': W1, 'b1': b1, 'W2': W2, 'b2': b2, 'W3': W3, 'b3': b3}
    _L2_gnn_all = _L2_gnn_setup()
    _L2_gnn_in = {k: v for k, v in _L2_gnn_all.items() if k in ('W1', 'b1', 'W2', 'b2', 'W3', 'b3')}
    del _L2_gnn_all

    def _L2_ffn_setup():
        import jax, jax.numpy as jnp
        import numpy as np
        TOP_K = 2
        LN_EPS = 1e-05
        key = jax.random.key(seed)
        ks = jax.random.split(key, 8)
        B, S, D, E, H = (16, 1024, 256, 8, 1024)
        x = jax.random.normal(ks[0], (B, S, D), dtype=jnp.float32)
        Wr = jax.random.normal(ks[1], (D, E), dtype=jnp.float32) * 0.1
        br = jnp.zeros((E,), dtype=jnp.float32)
        ln_g = jnp.ones((E, D), dtype=jnp.float32)
        ln_b = jnp.zeros((E, D), dtype=jnp.float32)
        W1 = jax.random.normal(ks[2], (E, D, H), dtype=jnp.float32) * (1.0 / np.sqrt(D))
        b1 = jnp.zeros((E, H), dtype=jnp.float32)
        W2 = jax.random.normal(ks[3], (E, H, D), dtype=jnp.float32) * (1.0 / np.sqrt(H))
        b2 = jnp.zeros((E, D), dtype=jnp.float32)
        return {'x': x, 'Wr': Wr, 'br': br, 'ln_g': ln_g, 'ln_b': ln_b, 'W1': W1, 'b1': b1, 'W2': W2, 'b2': b2}
    _L2_ffn_all = _L2_ffn_setup()
    _L2_ffn_in = {k: v for k, v in _L2_ffn_all.items() if k in ('Wr', 'br', 'ln_g', 'ln_b', 'W1', 'b1', 'W2', 'b2')}
    del _L2_ffn_all

    def _L3_gnn_setup():
        import jax, jax.numpy as jnp
        import numpy as np
        N_NODES = 50000
        key = jax.random.key(seed)
        k1, k2, k3 = jax.random.split(key, 3)
        x = jax.random.normal(k1, (N_NODES, 256), dtype=jnp.float32)
        W = jax.random.normal(k2, (256, 256), dtype=jnp.float32) * (1.0 / np.sqrt(256))
        edge_index = jax.random.randint(k3, (2, 50000), 0, N_NODES, dtype=jnp.int64)
        return {'x': x, 'W': W, 'edge_index': edge_index}
    _L3_gnn_all = _L3_gnn_setup()
    _L3_gnn_in = {k: v for k, v in _L3_gnn_all.items() if k in ('W',)}
    del _L3_gnn_all

    def _L3_ffn_setup():
        import jax, jax.numpy as jnp
        import numpy as np
        B, S, D, E, H, K = (4, 128, 256, 8, 512, 2)
        key = jax.random.key(seed)
        ks = jax.random.split(key, 6)
        x = jax.random.normal(ks[0], (B, S, D), jnp.float32)
        Wg = jax.random.normal(ks[1], (D, E), jnp.float32) * 0.02
        bg = jnp.zeros((E,), jnp.float32)
        W1 = jax.random.normal(ks[2], (E, D, H), jnp.float32) * 0.02
        b1 = jnp.zeros((E, H), jnp.float32)
        W2 = jax.random.normal(ks[3], (E, H, D), jnp.float32) * 0.02
        b2 = jnp.zeros((E, D), jnp.float32)
        return {'x': x, 'Wg': Wg, 'bg': bg, 'W1': W1, 'b1': b1, 'W2': W2, 'b2': b2}
    _L3_ffn_all = _L3_ffn_setup()
    _L3_ffn_in = {k: v for k, v in _L3_ffn_all.items() if k in ('Wg', 'bg', 'W1', 'b1', 'W2', 'b2')}
    del _L3_ffn_all
    return {'x': x, 'src': src, 'dst': dst, 'L0_gnn_W': _L0_gnn_in['W'], 'L0_gnn_att_src': _L0_gnn_in['att_src'], 'L0_gnn_att_dst': _L0_gnn_in['att_dst'], 'L0_gnn_bias': _L0_gnn_in['bias'], 'L0_ffn_router_w': _L0_ffn_in['router_w'], 'L0_ffn_w1': _L0_ffn_in['w1'], 'L0_ffn_b1': _L0_ffn_in['b1'], 'L0_ffn_w2': _L0_ffn_in['w2'], 'L0_ffn_b2': _L0_ffn_in['b2'], 'L1_gnn_W1': _L1_gnn_in['W1'], 'L1_gnn_a1_src': _L1_gnn_in['a1_src'], 'L1_gnn_a1_dst': _L1_gnn_in['a1_dst'], 'L1_gnn_W2': _L1_gnn_in['W2'], 'L1_gnn_a2_src': _L1_gnn_in['a2_src'], 'L1_gnn_a2_dst': _L1_gnn_in['a2_dst'], 'L1_ffn_U_i': _L1_ffn_in['U_i'], 'L1_ffn_V_i': _L1_ffn_in['V_i'], 'L1_ffn_b_i': _L1_ffn_in['b_i'], 'L1_ffn_U_f': _L1_ffn_in['U_f'], 'L1_ffn_V_f': _L1_ffn_in['V_f'], 'L1_ffn_b_f': _L1_ffn_in['b_f'], 'L1_ffn_U_c': _L1_ffn_in['U_c'], 'L1_ffn_V_c': _L1_ffn_in['V_c'], 'L1_ffn_b_c': _L1_ffn_in['b_c'], 'L1_ffn_U_o': _L1_ffn_in['U_o'], 'L1_ffn_V_o': _L1_ffn_in['V_o'], 'L1_ffn_b_o': _L1_ffn_in['b_o'], 'L2_gnn_W1': _L2_gnn_in['W1'], 'L2_gnn_b1': _L2_gnn_in['b1'], 'L2_gnn_W2': _L2_gnn_in['W2'], 'L2_gnn_b2': _L2_gnn_in['b2'], 'L2_gnn_W3': _L2_gnn_in['W3'], 'L2_gnn_b3': _L2_gnn_in['b3'], 'L2_ffn_Wr': _L2_ffn_in['Wr'], 'L2_ffn_br': _L2_ffn_in['br'], 'L2_ffn_ln_g': _L2_ffn_in['ln_g'], 'L2_ffn_ln_b': _L2_ffn_in['ln_b'], 'L2_ffn_W1': _L2_ffn_in['W1'], 'L2_ffn_b1': _L2_ffn_in['b1'], 'L2_ffn_W2': _L2_ffn_in['W2'], 'L2_ffn_b2': _L2_ffn_in['b2'], 'L3_gnn_W': _L3_gnn_in['W'], 'L3_ffn_Wg': _L3_ffn_in['Wg'], 'L3_ffn_bg': _L3_ffn_in['bg'], 'L3_ffn_W1': _L3_ffn_in['W1'], 'L3_ffn_b1': _L3_ffn_in['b1'], 'L3_ffn_W2': _L3_ffn_in['W2'], 'L3_ffn_b2': _L3_ffn_in['b2']}

def reference(x, src, dst, L0_gnn_W, L0_gnn_att_src, L0_gnn_att_dst, L0_gnn_bias, L0_ffn_router_w, L0_ffn_w1, L0_ffn_b1, L0_ffn_w2, L0_ffn_b2, L1_gnn_W1, L1_gnn_a1_src, L1_gnn_a1_dst, L1_gnn_W2, L1_gnn_a2_src, L1_gnn_a2_dst, L1_ffn_U_i, L1_ffn_V_i, L1_ffn_b_i, L1_ffn_U_f, L1_ffn_V_f, L1_ffn_b_f, L1_ffn_U_c, L1_ffn_V_c, L1_ffn_b_c, L1_ffn_U_o, L1_ffn_V_o, L1_ffn_b_o, L2_gnn_W1, L2_gnn_b1, L2_gnn_W2, L2_gnn_b2, L2_gnn_W3, L2_gnn_b3, L2_ffn_Wr, L2_ffn_br, L2_ffn_ln_g, L2_ffn_ln_b, L2_ffn_W1, L2_ffn_b1, L2_ffn_W2, L2_ffn_b2, L3_gnn_W, L3_ffn_Wg, L3_ffn_bg, L3_ffn_W1, L3_ffn_b1, L3_ffn_W2, L3_ffn_b2):
    import jax
    import jax.numpy as jnp

    def _L0_gnn_ref(x, edge_index, W, att_src, att_dst, bias):
        import jax, jax.numpy as jnp
        import numpy as np
        N_NODES = 50000
        N_EDGES = 25000
        F_IN = 256
        HEADS = 4
        C_OUT = 64
        NEG_SLOPE = 0.2
        N = x.shape[0]
        H, C = att_src.shape
        loops = jnp.arange(N, dtype=edge_index.dtype)
        src = jnp.concatenate([edge_index[0], loops])
        dst = jnp.concatenate([edge_index[1], loops])
        h = (x @ W.T).reshape(N, H, C)
        a_s = jnp.einsum('nhc,hc->nh', h, att_src)
        a_d = jnp.einsum('nhc,hc->nh', h, att_dst)
        e = jax.nn.leaky_relu(a_s[src] + a_d[dst], NEG_SLOPE)
        m = jax.ops.segment_max(e, dst, num_segments=N)
        m = jnp.where(jnp.isfinite(m), m, 0.0)
        p = jnp.exp(e - m[dst])
        denom = jax.ops.segment_sum(p, dst, num_segments=N)
        alpha = p / (denom[dst] + 1e-16)
        msg = alpha[:, :, None] * h[src]
        out = jax.ops.segment_sum(msg, dst, num_segments=N)
        out = out.reshape(N, H * C) + bias
        out = jax.nn.elu(out) + x
        return out

    def _L0_ffn_ref(input_embeddings, router_w, w1, b1, w2, b2):
        import jax, jax.numpy as jnp
        import numpy as np
        NUM_EXPERTS = 8
        TOP_K = 2
        B, S, D = (8, 256, 256)

        def _moe(tokens, router_w, w1, b1, w2, b2):
            N = tokens.shape[0]
            E = router_w.shape[0]
            logits = tokens.astype(jnp.float32) @ router_w.astype(jnp.float32).T
            probs = jax.nn.softmax(logits, axis=-1)
            rw, re = jax.lax.top_k(probs, TOP_K)
            if TOP_K > 1:
                rw = rw / jnp.maximum(rw.sum(-1, keepdims=True), 1e-12)
            rw = rw.astype(tokens.dtype)
            combine = jnp.zeros((N, E), tokens.dtype).at[jnp.arange(N)[:, None], re].set(rw)
            out = tokens
            for e in range(E):
                h = jax.nn.gelu(tokens @ w1[e] + b1[e], approximate=False)
                y = h @ w2[e] + b2[e]
                out = out + combine[:, e:e + 1] * y
            return out
        b, s, d = input_embeddings.shape
        tokens = input_embeddings.reshape(b * s, d)
        return _moe(tokens, router_w, w1, b1, w2, b2).reshape(b, s, d)

    def _L1_gnn_ref(x, edge_index, W1, a1_src, a1_dst, W2, a2_src, a2_dst):
        import jax, jax.numpy as jnp
        import numpy as np
        N = 50000
        E_RAND = 25000
        IN, HID, H, OUT = (256, 64, 4, 256)
        NEG_SLOPE = 0.2

        def gat_layer(h, W, a_src, a_dst, src, dst, concat):
            n = h.shape[0]
            nh, nf = a_src.shape
            hp = (h @ W.T).reshape(n, nh, nf)
            e = (hp[src] * a_src).sum(-1) + (hp[dst] * a_dst).sum(-1)
            e = jnp.where(e > 0, e, NEG_SLOPE * e)
            e_max = jax.ops.segment_max(e, dst, num_segments=n)
            ex = jnp.exp(e - e_max[dst])
            e_sum = jax.ops.segment_sum(ex, dst, num_segments=n)
            alpha = ex / (e_sum[dst] + 1e-16)
            out = jax.ops.segment_sum(hp[src] * alpha[..., None], dst, num_segments=n)
            return out.reshape(n, nh * nf) if concat else out.mean(axis=1)
        src, dst = (edge_index[0], edge_index[1])
        h = jax.nn.relu(gat_layer(x, W1, a1_src, a1_dst, src, dst, True))
        return gat_layer(h, W2, a2_src, a2_dst, src, dst, False)

    def _L1_ffn_ref(x, U_i, V_i, b_i, U_f, V_f, b_f, U_c, V_c, b_c, U_o, V_o, b_o):
        import jax, jax.numpy as jnp
        import numpy as np
        from jax import lax
        B, T, _ = x.shape
        H = U_i.shape[1]
        xt = jnp.swapaxes(x, 0, 1)
        xi = xt @ U_i + b_i
        xf = xt @ U_f + b_f
        xg = xt @ U_c + b_c
        xo = xt @ U_o + b_o
        h0 = jnp.zeros((B, H), x.dtype)
        c0 = jnp.zeros((B, H), x.dtype)

        def step(carry, xs):
            h, c = carry
            xi_t, xf_t, xg_t, xo_t = xs
            i_t = jax.nn.sigmoid(xi_t + h @ V_i)
            f_t = jax.nn.sigmoid(xf_t + h @ V_f)
            g_t = jnp.tanh(xg_t + h @ V_c)
            o_t = jax.nn.sigmoid(xo_t + h @ V_o)
            c_new = h * c + i_t * g_t
            h_new = o_t * jnp.tanh(c_new)
            return ((h_new, c_new), h_new)
        (_, _), hs = lax.scan(step, (h0, c0), (xi, xf, xg, xo))
        return jnp.swapaxes(hs, 0, 1)

    def _L2_gnn_ref(x, edge_index, batch, W1, b1, W2, b2, W3, b3):
        import jax, jax.numpy as jnp
        import numpy as np

        def gcn_layer(h, src, dst, norm, n, W, b):
            h = h @ W
            msg = h[src] * norm[:, None]
            agg = jax.ops.segment_sum(msg, dst, num_segments=n)
            return agg + b
        n = x.shape[0]
        loop = jnp.arange(n, dtype=edge_index.dtype)
        src = jnp.concatenate([edge_index[0], loop])
        dst = jnp.concatenate([edge_index[1], loop])
        deg = jax.ops.segment_sum(jnp.ones_like(dst, dtype=x.dtype), dst, num_segments=n)
        disq = jnp.where(deg > 0, deg ** (-0.5), 0.0)
        norm = disq[src] * disq[dst]
        h = gcn_layer(x, src, dst, norm, n, W1, b1)
        h = jax.nn.relu(h)
        h = gcn_layer(h, src, dst, norm, n, W2, b2)
        h = jax.nn.relu(h)
        h = gcn_layer(h, src, dst, norm, n, W3, b3)
        return h

    def _L2_ffn_ref(x, Wr, br, ln_g, ln_b, W1, b1, W2, b2):
        import jax, jax.numpy as jnp
        import numpy as np
        TOP_K = 2
        LN_EPS = 1e-05
        B, S, D = x.shape
        N = B * S
        xt = x.reshape(N, D)
        logits = xt @ Wr + br
        probs = jax.nn.softmax(logits, axis=-1)
        top_p, top_idx = jax.lax.top_k(probs, TOP_K)
        weights = top_p / top_p.sum(axis=-1, keepdims=True)
        mu = xt.mean(axis=-1, keepdims=True)
        var = ((xt - mu) ** 2).mean(axis=-1, keepdims=True)
        xn = (xt - mu) * jax.lax.rsqrt(var + LN_EPS)
        xe = xn[None, :, :] * ln_g[:, None, :] + ln_b[:, None, :]
        h = jax.nn.gelu(jnp.einsum('end,edh->enh', xe, W1) + b1[:, None, :], approximate=False)
        y = jnp.einsum('enh,ehd->end', h, W2) + b2[:, None, :]
        y_tok = jnp.transpose(y, (1, 0, 2))
        sel = jnp.take_along_axis(y_tok, top_idx[:, :, None], axis=1)
        out = (weights[:, :, None] * sel).sum(axis=1)
        return out.reshape(B, S, D)

    def _L3_gnn_ref(x, W, edge_index):
        import jax, jax.numpy as jnp
        import numpy as np
        N_NODES = 50000
        N = x.shape[0]
        src, dst = (edge_index[0], edge_index[1])
        h = x @ W
        deg = jax.ops.segment_sum(jnp.ones_like(dst, dtype=h.dtype), dst, num_segments=N)
        deg_inv_sqrt = jnp.where(deg > 0, jax.lax.rsqrt(jnp.maximum(deg, 1)), 0.0)
        norm = deg_inv_sqrt[src] * deg_inv_sqrt[dst]
        msgs = h[src] * norm[:, None]
        out = jax.ops.segment_sum(msgs, dst, num_segments=N)
        return out

    def _L3_ffn_ref(x, Wg, bg, W1, b1, W2, b2):
        import jax, jax.numpy as jnp
        import numpy as np
        B, S, D, E, H, K = (4, 128, 256, 8, 512, 2)
        Bv, Sv, Dv = x.shape
        gate_scores = x @ Wg + bg
        _, idx = jax.lax.top_k(gate_scores, K)
        mask = jax.nn.one_hot(idx, E, dtype=x.dtype).sum(axis=-2)
        xf = x.reshape(-1, Dv)
        mf = mask.reshape(-1, E)
        h = jax.nn.gelu(jnp.einsum('td,edh->teh', xf, W1) + b1[None], approximate=False)
        y = jnp.einsum('teh,ehd->ted', h, W2) + b2[None]
        out = jnp.einsum('ted,te->td', y, mf)
        return out.reshape(Bv, Sv, Dv)
    edge_index = jnp.stack([src, dst])
    batch0 = jnp.zeros((3125,), jnp.int32)
    x = x + _L0_gnn_ref(_layernorm(x, axis=-1), edge_index, L0_gnn_W, L0_gnn_att_src, L0_gnn_att_dst, L0_gnn_bias)
    x = x + _L0_ffn_ref(_layernorm(x, axis=-1)[None], L0_ffn_router_w, L0_ffn_w1, L0_ffn_b1, L0_ffn_w2, L0_ffn_b2)[0]
    x = x + _L1_gnn_ref(_layernorm(x, axis=-1), edge_index, L1_gnn_W1, L1_gnn_a1_src, L1_gnn_a1_dst, L1_gnn_W2, L1_gnn_a2_src, L1_gnn_a2_dst)
    x = x + _L1_ffn_ref(_layernorm(x, axis=-1)[None], L1_ffn_U_i, L1_ffn_V_i, L1_ffn_b_i, L1_ffn_U_f, L1_ffn_V_f, L1_ffn_b_f, L1_ffn_U_c, L1_ffn_V_c, L1_ffn_b_c, L1_ffn_U_o, L1_ffn_V_o, L1_ffn_b_o)[0]
    x = x + _L2_gnn_ref(_layernorm(x, axis=-1), edge_index, batch0, L2_gnn_W1, L2_gnn_b1, L2_gnn_W2, L2_gnn_b2, L2_gnn_W3, L2_gnn_b3)
    x = x + _L2_ffn_ref(_layernorm(x, axis=-1)[None], L2_ffn_Wr, L2_ffn_br, L2_ffn_ln_g, L2_ffn_ln_b, L2_ffn_W1, L2_ffn_b1, L2_ffn_W2, L2_ffn_b2)[0]
    x = x + _L3_gnn_ref(_layernorm(x, axis=-1), L3_gnn_W, edge_index)
    x = x + _L3_ffn_ref(_layernorm(x, axis=-1)[None], L3_ffn_Wg, L3_ffn_bg, L3_ffn_W1, L3_ffn_b1, L3_ffn_W2, L3_ffn_b2)[0]
    return x

_drawn_inputs = setup_inputs


def setup_inputs(seed=0):
    import zlib

    import numpy as np

    out = dict(_drawn_inputs(seed))
    spreads = {'L0_gnn_bias': (0.0, 0.1),
     'L0_ffn_b1': (0.0, 0.37),
     'L0_ffn_b2': (0.0, 0.1),
     'L2_gnn_b1': (0.0, 0.418),
     'L2_gnn_b2': (0.0, 0.281),
     'L2_gnn_b3': (0.0, 0.1),
     'L2_ffn_br': (0.0, 0.287),
     'L2_ffn_ln_g': (1.0, 0.2),
     'L2_ffn_ln_b': (0.0, 0.417),
     'L2_ffn_b1': (0.0, 0.421),
     'L2_ffn_b2': (0.0, 0.288),
     'L3_ffn_bg': (0.0, 0.1),
     'L3_ffn_b1': (0.0, 0.681),
     'L3_ffn_b2': (0.0, 0.1)}
    factors = {'L0_gnn_att_dst': 3.771,
     'L1_gnn_a1_src': 3.098,
     'L1_gnn_a1_dst': 8.0,
     'L1_gnn_a2_src': 8.0,
     'L1_gnn_a2_dst': 8.0,
     'L1_ffn_U_i': 4.139,
     'L1_ffn_V_i': 8.0,
     'L1_ffn_b_i': 24.863,
     'L1_ffn_V_c': 5.985,
     'L1_ffn_b_c': 8.0,
     'L1_ffn_U_o': 3.744,
     'L1_ffn_V_o': 8.0,
     'L1_ffn_b_o': 8.0,
     'L2_gnn_W1': 4.236}
    for name, (base, spread) in spreads.items():
        noise = np.random.default_rng([zlib.crc32(name.encode()), seed]).standard_normal(out[name].shape)
        drawn = base * np.exp(spread * noise) if base else spread * noise
        out[name] = jnp.asarray(drawn.astype(out[name].dtype))
    for name, factor in factors.items():
        out[name] = (out[name] * factor).astype(out[name].dtype)
    return out
```

```python
import concourse.bass as bass
from concourse import mybir
from contextlib import ExitStack, contextmanager

N, E, D = 3125, 50000, 256
P, T = 125, 25
NN = N * N
HUGE = 1.0e30
CAP = 3.0e38
TOL = 2.0 ** -18
EPS = 1e-5


class Unit:

    def __init__(self, sem):
        self.sem, self.count, self.queue = sem, 0, []


class Program:

    NAMES = ("tensor", "vector", "scalar", "gpsimd", "sync")

    def __init__(self, nc, tag, lanes):
        self.nc = nc
        self.units = {n: Unit(nc.alloc_semaphore(f"{tag}_{n}")) for n in self.NAMES}
        self.lanes = [[nc.alloc_semaphore(f"{tag}_dma{i}"), 0] for i in range(lanes)]

    def add(self, name, fn, waits):
        u = self.units[name]
        u.count += 1
        u.queue.append((fn, [w for w in waits if w is not None], u.sem, 1))
        return (u.sem, u.count)

    def pe(self, fn, *waits):
        return self.add("tensor", fn, waits)

    def ve(self, fn, *waits):
        return self.add("vector", fn, waits)

    def se(self, fn, *waits):
        return self.add("scalar", fn, waits)

    def ge(self, fn, *waits):
        return self.add("gpsimd", fn, waits)

    def dma(self, lane, fn, *waits, by="sync"):
        at = self.lanes[lane]
        at[1] += 16
        self.units[by].queue.append((fn, [w for w in waits if w is not None], at[0], 16))
        return (at[0], at[1])

    def hold(self, name, *waits):
        self.units[name].queue.append((None, [w for w in waits if w is not None], None, 0))

    def flush(self):
        nc = self.nc
        with nc.Block() as block:
            for name in self.NAMES:
                queue, self.units[name].queue = self.units[name].queue, []

                def body(e, queue=queue):
                    passed = {}
                    if not queue:
                        e.nop()
                    for fn, waits, sem, by in queue:
                        for s, v in waits:
                            if passed.get(s.num, 0) < v:
                                e.wait_ge(s, v)
                                passed[s.num] = v
                        if fn is not None:
                            fn(e).then_inc(sem, by)

                block_of(block, name)(body)

    def numbers(self):
        nums = [u.sem.num for u in self.units.values()] + [s.num for s, _ in self.lanes]
        assert max(nums) - min(nums) + 1 == len(nums)
        return range(min(nums), max(nums) + 1)

    def rewind(self):
        for u in self.units.values():
            u.count = 0
        for lane in self.lanes:
            lane[1] = 0


def block_of(block, name):
    return {"tensor": block.tensor, "vector": block.vector, "scalar": block.scalar,
            "gpsimd": block.gpsimd, "sync": block.sync}[name]


class Ring:

    def __init__(self, items):
        self.items, self.free, self.at = list(items), [None] * len(items), -1

    def take(self):
        self.at = (self.at + 1) % len(self.items)
        return self.items[self.at], self.free[self.at], self.at

    def give(self, i, mark):
        self.free[i] = mark


def program(nc, a, upto=99, start=0):
    f32, bf16, i32 = mybir.dt.float32, mybir.dt.bfloat16, mybir.dt.int32
    ALU = mybir.AluOpType
    ACT = mybir.ActivationFunctionType
    AX = mybir.AxisListType
    p = Program(nc, "m", 24)
    q = Program(nc, "r", 1)
    top = ExitStack()
    names = [0]

    def sb(ctx, shape, dt=f32):
        names[0] += 1
        return ctx.enter_context(nc.sbuf_tensor(f"sb{names[0]}", shape, dt))

    @contextmanager
    def phase():
        with ExitStack() as ctx:
            yield ctx
            p.flush()

    A1 = nc.dram_tensor("adj", (NN + 128, 1), f32).ap()
    NEG = nc.dram_tensor("neg", (T, P, N), bf16).ap()
    KD = nc.dram_tensor("keys", (P, 400), f32).ap()
    adj = A1[0:NN, :].rearrange("(t p i) o -> t p (i o)", p=P, i=N)

    with top:
        PS = top.enter_context(nc.psum_tensor("ps", [128, 8, 512], f32))
        X = sb(top, [P, T, D])
        ident = sb(top, [128, 128])
        ones = sb(top, [128, 128])
        epsc = sb(top, [128, 1])
        deg = sb(top, [P, T])
        dis0 = sb(top, [P, T])
        dis1 = sb(top, [P, T])

        def bank(i, n=512, rows=128):
            return PS[0:rows, i, 0:n]

        def layernorm(ctx, src, dst, *waits):
            st = sb(ctx, [P, T, 6])
            mv = sb(ctx, [P, T, 2])
            rs = sb(ctx, [P, T, 2])
            for t in range(T):
                m = p.ve(lambda e, t=t: e.bn_stats(st[:, t, :], src[:, t, :]), *waits)
            for t in range(T):
                m = p.ve(lambda e, t=t: e.bn_aggr(mv[:, t, :], st[:, t, :]), m)
            m = p.se(lambda e: e.activation(rs[:, :, 0], mv[:, :, 1], ACT.Sqrt, bias=epsc[0:P, :]), m)
            m = p.ve(lambda e: e.reciprocal(rs[:, :, 1], rs[:, :, 0]), m)
            marks = []
            for t in range(T):
                marks.append(p.ve(lambda e, t=t: e.tensor_scalar(
                    dst[:, t, :], src[:, t, :], mv[:, t, 0:1], rs[:, t, 1:2], ALU.subtract, ALU.mult), m))
            return marks

        turn = [0]

        def evacuate(out, src, mark):
            turn[0] += 1
            if turn[0] % 2:
                return p.se(lambda e: e.activation(out, src, ACT.Copy), mark)
            return p.ve(lambda e: e.tensor_copy(out, src), mark)

        def transposed(src, dst, marks, banks):
            out = []
            for g in range(7):
                ts = range(4 * g, min(4 * g + 4, T))
                both = []
                for h in range(2):
                    b, free, i = banks.take()

                    def go(e, ts=ts, h=h, b=b):
                        for n, t in enumerate(ts):
                            r = e.transpose(PS[:, b, n * P:n * P + P],
                                            src[:, t, h * 128:h * 128 + 128], ident[0:P, 0:P])
                        return r

                    m = p.pe(go, free, marks[ts[-1]])
                    n = len(ts) * P
                    m = evacuate(dst[:, h, 500 * g:500 * g + n], bank(b, n), m)
                    banks.give(i, m)
                    both.append(m)
                out.append(both)
            return out

        def rows_gemm(XT, W, marks, banks, sink, *waits):
            for t0 in range(0, T, 2):
                ts = range(t0, min(t0 + 2, T))
                b, free, i = banks.take()

                def go(e, ts=ts, b=b):
                    for n, t in enumerate(ts):
                        for k in range(2):
                            r = e.matmul(PS[0:P, b, n * D:n * D + D], XT[:, k, t * P:t * P + P],
                                         W[:, k, :], start=k == 0, stop=k == 1)
                    return r

                m = p.pe(go, free, *marks[ts[-1] // 4], *marks[ts[0] // 4], *waits)
                banks.give(i, sink(b, ts, m))

        def small_gemm(XT, W, n, marks, b, free, *waits):
            def go(e):
                for t in range(T):
                    for k in range(2):
                        r = e.matmul(PS[0:P, b, t * n:t * n + n], XT[:, k, t * P:t * P + P],
                                     W[:, k, :], start=k == 0, stop=k == 1)
                return r
            return p.pe(go, free, *[m for ms in marks for m in ms], *waits)

        def spread(DG, col, row, banks, mark, busy=None, over=()):
            m = p.ve(lambda e: e.tensor_tensor(
                DG[:, :, :], ident[0:P, 0:P].unsqueeze(1).broadcast_to([P, T, P]),
                col.unsqueeze(2).broadcast_to([P, T, P]), ALU.mult), mark, busy)
            flat = DG[:, :, :].rearrange("p t i -> p (t i)")
            for g in range(7):
                n = min(500, N - 500 * g)
                b, free, i = banks.take()
                last = p.pe(lambda e, b=b, g=g, n=n: e.matmul(
                    bank(b, n, P), ones[0:P, 0:P], flat[:, 500 * g:500 * g + n], start=True, stop=True),
                    m, free)
                ev = p.se(lambda e, b=b, g=g, n=n: e.activation(
                    row[:, 500 * g:500 * g + n], bank(b, n, P), ACT.Copy), last, *over)
                banks.give(i, ev)
            return ev, last

        def broadcast_row(ap, parts):
            return ap.unsqueeze(0).broadcast_to([parts, ap.shape[0]])

        with phase() as ctx:
            z = p.ge(lambda e: e.memset(ident[:, :], 0.0))
            p.ge(lambda e: e.affine_select(out=ident[:, :], in_=ident[:, :], compare_op=ALU.not_equal,
                                           fill=1.0, base=0, pattern=[[-1, 128]], channel_multiplier=1), z)
            p.ge(lambda e: e.memset(ones[:, :], 1.0))
            p.ge(lambda e: e.memset(epsc[:, :], EPS))
            p.hold("sync", p.dma(0, lambda e: e.dma_start(X[:, :, :], a["x"].rearrange("(t p) d -> p t d", p=P))))

        def edges(ctx):
            C, G = 400, 40
            se_, de = sb(ctx, [P, C], i32), sb(ctx, [P, C], i32)
            key = sb(ctx, [P, C])
            R = sb(ctx, [P, P, G])
            Q = sb(ctx, [P, G, P])
            low = sb(ctx, [P, P])
            cnt = sb(ctx, [P, C])
            dup = sb(ctx, [P, C])
            spare = sb(ctx, [P, 1])
            idx = sb(ctx, [P, C], i32)
            zero = sb(ctx, [P, N])
            z = p.ve(lambda e: e.memset(zero[:, :], 0.0))
            for t in range(T):
                zd = p.dma(3, lambda e, t=t: e.dma_start(adj[t], zero[:, :]), z)
            zd = p.dma(3, lambda e: e.dma_start(A1[NN:NN + 125, :], zero[:, 0:1]), z)
            l1 = p.dma(1, lambda e: e.dma_start(se_[:, :], a["src"].rearrange("(p c) -> p c", p=P)))
            l2 = p.dma(2, lambda e: e.dma_start(de[:, :], a["dst"].rearrange("(p c) -> p c", p=P)))
            m1 = p.ge(lambda e: e.memset(low[:, :], 1.0))
            m1 = p.ge(lambda e: e.affine_select(out=low[:, :], in_=low[:, :], compare_op=ALU.is_gt, fill=0.0,
                                                base=0, pattern=[[-1, P]], channel_multiplier=1), m1)
            m2 = p.ge(lambda e: e.iota(spare[:, :], [[0, 1]], base=NN, channel_multiplier=1,
                                       allow_small_or_imprecise_dtypes=True))
            k0 = p.ve(lambda e: e.scalar_tensor_tensor(key[:, :], se_[:, :], float(N), de[:, :],
                                                       ALU.mult, ALU.add), l1, l2)
            kd = p.dma(4, lambda e: e.dma_start(KD, key[:, :]), k0)
            flat = KD.rearrange("p c -> (p c)").unsqueeze(0).broadcast_to([P, P * C])\
                .rearrange("q (f c) -> q f c", c=C)
            read, done = None, None
            for g in range(C // G):
                s = slice(g * G, g * G + G)
                ld = p.dma(5, lambda e, s=s: e.dma_start(R[:, :, :], flat[:, :, s]), kd, read)
                m = p.ve(lambda e, s=s: e.tensor_tensor(
                    Q[:, :, :], R[:, :, :].rearrange("p f c -> p c f"),
                    key[:, s].unsqueeze(2).broadcast_to([P, G, P]), ALU.is_equal), ld, done)
                read = m
                m = p.ve(lambda e, s=s: e.tensor_reduce(cnt[:, s], Q[:, :, :], AX.X, ALU.add), m)
                m = p.ve(lambda e, s=s: e.tensor_tensor(
                    Q[:, :, :], Q[:, :, :], low[:, :].unsqueeze(1).broadcast_to([P, G, P]), ALU.mult), m, m1)
                m = p.ve(lambda e, s=s: e.tensor_reduce(dup[:, s], Q[:, :, :], AX.X, ALU.max), m)
                done = m
            m = p.ve(lambda e: e.tensor_scalar(zero[:, 0:C], key[:, :], spare[:, 0:1], None, ALU.subtract),
                     m, m2, zd)
            m = p.ve(lambda e: e.tensor_scalar(dup[:, :], dup[:, :], -1.0, 1.0, ALU.mult, ALU.add), m)
            m = p.ve(lambda e: e.tensor_tensor(zero[:, 0:C], zero[:, 0:C], dup[:, :], ALU.mult), m)
            m = p.ve(lambda e: e.tensor_scalar(idx[:, :], zero[:, 0:C], spare[:, 0:1], None, ALU.add), m)
            last = zd
            for c in range(C):
                last = p.dma(23, lambda e, c=c: e.indirect_dma_start(
                    A1, bass.IndirectOffsetOnAxis(idx[:, c:c + 1], 0), cnt[:, c:c + 1], None,
                    compute_op=ALU.add), m, last, by="gpsimd")
            p.hold("gpsimd", last)

        with phase() as ctx:
            edges(ctx)

        with phase() as ctx:
            tiles = Ring([sb(ctx, [P, T, P]) for _ in range(2)])
            outs = Ring([sb(ctx, [P, N], bf16) for _ in range(2)])
            banks = Ring(range(8))
            cols = A1[0:NN, :].rearrange("(t p i) o -> p t (i o)", p=P, i=N)
            dp = sb(ctx, [P, T, 7])
            z = p.ve(lambda e: e.memset(dp[:, :, :], 0.0))
            for bk in range(T):
                tile, free, i = tiles.take()
                ld = p.dma(1 + i, lambda e, tile=tile, bk=bk: e.dma_start(
                    tile[:, :, :], cols[:, :, bk * P:bk * P + P]), free)
                o, ofree, oi = outs.take()
                for g in range(7):
                    js = range(4 * g, min(4 * g + 4, T))
                    b, bfree, bi = banks.take()

                    def go(e, js=js, b=b, tile=tile):
                        for n, j in enumerate(js):
                            r = e.transpose(PS[0:P, b, n * P:n * P + P], tile[:, j, :], ident[0:P, 0:P])
                        return r

                    n = len(js) * P
                    last = p.pe(go, ld, bfree)
                    m = p.ve(lambda e, b=b, n=n, g=g, bk=bk: e.tensor_reduce(
                        dp[:, bk, g:g + 1], bank(b, n, P), AX.X, ALU.add), last, z)
                    m = p.ve(lambda e, b=b, n=n, g=g, o=o: e.tensor_scalar(
                        o[:, 500 * g:500 * g + n], bank(b, n, P), 0.0, -HUGE, ALU.is_equal, ALU.mult),
                        ofree)
                    banks.give(bi, m)
                tiles.give(i, last)
                outs.give(oi, p.dma(3 + oi, lambda e, o=o, bk=bk: e.dma_start(NEG[bk], o[:, :]), m, by="scalar"))
            p.hold("scalar", *outs.free)
            m = p.ve(lambda e: e.tensor_reduce(deg[:, :], dp[:, :, :], AX.X, ALU.add), m)
            tmp = sb(ctx, [P, T, 3])
            m1 = p.ve(lambda e: e.tensor_scalar(tmp[:, :, 0], deg[:, :], 1.0, None, ALU.add), m)
            m1 = p.se(lambda e: e.activation(tmp[:, :, 0], tmp[:, :, 0], ACT.Sqrt), m1)
            m1 = p.ve(lambda e: e.reciprocal(dis0[:, :], tmp[:, :, 0]), m1)
            m1 = p.ve(lambda e: e.tensor_scalar(tmp[:, :, 1], deg[:, :], 1.0, None, ALU.max), m1)
            m1 = p.se(lambda e: e.activation(tmp[:, :, 1], tmp[:, :, 1], ACT.Sqrt), m1)
            m1 = p.ve(lambda e: e.reciprocal(tmp[:, :, 1], tmp[:, :, 1]), m1)
            m1 = p.ve(lambda e: e.tensor_scalar(tmp[:, :, 2], deg[:, :], 0.0, None, ALU.is_gt), m1)
            p.ve(lambda e: e.tensor_tensor(dis1[:, :], tmp[:, :, 1], tmp[:, :, 2], ALU.mult), m1)

        def attention(ctx, H, C, HA, SD, loops, finish):
            M = sb(ctx, [P, T, H])
            c1 = sb(ctx, [P, T, H])
            c2 = sb(ctx, [P, T, H])
            s2 = sb(ctx, [P, T, H])
            with ExitStack() as c:
                banks = Ring(range(8))
                DG = sb(c, [P, T, P])
                SR = [sb(c, [P, N]) for _ in range(H)]
                negs = Ring([sb(c, [P, N], bf16) for _ in range(3)])
                junk = Ring([sb(c, [P, N], bf16) for _ in range(2)])
                notI = sb(c, [P, P])
                ni = p.ve(lambda e: e.tensor_scalar(notI[:, :], ident[0:P, 0:P], -1.0, 1.0, ALU.mult, ALU.add))
                marks, busy = [], None
                for h in range(H):
                    m, busy = spread(DG, SD[:, :, h], SR[h], banks, None, busy)
                    marks.append(m)
                for b in range(T):
                    neg, free, i = negs.take()
                    ld = p.dma(1 + i, lambda e, neg=neg, b=b: e.dma_start(neg[:, :], NEG[b]), free)
                    if loops:
                        ld = p.ve(lambda e, neg=neg, b=b: e.tensor_tensor(
                            neg[:, b * P:b * P + P], neg[:, b * P:b * P + P], notI[:, :], ALU.mult), ld, ni)
                    for h in range(H):
                        j, jfree, ji = junk.take()
                        m = p.ve(lambda e, j=j, neg=neg, h=h, b=b: e.tensor_tensor_reduce(
                            out=j[:, :], in0=neg[:, :], in1=SR[h][:, :], scale=1.0, scalar=-HUGE,
                            op0=ALU.add, op1=ALU.max, accum_out=M[:, b, h:h + 1]), ld, marks[h], jfree)
                        junk.give(ji, m)
                    negs.give(i, m)
                d = SD[:, :, H:2 * H]
                m = p.ve(lambda e: e.tensor_tensor(c1[:, :, :], M[:, :, :], d, ALU.add), m)
                m = p.ve(lambda e: e.scalar_tensor_tensor(M[:, :, :], c1[:, :, :], 0.2, c1[:, :, :],
                                                          ALU.mult, ALU.max), m)
                m = p.ve(lambda e: e.tensor_tensor(c1[:, :, :], d, M[:, :, :], ALU.subtract), m)
                m = p.ve(lambda e: e.scalar_tensor_tensor(c2[:, :, :], d, 0.2, M[:, :, :],
                                                          ALU.mult, ALU.subtract), m)
                m = p.ve(lambda e: e.tensor_scalar(s2[:, :, :], SD[:, :, 0:H], 0.2, None, ALU.mult), m)
                p.flush()
            DG = sb(ctx, [P, T, P])
            R1, R2 = sb(ctx, [P, N]), sb(ctx, [P, N])
            work = Ring([sb(ctx, [P, N]) for _ in range(2)])
            ads = Ring([sb(ctx, [P, N]) for _ in range(2)])
            lane = 1
            if C == 64:
                sets = [(range(0, T), 7)]
            else:
                sets = [(range(0, 7), 1), (range(7, 13), 1), (range(13, 19), 1), (range(19, 25), 1)]
            busy = zlast = tlast = None
            ended = [None, None]
            for h in range(H):
                if C == 64:
                    base = 4 * (h % 2)
                    spare = Ring([4 - base + k for k in range(4)])
                    spare.free = [ended[1 - h % 2]] * 4
                else:
                    base = 0
                    spare = Ring([7])
                r1, busy = spread(DG, c1[:, :, h], R1, spare, m, busy, (zlast,))
                rows, busy = spread(DG, c2[:, :, h], R2, spare, m, busy, (tlast,))
                for tiles, per in sets:
                    lo, n = tiles[0] * P, len(tiles) * P
                    for j in range(T):
                        ad, free, ai = ads.take()
                        ld = p.dma(lane + ai, lambda e, ad=ad, j=j, lo=lo, n=n: e.dma_start(
                            ad[:, 0:n], adj[j][:, lo:lo + n]), free)
                        if loops and j in tiles:
                            ld = p.ve(lambda e, ad=ad, at=(j - tiles[0]) * P: e.tensor_tensor(
                                ad[:, at:at + P], ad[:, at:at + P], ident[0:P, 0:P], ALU.add), ld)
                        w, wfree, wi = work.take()
                        zlast = p.se(lambda e, w=w, j=j, h=h, lo=lo, n=n: e.activation(
                            w[:, 0:n], R1[:, lo:lo + n], ACT.Identity, bias=SD[:, j, h:h + 1]), r1, wfree)
                        tlast = p.ve(lambda e, w=w, j=j, h=h, lo=lo, n=n: e.scalar_tensor_tensor(
                            w[:, 0:n], R2[:, lo:lo + n], s2[:, j, h:h + 1], w[:, 0:n],
                            ALU.add, ALU.max), rows, zlast)
                        mk = p.se(lambda e, w=w, n=n: e.activation(w[:, 0:n], w[:, 0:n], ACT.Exp), tlast)
                        mk = p.ve(lambda e, w=w, ad=ad, n=n: e.scalar_tensor_tensor(
                            w[:, 0:n], w[:, 0:n], CAP, ad[:, 0:n], ALU.min, ALU.mult), mk, ld)
                        ads.give(ai, mk)

                        def go(e, w=w, j=j, h=h, tiles=tiles, per=per, base=base):
                            for n, t in enumerate(tiles):
                                b, at = base + n // per, (n % per) * (C + 1)
                                r = e.matmul(PS[0:P, b, at:at + C + 1], w[:, n * P:n * P + P],
                                             HA[:, j, h, :], start=(j == 0 and n % per == 0),
                                             stop=j == T - 1, skip_group_check=True)
                            return r

                        mk = p.pe(go, mk, ended[h % 2] if j == 0 else None)
                        work.give(wi, mk)
                    ended[h % 2] = finish(h, tiles, per, base, mk)

        def gat(XTm, banks, ctx, XT, W, WN, AB, H, C, HA, SD):
            w = sb(ctx, [128, 2, D])
            wn = sb(ctx, [128, 2, D])
            ab = sb(ctx, [128, 2, 2 * H])
            wa = sb(ctx, [128, 2, 2 * H])
            l1 = p.dma(1, lambda e: e.dma_start(w[:, :, :], W.rearrange("(k p) n -> p k n", p=128)))
            l2 = p.dma(2, lambda e: e.dma_start(wn[:, :, :], WN.rearrange("(k p) n -> p k n", p=128)))
            l3 = p.dma(3, lambda e: e.dma_start(ab[:, :, :], AB.rearrange("(k p) n -> p k n", p=128)))
            b, free, i = banks.take()

            def go(e):
                for k in range(2):
                    for c in range(2):
                        r = e.matmul(PS[:, b, 64 * k:64 * k + 2 * H], wn[:, c, k * 128:k * 128 + 128],
                                     ab[:, c, :], start=c == 0, stop=c == 1)
                return r

            m = p.pe(go, l2, l3, free)
            for k in range(2):
                m2 = p.ve(lambda e, k=k: e.tensor_copy(wa[:, k, :], PS[:, b, 64 * k:64 * k + 2 * H]), m)
            banks.give(i, m2)
            b2, free, i = banks.take()
            m = small_gemm(XT, wa, 2 * H, XTm, b2, free, m2)
            m = p.ve(lambda e: e.tensor_copy(SD[:, :, :].rearrange("p t n -> p (t n)"),
                                             bank(b2, T * 2 * H, P)), m)
            banks.give(i, m)
            p.ge(lambda e: e.memset(HA[:, :, :, C:C + 1], 1.0))

            def sink(b, ts, m):
                return evacuate(HA[:, ts[0]:ts[-1] + 1, :, 0:C],
                                bank(b, len(ts) * D, P).rearrange("p (t h c) -> p t h c", h=H, c=C), m)

            rows_gemm(XT, w, XTm, banks, sink, l1)

        def numerators(base, n, per, C):
            out = []
            for b in range((n + per - 1) // per):
                k = min(per, n - b * per)
                out.append((b * per, k, PS[0:P, base + b, 0:k * (C + 1)].rearrange("p (t c) -> p t c", c=C + 1)))
            return out

        def normalised(rec, base, tiles, per, C, mark, then):
            for at, k, s in numerators(base, len(tiles), per, C):
                m = p.ve(lambda e, s=s, k=k: e.tensor_scalar(rec[:, 0:k, :], s[:, :, C:C + 1], 1e-16, None,
                                                             ALU.add), mark)
                m = p.ve(lambda e, k=k: e.reciprocal(rec[:, 0:k, :], rec[:, 0:k, :]), m)
                mark = then(tiles[0] + at, k, s[:, :, 0:C], rec[:, 0:k, :].broadcast_to([P, k, C]), m)
            return mark

        if start < 1 <= upto:
            with phase() as ctx:
                HA = sb(ctx, [P, T, 4, 65])
                SD = sb(ctx, [P, T, 8])
                with ExitStack() as c:
                    XN = sb(c, [P, T, D])
                    XT = sb(c, [128, 2, N])
                    marks = layernorm(c, X, XN)
                    banks = Ring(range(8))
                    xm = transposed(XN, XT, marks, banks)
                    gat(xm, banks, c, XT, a["L0_gnn_WT"], a["L0_gnn_W"], a["L0_gnn_AB"], 4, 64, HA, SD)
                    p.ve(lambda e: e.tensor_tensor(X[:, :, :], X[:, :, :], XN[:, :, :], ALU.add), marks[-1])
                    p.flush()
                bias = sb(ctx, [P, D])
                rec = sb(ctx, [P, 7, 1])
                o = sb(ctx, [P, 7, 64])
                o2 = sb(ctx, [P, 7, 64])
                bl = p.dma(10, lambda e: e.dma_start(bias[:, :], broadcast_row(a["L0_gnn_bias"], P)))

                def finish(h, tiles, per, base, mark):
                    def then(t0, k, s, r, m):
                        m = p.ve(lambda e: e.tensor_tensor(o[:, 0:k, :], s, r, ALU.mult), m)
                        end.append(m)
                        m = p.ve(lambda e: e.tensor_tensor(
                            o[:, 0:k, :], o[:, 0:k, :],
                            bias[:, 64 * h:64 * h + 64].unsqueeze(1).broadcast_to([P, k, 64]), ALU.add), m, bl)
                        m = p.ve(lambda e: e.tensor_scalar(o2[:, 0:k, :], o[:, 0:k, :], 0.0, None, ALU.min), m)
                        m = p.se(lambda e: e.activation(o2[:, 0:k, :], o2[:, 0:k, :], ACT.Exp), m)
                        m = p.ve(lambda e: e.scalar_tensor_tensor(o[:, 0:k, :], o[:, 0:k, :], 0.0,
                                                                  o2[:, 0:k, :], ALU.max, ALU.add), m)
                        x = X[:, t0:t0 + k, 64 * h:64 * h + 64]
                        return p.ve(lambda e: e.scalar_tensor_tensor(x, o[:, 0:k, :], -1.0, x,
                                                                     ALU.add, ALU.add), m)
                    end = []
                    normalised(rec, base, tiles, per, 64, mark, then)
                    return end[-1]

                attention(ctx, 4, 64, HA, SD, True, finish)

        def routing(ctx, XT, xm, Wr, bias, norm, banks):
            wr = sb(ctx, [128, 2, 8])
            L = sb(ctx, [P, T, 8])
            R = sb(ctx, [P, T, 8])
            O1, O2, K = sb(ctx, [P, T, 8]), sb(ctx, [P, T, 8]), sb(ctx, [P, T, 8])
            io = sb(ctx, [P, 8])
            s1 = sb(ctx, [P, T, 1])
            l1 = p.dma(14, lambda e: e.dma_start(wr[:, :, :], Wr.rearrange("(k p) n -> p k n", p=128)))
            i0 = p.ge(lambda e: e.iota(io[:, :], [[1, 8]], base=0, channel_multiplier=0,
                                       allow_small_or_imprecise_dtypes=True))
            b, free, i = banks.take()
            m = small_gemm(XT, wr, 8, xm, b, free, l1)
            lv = PS[0:P, b, 0:8 * T].rearrange("p (t n) -> p t n", n=8)
            if bias is not None:
                br = sb(ctx, [P, 8])
                l2 = p.dma(15, lambda e: e.dma_start(br[:, :], broadcast_row(bias, P)))
                m = p.ve(lambda e: e.tensor_tensor(L[:, :, :], lv, br[:, :].unsqueeze(1).broadcast_to([P, T, 8]),
                                                   ALU.add), m, l2)
            else:
                m = p.ve(lambda e: e.tensor_copy(L[:, :, :], lv), m)
            banks.give(i, m)
            sx = s1[:, :, :].broadcast_to([P, T, 8])
            iob = io[:, :].unsqueeze(1).broadcast_to([P, T, 8])

            def red(src, op, m):
                return p.ve(lambda e: e.tensor_reduce(s1[:, :, 0], src[:, :, :], AX.X, op), m)

            def tt(out, x, y, op, m, *w):
                return p.ve(lambda e: e.tensor_tensor(out[:, :, :], x[:, :, :] if x is not None else None, y, op),
                            m, *w)

            if norm is not None:
                m = red(L, ALU.max, m)
                m = tt(L, L, sx, ALU.subtract, m)
                m = p.se(lambda e: e.activation(L[:, :, :], L[:, :, :], ACT.Exp), m)
                m = red(L, ALU.add, m)
                m = p.ve(lambda e: e.reciprocal(s1[:, :, :], s1[:, :, :]), m)
                m = tt(L, L, sx, ALU.mult, m)

            def first(src, out, m):
                m = red(src, ALU.max, m)
                m = tt(K, src, sx, ALU.is_equal, m)
                m = p.ve(lambda e: e.scalar_tensor_tensor(K[:, :, :], K[:, :, :], -8.0, iob, ALU.mult, ALU.add),
                         m, i0)
                m = red(K, ALU.min, m)
                return tt(out, K, sx, ALU.is_equal, m)

            m = first(L, O1, m)
            m = p.ve(lambda e: e.scalar_tensor_tensor(R[:, :, :], O1[:, :, :], -HUGE, L[:, :, :],
                                                      ALU.mult, ALU.add), m)
            m = first(R, O2, m)
            m = tt(O1, O1, O2[:, :, :], ALU.add, m)
            if norm is not None:
                m = tt(O1, O1, L[:, :, :], ALU.mult, m)
                m = red(O1, ALU.add, m)
                if norm == "probs":
                    m = p.ve(lambda e: e.tensor_scalar(s1[:, :, :], s1[:, :, :], 1e-12, None, ALU.max), m)
                m = p.ve(lambda e: e.reciprocal(s1[:, :, :], s1[:, :, :]), m)
                m = tt(O1, O1, sx, ALU.mult, m)
            return O1, m

        def experts(ctx, XT, xm, Cw, cm, W1, b1, W2, b2, hid, scale, banks1, banks2, xready):
            nh = hid // 128
            w1s = [sb(ctx, [128, 2, hid]) for _ in range(2)]
            w2s = [sb(ctx, [128, nh, D]) for _ in range(2)]
            b1s = [sb(ctx, [128, nh]) for _ in range(2)]
            hts = Ring([sb(ctx, [128, nh, 500]) for _ in range(2)])
            xes = Ring([sb(ctx, [128, 2, 500]) for _ in range(2)]) if scale else None
            if scale:
                gb = sb(ctx, [128, 2, 8])
                bb = sb(ctx, [128, 2, 8])
                lg = p.dma(12, lambda e: e.dma_start(gb[:, :, :], scale[0].rearrange("k p n -> p k n")))
                lb = p.dma(13, lambda e: e.dma_start(bb[:, :, :], scale[1].rearrange("k p n -> p k n")))
            CT = sb(ctx, [8, N])
            b2s = sb(ctx, [8, D])
            l2 = p.dma(11, lambda e: e.dma_start(b2s[:, :], b2))
            for g in range(7):
                ts = range(4 * g, min(4 * g + 4, T))
                b, free, i = banks1.take()

                def go(e, ts=ts, b=b):
                    for n, t in enumerate(ts):
                        r = e.transpose(PS[0:8, b, n * P:n * P + P], Cw[:, t, :], ident[0:P, 0:P])
                    return r

                m = p.pe(go, free, cm)
                ct = p.se(lambda e, b=b, g=g, n=len(ts) * P: e.activation(
                    CT[:, 500 * g:500 * g + n], PS[0:8, b, 0:n], ACT.Copy), m)
                banks1.give(i, ct)
            xlast = xready
            for t0 in range(0, T, 2):
                ts = range(t0, min(t0 + 2, T))
                b, free, i = banks2.take()

                def go(e, ts=ts, b=b):
                    for n, t in enumerate(ts):
                        r = e.matmul(PS[0:P, b, n * D:n * D + D], CT[:, t * P:t * P + P], b2s[:, :],
                                     start=True, stop=True)
                    return r

                m = p.pe(go, free, ct, l2)
                xs = X[:, ts[0]:ts[-1] + 1, :].rearrange("p t d -> p (t d)")
                xlast = p.ve(lambda e, b=b, xs=xs, n=len(ts) * D: e.tensor_tensor(
                    xs, xs, bank(b, n, P), ALU.add), m, xready)
                banks2.give(i, xlast)
            used = [None, None]
            loads = {}

            def load(ex):
                i = ex % 2
                w = used[i]
                loads[ex] = [
                    p.dma(1 + 3 * i, lambda e, i=i, ex=ex: e.dma_start(
                        w1s[i][:, :, :], W1[ex].rearrange("(k p) n -> p k n", p=128)), w),
                    p.dma(2 + 3 * i, lambda e, i=i, ex=ex: e.dma_start(
                        w2s[i][:, :, :], W2[ex].rearrange("(k p) n -> p k n", p=128)), w),
                    p.dma(3 + 3 * i, lambda e, i=i, ex=ex: e.dma_start(b1s[i][:, :], b1[ex]), w)]

            def up(ex, g):
                n = min(500, N - 500 * g)
                i = ex % 2
                if scale:
                    xe, xf, xi = xes.take()
                    for k in range(2):
                        m = p.ve(lambda e, k=k: e.tensor_scalar(
                            xe[:, k, 0:n], XT[:, k, 500 * g:500 * g + n], gb[:, k, ex:ex + 1],
                            bb[:, k, ex:ex + 1], ALU.mult, ALU.add), xf, lg, lb, *[y for x in xm for y in x])
                    src, xw = (lambda k: xe[:, k, 0:n]), [m]
                else:
                    src, xw = (lambda k: XT[:, k, 500 * g:500 * g + n]), xm[g]
                ht, hf, hi = hts.take()
                last = None
                for c in range(nh):
                    b, free, bi = banks1.take()

                    def go(e, b=b, c=c):
                        for k in range(2):
                            r = e.matmul(bank(b, n), w1s[i][:, k, 128 * c:128 * c + 128], src(k),
                                         start=k == 0, stop=k == 1)
                        return r

                    m = p.pe(go, free, *loads[ex], *xw)
                    if scale:
                        xes.give(xi, m)
                    last = p.se(lambda e, b=b, c=c: e.activation(
                        ht[:, c, 0:n], bank(b, n), ACT.Gelu, bias=b1s[i][:, c:c + 1]), m, hf)
                    banks1.give(bi, last)
                return ht, hi, last

            def down(ex, g, ht, hi, ready):
                nonlocal xlast
                i = ex % 2
                ts = range(4 * g, min(4 * g + 4, T))
                for t0 in range(0, len(ts), 2):
                    pair = ts[t0:t0 + 2]
                    b, free, bi = banks2.take()

                    def go(e, b=b, pair=pair, t0=t0):
                        for n in range(len(pair)):
                            for c in range(nh):
                                r = e.matmul(PS[0:P, b, n * D:n * D + D],
                                             ht[:, c, (t0 + n) * P:(t0 + n) * P + P],
                                             w2s[i][:, c, :], start=c == 0, stop=c == nh - 1)
                        return r

                    m = p.pe(go, free, ready, *loads[ex])
                    for n, t in enumerate(pair):
                        xlast = p.ve(lambda e, b=b, n=n, t=t: e.scalar_tensor_tensor(
                            X[:, t, :], PS[0:P, b, n * D:n * D + D], Cw[:, t, ex:ex + 1], X[:, t, :],
                            ALU.mult, ALU.add), m, lastx.get(t) or xlast)
                        lastx[t] = xlast
                    banks2.give(bi, xlast)
                hts.give(hi, m)
                return m

            lastx = {}
            load(0)
            load(1)
            before = None
            for ex in range(8):
                for g in range(7):
                    now = (ex, g, *up(ex, g))
                    if before:
                        m = down(*before)
                        if before[1] == 6:
                            used[before[0] % 2] = m
                            if before[0] + 2 < 8:
                                load(before[0] + 2)
                    before = now
            down(*before)

        if start < 2 <= upto:
            with phase() as ctx:
                XT = sb(ctx, [128, 2, N])
                banks = Ring(range(4))
                with ExitStack() as c:
                    XN = sb(c, [P, T, D])
                    marks = layernorm(c, X, XN)
                    transposed(XN, XT, marks, Ring(range(8)))
                    p.ve(lambda e: e.tensor_tensor(X[:, :, :], X[:, :, :], XN[:, :, :], ALU.add), marks[-1])
                    p.flush()
                none = [()] * 7
                Cw, cm = routing(ctx, XT, none, a["L0_ffn_router_wT"], None, "probs", banks)
                experts(ctx, XT, none, Cw, cm, a["L0_ffn_w1"], a["L0_ffn_b1"], a["L0_ffn_w2"],
                        a["L0_ffn_b2"], 256, None, banks, Ring(range(4, 8)), None)

        if start < 3 <= upto:
            with phase() as ctx:
                H1 = sb(ctx, [P, T, D])
                with ExitStack() as c0:
                    HA = sb(c0, [P, T, 4, 65])
                    SD = sb(c0, [P, T, 8])
                    with ExitStack() as c:
                        XN = sb(c, [P, T, D])
                        XT = sb(c, [128, 2, N])
                        marks = layernorm(c, X, XN)
                        banks = Ring(range(8))
                        xm = transposed(XN, XT, marks, banks)
                        gat(xm, banks, c, XT, a["L1_gnn_W1T"], a["L1_gnn_W1"], a["L1_gnn_AB1"], 4, 64, HA, SD)
                        p.flush()
                    rec = sb(c0, [P, 7, 1])

                    def finish(h, tiles, per, base, mark):
                        def then(t0, k, s, r, m):
                            x = H1[:, t0:t0 + k, 64 * h:64 * h + 64]
                            m = p.ve(lambda e: e.tensor_tensor(x, s, r, ALU.mult), m)
                            end.append(m)
                            return p.ve(lambda e: e.tensor_scalar(x, x, 0.0, None, ALU.max), m)
                        end = []
                        return normalised(rec, base, tiles, per, 64, mark, then)

                    attention(c0, 4, 64, HA, SD, False, finish)
                    p.flush()
                with ExitStack() as c0:
                    HB = sb(c0, [P, T, 1, 257])
                    SD = sb(c0, [P, T, 2])
                    with ExitStack() as c:
                        XT = sb(c, [128, 2, N])
                        banks = Ring(range(8))
                        xm = transposed(H1, XT, [None] * T, banks)
                        gat(xm, banks, c, XT, a["L1_gnn_W2T"], a["L1_gnn_W2"], a["L1_gnn_AB2"], 1, 256, HB, SD)
                        p.flush()
                    rec = sb(c0, [P, 1, 1])
                    o = sb(c0, [P, 1, 256])

                    def finish2(h, tiles, per, base, mark):
                        def then(t0, k, s, r, m):
                            m = p.ve(lambda e: e.tensor_tensor(o[:, :, :], s, r, ALU.mult), m)
                            x = X[:, t0:t0 + 1, :]
                            return p.ve(lambda e: e.tensor_tensor(x, x, o[:, :, :], ALU.add), m)
                        return normalised(rec, base, tiles, per, 256, mark, then)

                    attention(c0, 1, 256, HB, SD, False, finish2)
                    p.flush()

        if start < 4 <= upto:
            L, NC = 25, 125
            with ExitStack() as ctx:
                XG = sb(ctx, [128, 6, N])
                HS = sb(ctx, [128, 2, N])
                V = sb(ctx, [128, 2, 6, 128])
                with ExitStack() as c:
                    XT = sb(c, [128, 2, N])
                    U = sb(c, [128, 2, 6, 128])
                    bg = sb(c, [128, 6])
                    XN = sb(c, [P, T, D])
                    for n, g in enumerate("ioc"):
                        lu = p.dma(1 + n, lambda e, n=n, g=g: e.dma_start(
                            U[:, :, 2 * n:2 * n + 2, :],
                            a[f"L1_ffn_U_{g}"].rearrange("(k p) (m n) -> p k m n", p=128, m=2)))
                        lv = p.dma(4 + n, lambda e, n=n, g=g: e.dma_start(
                            V[:, :, 2 * n:2 * n + 2, :],
                            a[f"L1_ffn_V_{g}"].rearrange("(k p) (m n) -> p k m n", p=128, m=2)))
                        lb = p.dma(7 + n, lambda e, n=n, g=g: e.dma_start(
                            bg[:, 2 * n:2 * n + 2], a[f"L1_ffn_b_{g}"]))
                        p.hold("sync", lu, lv, lb)
                    marks = layernorm(c, X, XN)
                    p.flush()
                    banks = Ring(range(8))
                    xm = transposed(XN, XT, marks, banks)
                    for g in range(7):
                        n = min(500, N - 500 * g)
                        for m6 in range(6):
                            b, free, i = banks.take()

                            def go(e, b=b, m6=m6, g=g, n=n):
                                for k in range(2):
                                    r = e.matmul(bank(b, n), U[:, k, m6, :], XT[:, k, 500 * g:500 * g + n],
                                                 start=k == 0, stop=k == 1)
                                return r

                            m = p.pe(go, free, *xm[g])
                            m = p.se(lambda e, b=b, m6=m6, g=g, n=n: e.activation(
                                XG[:, m6, 500 * g:500 * g + n], bank(b, n), ACT.Identity,
                                bias=bg[:, m6:m6 + 1]), m)
                            banks.give(i, m)
                    p.flush()
                H0, C0 = sb(ctx, [128, 2, NC]), sb(ctx, [128, 2, NC])
                Cs = sb(ctx, [128, 2, NC])
                Gt = sb(ctx, [128, 6, NC])
                t1, t2 = sb(ctx, [128, 2, NC]), sb(ctx, [128, 2, NC])
                Ht = sb(ctx, [128, 2, NC])
                df = sb(ctx, [128, 4])
                ft = sb(ctx, [1, 2])
                go_on = sb(ctx, [1, 1], i32)
                for t in (H0, C0):
                    p.ge(lambda e, t=t: e.memset(t[:, :, :], 0.0))
                p.ge(lambda e: e.memset(go_on[:, :], 1))
                p.flush()
                HSv = HS[:, :, :].rearrange("p k (c s) -> p k s c", s=L)
                XGv = XG[:, :, :].rearrange("p g (c s) -> p g s c", s=L)
                with nc.Fori(0, NC):
                    flag = nc.values_load(go_on[0:1, 0:1], min_val=0, max_val=1)
                    nc.all_engine_barrier(sem_only=True)
                    with nc.If(flag == 1):
                        q.rewind()
                        hm = cm_ = q.ve(lambda e: e.tensor_copy(Cs[:, :, :], C0[:, :, :]))
                        gfree = None
                        for s in range(L):
                            hprev = (lambda k: H0[:, k, :]) if s == 0 else (lambda k, s=s: HSv[:, k, s - 1, :])
                            hall = H0[:, :, :] if s == 0 else HSv[:, :, s - 1, :]
                            ms = []
                            for b, gates in ((2 * (s % 2), (4, 5)), (2 * (s % 2) + 1, (0, 1, 2, 3))):
                                def go(e, b=b, gates=gates, hprev=hprev):
                                    for n, g6 in enumerate(gates):
                                        for k in range(2):
                                            r = e.matmul(PS[:, b, n * 128:n * 128 + NC], V[:, k, g6, :],
                                                         hprev(k), start=k == 0, stop=k == 1)
                                    return r
                                ms.append(q.pe(go, hm))
                            for n, (b, lo, hi) in enumerate(((2 * (s % 2), 4, 6), (2 * (s % 2) + 1, 0, 4))):
                                src = PS[:, b, :].rearrange("p (g c) -> p g c", c=128)[:, 0:hi - lo, 0:NC]
                                m = q.ve(lambda e, src=src, lo=lo, hi=hi, s=s: e.tensor_tensor(
                                    Gt[:, lo:hi, :], src, XGv[:, lo:hi, s, :], ALU.add), ms[n], gfree)
                                am = q.se(lambda e, lo=lo, hi=hi, n=n: e.activation(
                                    Gt[:, lo:hi, :], Gt[:, lo:hi, :], ACT.Sigmoid if n else ACT.Tanh), m)
                                if n == 0:
                                    m1 = q.ve(lambda e, hall=hall: e.tensor_tensor(
                                        t1[:, :, :], hall, Cs[:, :, :], ALU.mult), cm_)
                            m2 = q.ve(lambda e: e.tensor_tensor(t2[:, :, :], Gt[:, 0:2, :], Gt[:, 4:6, :],
                                                                ALU.mult), am)
                            cm_ = q.ve(lambda e: e.tensor_tensor(Cs[:, :, :], t1[:, :, :], t2[:, :, :],
                                                                 ALU.add), m1, m2)
                            am = q.se(lambda e: e.activation(t1[:, :, :], Cs[:, :, :], ACT.Tanh), cm_)
                            hm = q.ve(lambda e, s=s: e.tensor_tensor(HSv[:, :, s, :], Gt[:, 2:4, :],
                                                                     t1[:, :, :], ALU.mult), am)
                            gfree = hm
                        nb = NC - 1
                        new_h, new_c = HSv[:, :, L - 1, 0:nb], Cs[:, :, 0:nb]
                        m = q.ve(lambda e: e.tensor_tensor(t1[:, :, 0:nb], new_h, H0[:, :, 1:NC],
                                                           ALU.subtract), hm)
                        m = q.ve(lambda e: e.tensor_reduce(df[:, 0:1], t1[:, :, 0:nb], AX.XY, ALU.max,
                                                           apply_absolute_value=True), m)
                        m2 = q.ve(lambda e: e.tensor_tensor(t2[:, :, 0:nb], new_c, C0[:, :, 1:NC],
                                                            ALU.subtract), m)
                        m2 = q.ve(lambda e: e.tensor_reduce(df[:, 1:2], t2[:, :, 0:nb], AX.XY, ALU.max,
                                                            apply_absolute_value=True), m2)
                        q.ve(lambda e: e.tensor_copy(H0[:, :, 1:NC], new_h), m)
                        q.ve(lambda e: e.tensor_copy(C0[:, :, 1:NC], new_c), m2)
                        m = q.ve(lambda e: e.tensor_tensor(df[:, 2:3], df[:, 0:1], df[:, 1:2], ALU.max), m2)
                        m = q.pe(lambda e: e.transpose(PS[0:1, 7, 0:128], df[:, 2:3], ident[:, :]), m)
                        m = q.ve(lambda e: e.tensor_reduce(ft[:, 0:1], PS[0:1, 7, 0:128], AX.X, ALU.max), m)
                        m = q.ve(lambda e: e.tensor_scalar(go_on[:, :], ft[:, 0:1], TOL, None, ALU.is_gt), m)
                        q.hold("vector", m)
                        q.flush()
                        nc.multi_engine_barrier(list(mybir.ALL_ENGINES), sems_to_clear=q.numbers())
                banks = Ring(range(8))
                for t0 in range(0, T, 2):
                    ts = range(t0, min(t0 + 2, T))
                    b, free, i = banks.take()

                    def go(e, ts=ts, b=b):
                        for n, t in enumerate(ts):
                            for k in range(2):
                                r = e.transpose(PS[0:P, b, n * D + 128 * k:n * D + 128 * k + 128],
                                                HS[:, k, t * P:t * P + P], ident[:, :])
                        return r

                    m = p.pe(go, free)
                    xs = X[:, ts[0]:ts[-1] + 1, :].rearrange("p t d -> p (t d)")
                    banks.give(i, p.ve(lambda e, b=b, xs=xs, n=len(ts) * D: e.tensor_tensor(
                        xs, xs, bank(b, n, P), ALU.add), m))
                p.flush()

        def convolution(ctx, banks, XT, xm, W, dis, HS, finish):
            w = sb(ctx, [128, 2, D])
            l1 = p.dma(1, lambda e: e.dma_start(w[:, :, :], W.rearrange("(k p) n -> p k n", p=128)))

            def sink(b, ts, m):
                k = len(ts)
                return p.ve(lambda e: e.tensor_tensor(
                    HS[:, ts[0]:ts[0] + k, :], bank(b, k * D, P).rearrange("p (t d) -> p t d", d=D),
                    dis[:, ts[0]:ts[0] + k].unsqueeze(2).broadcast_to([P, k, D]), ALU.mult), m)

            rows_gemm(XT, w, xm, banks, sink, l1)
            p.flush()
            half = 13
            ads = Ring([sb(ctx, [P, half * P]) for _ in range(4)])
            free_b = None
            for tiles in (range(0, half), range(half, T)):
                lo, n = tiles[0] * P, len(tiles) * P
                for j in range(T):
                    ad, free, i = ads.take()
                    ld = p.dma(2 + i, lambda e, ad=ad, j=j, lo=lo, n=n: e.dma_start(
                        ad[:, 0:n], adj[j][:, lo:lo + n]), free)

                    def go(e, ad=ad, j=j, tiles=tiles):
                        for n, t in enumerate(tiles):
                            r = e.matmul(PS[0:P, n // 2, (n % 2) * D:(n % 2) * D + D],
                                         ad[:, n * P:n * P + P], HS[:, j, :],
                                         start=(j == 0 and n % 2 == 0), stop=j == T - 1,
                                         skip_group_check=True)
                        return r

                    m = p.pe(go, ld, free_b if j == 0 else None)
                    ads.give(i, m)
                for n in range(0, len(tiles), 2):
                    ts = tiles[n:n + 2]
                    free_b = finish(ts, PS[0:P, n // 2, 0:len(ts) * D].rearrange("p (t d) -> p t d", d=D), m)

        if start < 5 <= upto:
            with phase() as ctx:
                Y = sb(ctx, [P, T, D])
                XT = sb(ctx, [128, 2, N])
                HS = sb(ctx, [P, T, D])
                with ExitStack() as c:
                    marks = layernorm(c, X, Y)
                    p.flush()
                for layer in (1, 2, 3):
                    with ExitStack() as c:
                        bias = sb(c, [P, D])
                        bl = p.dma(10, lambda e, bias=bias, layer=layer: e.dma_start(
                            bias[:, :], broadcast_row(a[f"L2_gnn_b{layer}"], P)))
                        banks = Ring(range(8))
                        xm = transposed(Y, XT, [None] * T, banks)

                        def finish(ts, s, m, layer=layer, bias=bias, bl=bl):
                            k = len(ts)
                            y, hs = Y[:, ts[0]:ts[0] + k, :], HS[:, ts[0]:ts[0] + k, :]
                            dd = dis0[:, ts[0]:ts[0] + k].unsqueeze(2).broadcast_to([P, k, D])
                            bb = bias[:, :].unsqueeze(1).broadcast_to([P, k, D])
                            m = end = p.ve(lambda e: e.tensor_tensor(y, s, hs, ALU.add), m)
                            m = p.ve(lambda e: e.tensor_tensor(y, y, dd, ALU.mult), m)
                            m = p.ve(lambda e: e.tensor_tensor(y, y, bb, ALU.add), m, bl)
                            if layer < 3:
                                p.ve(lambda e: e.tensor_scalar(y, y, 0.0, None, ALU.max), m)
                            else:
                                x = X[:, ts[0]:ts[0] + k, :]
                                p.ve(lambda e: e.tensor_tensor(x, x, y, ALU.add), m)
                            return end

                        convolution(c, banks, XT, xm, a[f"L2_gnn_W{layer}"], dis0, HS, finish)
                        p.flush()

        if start < 6 <= upto:
            with phase() as ctx:
                banks = Ring(range(4))
                XT = sb(ctx, [128, 2, N])
                Cw = sb(ctx, [P, T, 8])
                none = [()] * 7
                with ExitStack() as c0:
                    XN = sb(c0, [P, T, D])
                    with ExitStack() as c:
                        marks = layernorm(c, X, XN)
                        xm = transposed(XN, XT, marks, Ring(range(8)))
                        p.flush()
                    Cw_, cm = routing(c0, XT, none, a["L2_ffn_Wr"], a["L2_ffn_br"], "plain", banks)
                    p.flush()
                    p.ve(lambda e: e.tensor_copy(Cw[:, :, :], Cw_[:, :, :]))
                    marks = layernorm(c0, XN, XN)
                    transposed(XN, XT, marks, Ring(range(8)))
                    p.flush()
                experts(ctx, XT, none, Cw, None, a["L2_ffn_W1"], a["L2_ffn_b1"], a["L2_ffn_W2"],
                        a["L2_ffn_b2"], 1024, (a["L2_ffn_ln_g"], a["L2_ffn_ln_b"]), banks,
                        Ring(range(4, 8)), None)

        if start < 7 <= upto:
            with phase() as ctx:
                Y = sb(ctx, [P, T, D])
                XT = sb(ctx, [128, 2, N])
                HS = sb(ctx, [P, T, D])
                outs = Ring([sb(ctx, [P, 2, D]) for _ in range(2)])
                marks = layernorm(ctx, X, Y)
                banks = Ring(range(8))
                xm = transposed(Y, XT, marks, banks)

                def finish3(ts, s, m):
                    k = len(ts)
                    dd = dis1[:, ts[0]:ts[0] + k].unsqueeze(2).broadcast_to([P, k, D])
                    x = X[:, ts[0]:ts[0] + k, :]
                    o, free, i = outs.take()
                    m = end = p.ve(lambda e: e.tensor_tensor(o[:, 0:k, :], s, dd, ALU.mult), m, free)
                    outs.give(i, p.ve(lambda e: e.tensor_tensor(x, x, o[:, 0:k, :], ALU.add), m))
                    return end

                convolution(ctx, banks, XT, xm, a["L3_gnn_W"], dis1, HS, finish3)

        if start < 8 <= upto:
            with phase() as ctx:
                XT = sb(ctx, [128, 2, N])
                banks = Ring(range(4))
                with ExitStack() as c:
                    XN = sb(c, [P, T, D])
                    marks = layernorm(c, X, XN)
                    transposed(XN, XT, marks, Ring(range(8)))
                    p.flush()
                none = [()] * 7
                Cw, cm = routing(ctx, XT, none, a["L3_ffn_Wg"], a["L3_ffn_bg"], None, banks)
                experts(ctx, XT, none, Cw, cm, a["L3_ffn_W1"], a["L3_ffn_b1"], a["L3_ffn_W2"],
                        a["L3_ffn_b2"], 512, None, banks, Ring(range(4, 8)), None)

        p.hold("sync", p.dma(0, lambda e: e.dma_start(a["out"].rearrange("(t p) d -> p t d", p=P), X[:, :, :])))
        p.flush()


def laid_out(inputs):
    import numpy as np

    x = {k: np.ascontiguousarray(v) for k, v in inputs.items()}
    out = {k: x[k] for k in (
        "x", "src", "dst", "L0_gnn_W", "L0_gnn_bias", "L0_ffn_w1", "L0_ffn_w2", "L0_ffn_b2",
        "L1_gnn_W1", "L1_gnn_W2", "L2_gnn_W1", "L2_gnn_b1", "L2_gnn_W2", "L2_gnn_b2", "L2_gnn_W3",
        "L2_gnn_b3", "L2_ffn_Wr", "L2_ffn_br", "L2_ffn_W1", "L2_ffn_W2", "L2_ffn_b2", "L3_gnn_W",
        "L3_ffn_Wg", "L3_ffn_bg", "L3_ffn_W1", "L3_ffn_W2", "L3_ffn_b2")}
    for k in ("i", "o", "c"):
        out[f"L1_ffn_U_{k}"] = x[f"L1_ffn_U_{k}"]
        out[f"L1_ffn_V_{k}"] = x[f"L1_ffn_V_{k}"]
        out[f"L1_ffn_b_{k}"] = np.ascontiguousarray(x[f"L1_ffn_b_{k}"].reshape(2, 128).T)
    for name, key in (("L0_gnn_WT", "L0_gnn_W"), ("L1_gnn_W1T", "L1_gnn_W1"), ("L1_gnn_W2T", "L1_gnn_W2"),
                      ("L0_ffn_router_wT", "L0_ffn_router_w")):
        out[name] = np.ascontiguousarray(x[key].T)
    for name, s, d in (("L0_gnn_AB", "L0_gnn_att_src", "L0_gnn_att_dst"),
                       ("L1_gnn_AB1", "L1_gnn_a1_src", "L1_gnn_a1_dst"),
                       ("L1_gnn_AB2", "L1_gnn_a2_src", "L1_gnn_a2_dst")):
        h, c = x[s].shape
        block = np.zeros((256, 2 * h), x[s].dtype)
        for i in range(h):
            block[i * c:(i + 1) * c, i] = x[s][i]
            block[i * c:(i + 1) * c, h + i] = x[d][i]
        out[name] = block
    for key in ("L0_ffn_b1", "L2_ffn_b1", "L3_ffn_b1"):
        e, h = x[key].shape
        out[key] = np.ascontiguousarray(x[key].reshape(e, h // 128, 128).transpose(0, 2, 1))
    for key in ("L2_ffn_ln_g", "L2_ffn_ln_b"):
        out[key] = np.ascontiguousarray(x[key].reshape(8, 2, 128).transpose(1, 2, 0))
    return out


def kernel(**inputs):
    import concourse.bacc as _bacc
    from concourse import mybir as _mybir
    from concourse.bass_utils import run_bass_kernel_spmd as _run

    nc = _bacc.Bacc("TRN2", target_bir_lowering=False, num_devices=1)
    arrays, args = {}, {}
    for name, v in laid_out(inputs).items():
        arrays[f"in_{name}"] = v
        args[name] = nc.dram_tensor(f"in_{name}", v.shape, _mybir.dt.from_np(v.dtype), kind="ExternalInput").ap()
    args["out"] = nc.dram_tensor("out_0", (3125, 256), _mybir.dt.float32, kind="ExternalOutput").ap()
    program(nc, args)
    r = _run(nc, [arrays], core_ids=[0])
    return r.results[0]["out_0"]
```

```python
import concourse.bass as bass
from concourse import mybir
from contextlib import ExitStack, contextmanager

N, E, D = 3125, 50000, 256
P, T = 125, 25
NN = N * N
HUGE = 1.0e30
CAP = 3.0e38
TOL = 2.0 ** -18
EPS = 1e-5
W, FOLD, ROWE = 18, 782, 2906


class Unit:

    def __init__(self, sem):
        self.sem, self.count, self.queue = sem, 0, []


class Program:

    NAMES = ("tensor", "vector", "scalar", "gpsimd", "sync")

    def __init__(self, nc, tag, lanes):
        self.nc = nc
        self.units = {n: Unit(nc.alloc_semaphore(f"{tag}_{n}")) for n in self.NAMES}
        self.lanes = [[nc.alloc_semaphore(f"{tag}_dma{i}"), 0] for i in range(lanes)]

    def add(self, name, fn, waits):
        u = self.units[name]
        u.count += 1
        u.queue.append((fn, [w for w in waits if w is not None], u.sem, 1))
        return (u.sem, u.count)

    def pe(self, fn, *waits):
        return self.add("tensor", fn, waits)

    def ve(self, fn, *waits):
        return self.add("vector", fn, waits)

    def se(self, fn, *waits):
        return self.add("scalar", fn, waits)

    def ge(self, fn, *waits):
        return self.add("gpsimd", fn, waits)

    def dma(self, lane, fn, *waits, by="sync"):
        at = self.lanes[lane]
        at[1] += 16
        self.units[by].queue.append((fn, [w for w in waits if w is not None], at[0], 16))
        return (at[0], at[1])

    def hold(self, name, *waits):
        self.units[name].queue.append((None, [w for w in waits if w is not None], None, 0))

    def flush(self):
        nc = self.nc
        with nc.Block() as block:
            for name in self.NAMES:
                queue, self.units[name].queue = self.units[name].queue, []

                def body(e, queue=queue):
                    passed = {}
                    if not queue:
                        e.nop()
                    for fn, waits, sem, by in queue:
                        for s, v in waits:
                            if passed.get(s.num, 0) < v:
                                e.wait_ge(s, v)
                                passed[s.num] = v
                        if fn is not None:
                            fn(e).then_inc(sem, by)

                block_of(block, name)(body)

    def numbers(self):
        nums = [u.sem.num for u in self.units.values()] + [s.num for s, _ in self.lanes]
        assert max(nums) - min(nums) + 1 == len(nums)
        return range(min(nums), max(nums) + 1)

    def rewind(self):
        for u in self.units.values():
            u.count = 0
        for lane in self.lanes:
            lane[1] = 0


def block_of(block, name):
    return {"tensor": block.tensor, "vector": block.vector, "scalar": block.scalar,
            "gpsimd": block.gpsimd, "sync": block.sync}[name]


class Ring:

    def __init__(self, items):
        self.items, self.free, self.at = list(items), [None] * len(items), -1

    def take(self):
        self.at = (self.at + 1) % len(self.items)
        return self.items[self.at], self.free[self.at], self.at

    def give(self, i, mark):
        self.free[i] = mark


def program(nc, a, upto=99, start=0):
    f32, bf16, i32, f16 = mybir.dt.float32, mybir.dt.bfloat16, mybir.dt.int32, mybir.dt.float16
    ALU = mybir.AluOpType
    ACT = mybir.ActivationFunctionType
    AX = mybir.AxisListType
    p = Program(nc, "m", 24)
    q = Program(nc, "r", 1)
    fb = Program(nc, "f", 7)
    top = ExitStack()
    names = [0]

    def sb(ctx, shape, dt=f32):
        names[0] += 1
        return ctx.enter_context(nc.sbuf_tensor(f"sb{names[0]}", shape, dt))

    @contextmanager
    def phase():
        with ExitStack() as ctx:
            yield ctx
            p.flush()

    A1 = nc.dram_tensor("adj", (NN + 128, 1), f32).ap()
    NEG = nc.dram_tensor("neg", (T, P, N), bf16).ap()
    ROWS = [nc.dram_tensor(f"rows{i}", (T * 4, P), f32).ap() for i in range(3)]
    EP = nc.dram_tensor("table", (ROWE, W * 4), f32).ap()
    KD = nc.dram_tensor("keys", (P, 400), f32).ap()
    adj = A1[0:NN, :].rearrange("(t p i) o -> t p (i o)", p=P, i=N)

    with top:
        PS = top.enter_context(nc.psum_tensor("ps", [128, 8, 512], f32))
        X = sb(top, [P, T, D])
        ident = sb(top, [128, 128])
        ones = sb(top, [128, 128])
        epsc = sb(top, [128, 1])
        deg = sb(top, [P, T])
        dis0 = sb(top, [P, T])
        dis1 = sb(top, [P, T])

        def bank(i, n=512, rows=128):
            return PS[0:rows, i, 0:n]

        def layernorm(ctx, src, dst, *waits):
            st = sb(ctx, [P, T, 6])
            mv = sb(ctx, [P, T, 2])
            rs = sb(ctx, [P, T, 2])
            for t in range(T):
                m = p.ve(lambda e, t=t: e.bn_stats(st[:, t, :], src[:, t, :]), *waits)
            for t in range(T):
                m = p.ve(lambda e, t=t: e.bn_aggr(mv[:, t, :], st[:, t, :]), m)
            m = p.se(lambda e: e.activation(rs[:, :, 0], mv[:, :, 1], ACT.Sqrt, bias=epsc[0:P, :]), m)
            m = p.ve(lambda e: e.reciprocal(rs[:, :, 1], rs[:, :, 0]), m)
            marks = []
            for t in range(T):
                marks.append(p.ve(lambda e, t=t: e.tensor_scalar(
                    dst[:, t, :], src[:, t, :], mv[:, t, 0:1], rs[:, t, 1:2], ALU.subtract, ALU.mult), m))
            return marks

        turn = [0]

        def evacuate(out, src, *marks):
            turn[0] += 1
            if turn[0] % 2:
                return p.se(lambda e: e.activation(out, src, ACT.Copy), *marks)
            return p.ve(lambda e: e.tensor_copy(out, src), *marks)

        def transposed(src, dst, marks, banks):
            out = []
            for g in range(7):
                ts = range(4 * g, min(4 * g + 4, T))
                both = []
                for h in range(2):
                    b, free, i = banks.take()

                    def go(e, ts=ts, h=h, b=b):
                        for n, t in enumerate(ts):
                            r = e.transpose(PS[:, b, n * P:n * P + P],
                                            src[:, t, h * 128:h * 128 + 128], ident[0:P, 0:P])
                        return r

                    m = p.pe(go, free, marks[ts[-1]])
                    n = len(ts) * P
                    m = evacuate(dst[:, h, 500 * g:500 * g + n], bank(b, n), m)
                    banks.give(i, m)
                    both.append(m)
                out.append(both)
            return out

        def rows_gemm(XT, W, marks, banks, sink, *waits):
            for t0 in range(0, T, 2):
                ts = range(t0, min(t0 + 2, T))
                b, free, i = banks.take()

                def go(e, ts=ts, b=b):
                    for n, t in enumerate(ts):
                        for k in range(2):
                            r = e.matmul(PS[0:P, b, n * D:n * D + D], XT[:, k, t * P:t * P + P],
                                         W[:, k, :], start=k == 0, stop=k == 1)
                    return r

                m = p.pe(go, free, *marks[ts[-1] // 4], *marks[ts[0] // 4], *waits)
                banks.give(i, sink(b, ts, m))

        def small_gemm(XT, W, n, marks, b, free, *waits):
            def go(e):
                for t in range(T):
                    for k in range(2):
                        r = e.matmul(PS[0:P, b, t * n:t * n + n], XT[:, k, t * P:t * P + P],
                                     W[:, k, :], start=k == 0, stop=k == 1)
                return r
            return p.pe(go, free, *[m for ms in marks for m in ms], *waits)

        def broadcast_row(ap, parts):
            return ap.unsqueeze(0).broadcast_to([parts, ap.shape[0]])

        with phase() as ctx:
            z = p.ge(lambda e: e.memset(ident[:, :], 0.0))
            p.ge(lambda e: e.affine_select(out=ident[:, :], in_=ident[:, :], compare_op=ALU.not_equal,
                                           fill=1.0, base=0, pattern=[[-1, 128]], channel_multiplier=1), z)
            p.ge(lambda e: e.memset(ones[:, :], 1.0))
            p.ge(lambda e: e.memset(epsc[:, :], EPS))
            p.hold("sync", p.dma(0, lambda e: e.dma_start(X[:, :, :], a["x"].rearrange("(t p) d -> p t d", p=P))))

        def edges(ctx):
            C, G = 400, 40
            se_, de = sb(ctx, [P, C], i32), sb(ctx, [P, C], i32)
            key = sb(ctx, [P, C])
            R = sb(ctx, [P, P, G])
            Q = sb(ctx, [P, G, P])
            low = sb(ctx, [P, P])
            cnt = sb(ctx, [P, C])
            dup = sb(ctx, [P, C])
            spare = sb(ctx, [P, 1])
            idx = sb(ctx, [P, C], i32)
            zero = sb(ctx, [P, N])
            z = p.ve(lambda e: e.memset(zero[:, :], 0.0))
            for t in range(T):
                zd = p.dma(3, lambda e, t=t: e.dma_start(adj[t], zero[:, :]), z)
            zd = p.dma(3, lambda e: e.dma_start(A1[NN:NN + 125, :], zero[:, 0:1]), z)
            l1 = p.dma(1, lambda e: e.dma_start(se_[:, :], a["src"].rearrange("(p c) -> p c", p=P)))
            l2 = p.dma(2, lambda e: e.dma_start(de[:, :], a["dst"].rearrange("(p c) -> p c", p=P)))
            m1 = p.ge(lambda e: e.memset(low[:, :], 1.0))
            m1 = p.ge(lambda e: e.affine_select(out=low[:, :], in_=low[:, :], compare_op=ALU.is_gt, fill=0.0,
                                                base=0, pattern=[[-1, P]], channel_multiplier=1), m1)
            m2 = p.ge(lambda e: e.iota(spare[:, :], [[0, 1]], base=NN, channel_multiplier=1,
                                       allow_small_or_imprecise_dtypes=True))
            k0 = p.ve(lambda e: e.scalar_tensor_tensor(key[:, :], se_[:, :], float(N), de[:, :],
                                                       ALU.mult, ALU.add), l1, l2)
            kd = p.dma(4, lambda e: e.dma_start(KD, key[:, :]), k0)
            flat = KD.rearrange("p c -> (p c)").unsqueeze(0).broadcast_to([P, P * C])\
                .rearrange("q (f c) -> q f c", c=C)
            read, done = None, None
            for g in range(C // G):
                s = slice(g * G, g * G + G)
                ld = p.dma(5, lambda e, s=s: e.dma_start(R[:, :, :], flat[:, :, s]), kd, read)
                m = p.ve(lambda e, s=s: e.tensor_tensor(
                    Q[:, :, :], R[:, :, :].rearrange("p f c -> p c f"),
                    key[:, s].unsqueeze(2).broadcast_to([P, G, P]), ALU.is_equal), ld, done)
                read = m
                m = p.ve(lambda e, s=s: e.tensor_reduce(cnt[:, s], Q[:, :, :], AX.X, ALU.add), m)
                m = p.ve(lambda e, s=s: e.tensor_tensor(
                    Q[:, :, :], Q[:, :, :], low[:, :].unsqueeze(1).broadcast_to([P, G, P]), ALU.mult), m, m1)
                m = p.ve(lambda e, s=s: e.tensor_reduce(dup[:, s], Q[:, :, :], AX.X, ALU.max), m)
                done = m
            m = p.ve(lambda e: e.tensor_scalar(zero[:, 0:C], key[:, :], spare[:, 0:1], None, ALU.subtract),
                     m, m2, zd)
            m = p.ve(lambda e: e.tensor_scalar(dup[:, :], dup[:, :], -1.0, 1.0, ALU.mult, ALU.add), m)
            m = p.ve(lambda e: e.tensor_tensor(zero[:, 0:C], zero[:, 0:C], dup[:, :], ALU.mult), m)
            m = p.ve(lambda e: e.tensor_scalar(idx[:, :], zero[:, 0:C], spare[:, 0:1], None, ALU.add), m)
            last = zd
            for c in range(C):
                last = p.dma(-1, lambda e, c=c: e.indirect_dma_start(
                    A1, bass.IndirectOffsetOnAxis(idx[:, c:c + 1], 0), cnt[:, c:c + 1], None,
                    compute_op=ALU.add), m, last, by="gpsimd")
            p.hold("gpsimd", last)

        def masks(ctx):
            tiles = Ring([sb(ctx, [P, T, P]) for _ in range(2)])
            outs = Ring([sb(ctx, [P, N], bf16) for _ in range(2)])
            banks = Ring(range(8))
            cols = A1[0:NN, :].rearrange("(t p i) o -> p t (i o)", p=P, i=N)
            dp = sb(ctx, [P, T, 7])
            z = p.ve(lambda e: e.memset(dp[:, :, :], 0.0))
            for bk in range(T):
                tile, free, i = tiles.take()
                ld = p.dma(1 + i, lambda e, tile=tile, bk=bk: e.dma_start(
                    tile[:, :, :], cols[:, :, bk * P:bk * P + P]), free)
                o, ofree, oi = outs.take()
                for g in range(7):
                    js = range(4 * g, min(4 * g + 4, T))
                    b, bfree, bi = banks.take()

                    def go(e, js=js, b=b, tile=tile):
                        for n, j in enumerate(js):
                            r = e.transpose(PS[0:P, b, n * P:n * P + P], tile[:, j, :], ident[0:P, 0:P])
                        return r

                    n = len(js) * P
                    last = p.pe(go, ld, bfree)
                    m = p.ve(lambda e, b=b, n=n, g=g, bk=bk: e.tensor_reduce(
                        dp[:, bk, g:g + 1], bank(b, n, P), AX.X, ALU.add), last, z)
                    m = p.ve(lambda e, b=b, n=n, g=g, o=o: e.tensor_scalar(
                        o[:, 500 * g:500 * g + n], bank(b, n, P), 0.0, -HUGE, ALU.is_equal, ALU.mult),
                        ofree)
                    banks.give(bi, m)
                tiles.give(i, last)
                outs.give(oi, p.dma(3 + oi, lambda e, o=o, bk=bk: e.dma_start(NEG[bk], o[:, :]), m, by="scalar"))
            p.hold("scalar", *outs.free)
            p.ve(lambda e: e.tensor_reduce(deg[:, :], dp[:, :, :], AX.X, ALU.add), m)

        redo = sb(top, [1, 1], i32)
        flat = EP.rearrange("r c -> (r c)")
        cols = A1[0:NN, :].rearrange("(t p i) o -> p t (i o)", p=P, i=N)
        with ExitStack() as ctx:
            ioN = sb(ctx, [128, N])
            ioF = sb(ctx, [128, FOLD], f16)
            at = sb(ctx, [128, T], i32)
            S = [sb(ctx, [128, FOLD + 2], bf16) for _ in range(8)]
            with ExitStack() as c:
                se_, de = sb(c, [P, 400], i32), sb(c, [P, 400], i32)
                rec = sb(c, [P, 400, 4])
                sf, df_ = sb(c, [P, 400]), sb(c, [P, 400])
                ge_ = [sb(c, [P, 400]) for _ in range(3)]
                below = sb(c, [P, T, 400])
                cnt = sb(c, [P, T])
                af = sb(c, [128, T])
                part = sb(c, [128, 1])
                pad = sb(c, [16, 577])
                l1 = p.dma(1, lambda e: e.dma_start(se_[:, :], a["src"].rearrange("(p c) -> p c", p=P)))
                l2 = p.dma(2, lambda e: e.dma_start(de[:, :], a["dst"].rearrange("(p c) -> p c", p=P)))
                g0 = p.ge(lambda e: e.iota(ioN[:, :], [[1, N]], base=0, channel_multiplier=0,
                                           allow_small_or_imprecise_dtypes=True))
                g1 = p.ge(lambda e: e.iota(part[:, :], [[0, 1]], base=0, channel_multiplier=1,
                                           allow_small_or_imprecise_dtypes=True))
                m = p.ve(lambda e: e.memset(pad[:, :], -1.0))
                zd = p.dma(3, lambda e: e.dma_start(
                    flat[4 * E:ROWE * W * 4].rearrange("(p c) -> p c", p=16), pad[:, :]), m)
                for t in S:
                    m = p.ve(lambda e, t=t: e.memset(t[:, FOLD:FOLD + 1], 1.0))
                    m = p.ve(lambda e, t=t: e.memset(t[:, FOLD + 1:FOLD + 2], 0.0))
                m0 = p.ve(lambda e: e.memset(rec[:, :, 3], 0.0))
                ms = p.ve(lambda e: e.tensor_copy(sf[:, :], se_[:, :]), l1)
                md = p.ve(lambda e: e.tensor_copy(df_[:, :], de[:, :]), l2)
                mg = [p.ve(lambda e, k=k: e.tensor_scalar(ge_[k][:, :], sf[:, :], float(FOLD * (k + 1)), None,
                                                          ALU.is_ge), ms) for k in range(3)]
                m = ms
                for k in range(3):
                    m = p.ve(lambda e, k=k: e.scalar_tensor_tensor(
                        sf[:, :], ge_[k][:, :], -float(FOLD), sf[:, :], ALU.mult, ALU.add), m, mg[2])
                w1 = p.ve(lambda e: e.tensor_copy(rec[:, :, 1], sf[:, :]), m)
                m = p.ve(lambda e: e.tensor_scalar(sf[:, :], ge_[0][:, :], 63.0, 1.0, ALU.mult, ALU.add), w1)
                m = p.ve(lambda e: e.scalar_tensor_tensor(sf[:, :], ge_[1][:, :], 4032.0, sf[:, :],
                                                          ALU.mult, ALU.add), m)
                w2 = p.ve(lambda e: e.scalar_tensor_tensor(rec[:, :, 2], ge_[2][:, :], 258048.0, sf[:, :],
                                                           ALU.mult, ALU.add), m)
                w0 = p.ve(lambda e: e.tensor_copy(rec[:, :, 0], df_[:, :]), md)
                wd = p.dma(4, lambda e: e.dma_start(
                    flat[0:4 * E].rearrange("(p c) -> p c", p=P),
                    rec[:, :, :].rearrange("p c k -> p (c k)")), m0, w0, w1, w2)
                m = p.ve(lambda e: e.tensor_tensor(
                    below[:, :, :], df_[:, :].unsqueeze(1).broadcast_to([P, T, 400]),
                    ioN[0:P, 0:T * P].rearrange("p (t i) -> p t i", i=P)[:, :, 0:1].broadcast_to([P, T, 400]),
                    ALU.is_lt), md, g0)
                m = p.ve(lambda e: e.tensor_reduce(cnt[:, :], below[:, :, :], AX.X, ALU.add), m)
                m = p.pe(lambda e: e.matmul(PS[:, 0, 0:T], ones[0:P, :], cnt[:, :], start=True, stop=True), m)
                m = p.ve(lambda e: e.tensor_scalar(af[:, :], PS[:, 0, 0:T], 1.0 / W, -0.55, ALU.mult, ALU.add), m)
                m = p.ve(lambda e: e.tensor_scalar(af[:, :], af[:, :], 0.0, None, ALU.max), m)
                m = p.ve(lambda e: e.tensor_copy(at[:, :], af[:, :]), m)
                m = p.ve(lambda e: e.tensor_copy(af[:, :], at[:, :]), m)
                m = p.ve(lambda e: e.tensor_scalar(af[:, :], af[:, :], part[:, 0:1], None, ALU.add), m, g1)
                p.ve(lambda e: e.tensor_copy(at[:, :], af[:, :]), m)
                p.ve(lambda e: e.tensor_copy(ioF[:, :], ioN[:, 0:FOLD]), g0)
                p.hold("sync", zd, wd)
                p.flush()
            egs = Ring([sb(ctx, [128, W, 4]) for _ in range(3)])
            dts = Ring([sb(ctx, [128, W, P], bf16) for _ in range(2)])
            hots = Ring(S)
            sums = Ring((0, 2))
            vis = Ring([sb(ctx, [P, 2, 392], i32) for _ in range(2)])
            qis = Ring([sb(ctx, [P, FOLD], i32) for _ in range(3)])
            ats = Ring([sb(ctx, [P, 4 * FOLD]) for _ in range(2)])
            outs = Ring([sb(ctx, [P, N], bf16) for _ in range(2)])
            oas = Ring([sb(ctx, [P, T, P]) for _ in range(2)])
            banks = Ring(range(4, 8))

            def front(b):
                eg, free, ei = egs.take()
                ld = p.dma(-1, lambda e: e.indirect_dma_start(
                    eg[:, :, :].rearrange("p w k -> p (w k)"), None, EP,
                    bass.IndirectOffsetOnAxis(at[:, b:b + 1], 0)), *(free or []), by="gpsimd")
                dt, free, di = dts.take()
                for w in range(W):
                    md = p.ge(lambda e, w=w: e.tensor_scalar(
                        dt[:, w, :], ioN[:, b * P:b * P + P], eg[:, w, 0:1], None, ALU.is_equal), ld, free)
                bank2, bfree, bi = sums.take()
                for w in range(W):
                    hot, hfree, hi = hots.take()
                    ms = p.ve(lambda e, w=w, hot=hot: e.tensor_scalar(
                        hot[:, 0:FOLD], ioF[:, :], eg[:, w, 1:2], eg[:, w, 2:3], ALU.is_equal, ALU.mult),
                        ld, hfree)

                    def go(e, w=w, hot=hot):
                        for k in range(2):
                            r = e.matmul(PS[0:P, bank2 + k, 0:392], dt[:, w, :], hot[:, 392 * k:392 * k + 392],
                                         start=w == 0, stop=w == W - 1)
                        return r

                    m = p.pe(go, ms, md, *((bfree or []) if w == 0 else []))
                    hots.give(hi, m)
                egs.give(ei, [ms, md])
                dts.give(di, m)
                return b, bank2, bi, m

            def back(b, bank2, bi, mark):
                vi, free, vv = vis.take()
                m1 = p.se(lambda e: e.activation(vi[:, :, :], PS[0:P, bank2:bank2 + 2, 0:392], ACT.Copy),
                          mark, free)
                p.ve(lambda e: e.tensor_copy(deg[:, b:b + 1], vi[:, 1, FOLD - 392:FOLD - 391]), m1)
                sums.give(bi, [m1])
                A, afree, ai = ats.take()
                flat_v = vi[:, :, :].rearrange("p a c -> p (a c)")
                for k in range(4):
                    qi, free, qq = qis.take()
                    m = p.ve(lambda e, k=k, qi=qi: e.tensor_scalar(
                        qi[:, :], flat_v[:, 0:FOLD], 6 * k, 63, ALU.logical_shift_right, ALU.bitwise_and),
                        m1, free)
                    mc = p.se(lambda e, k=k, qi=qi: e.activation(
                        A[:, FOLD * k:FOLD * k + FOLD], qi[:, :], ACT.Copy), m, *(afree or []))
                    qis.give(qq, mc)
                vis.give(vv, m)
                o, free, oi = outs.take()
                mn = p.ve(lambda e: e.tensor_scalar(o[:, :], A[:, 0:N], 0.0, -HUGE, ALU.is_equal, ALU.mult),
                          mc, free)
                outs.give(oi, p.dma(1 + oi, lambda e: e.dma_start(NEG[b], o[:, :]), mn, by="sync"))
                oa, ofree, ii = oas.take()
                for g in range(7):
                    js = range(4 * g, min(4 * g + 4, T))
                    bk, bfree, bki = banks.take()

                    def go(e, js=js, bk=bk):
                        for n, j in enumerate(js):
                            r = e.transpose(PS[0:P, bk, n * P:n * P + P], A[:, j * P:j * P + P],
                                            ident[0:P, 0:P])
                        return r

                    mt = p.pe(go, mc, bfree)
                    m = p.se(lambda e, js=js, bk=bk: e.activation(
                        oa[:, js[0]:js[-1] + 1, :].rearrange("p t i -> p (t i)"),
                        bank(bk, len(js) * P, P), ACT.Copy), mt, ofree)
                    banks.give(bki, m)
                ats.give(ai, [mn, mt])
                oas.give(ii, p.dma(3 + ii, lambda e: e.dma_start(cols[:, :, b * P:b * P + P], oa[:, :, :]), m,
                                   by="sync"))

            before = None
            for b in range(T):
                now = front(b)
                if before:
                    back(*before)
                before = now
            back(*before)
            p.hold("sync", *outs.free, *oas.free)
            p.flush()
            rd = sb(ctx, [P, 2])
            rr = sb(ctx, [1, 4])
            m = p.ve(lambda e: e.tensor_reduce(rd[:, 0:1], deg[:, :], AX.X, ALU.add))
            m = p.ve(lambda e: e.tensor_reduce(rd[:, 1:2], deg[:, :], AX.X, ALU.max), m)

            def go(e):
                e.matmul(PS[0:1, 0, 0:2], ones[0:P, 0:1], rd[:, :], start=True, stop=True)
                return e.transpose(PS[0:1, 1, 0:P], rd[:, 1:2], ident[0:P, 0:P])

            m = p.pe(go, m)
            m1 = p.ve(lambda e: e.tensor_scalar(rr[:, 0:1], PS[0:1, 0, 0:1], float(E), None, ALU.not_equal), m)
            m2 = p.ve(lambda e: e.tensor_reduce(rr[:, 1:2], PS[0:1, 1, 0:P], AX.X, ALU.max), m)
            m2 = p.ve(lambda e: e.tensor_scalar(rr[:, 2:3], rr[:, 1:2], 63.0, None, ALU.is_gt), m2)
            p.ve(lambda e: e.tensor_tensor(redo[:, :], rr[:, 0:1], rr[:, 2:3], ALU.max), m1, m2)
            p.flush()
        flag = nc.values_load(redo[0:1, 0:1], min_val=0, max_val=1)
        nc.all_engine_barrier(sem_only=True)
        with nc.If(flag == 1):
            main, p = p, fb
            with phase() as ctx:
                edges(ctx)
            with phase() as ctx:
                masks(ctx)
            p = main

        with phase() as ctx:
            m = None
            tmp = sb(ctx, [P, T, 3])
            m1 = p.ve(lambda e: e.tensor_scalar(tmp[:, :, 0], deg[:, :], 1.0, None, ALU.add), m)
            m1 = p.se(lambda e: e.activation(tmp[:, :, 0], tmp[:, :, 0], ACT.Sqrt), m1)
            m1 = p.ve(lambda e: e.reciprocal(dis0[:, :], tmp[:, :, 0]), m1)
            m1 = p.ve(lambda e: e.tensor_scalar(tmp[:, :, 1], deg[:, :], 1.0, None, ALU.max), m1)
            m1 = p.se(lambda e: e.activation(tmp[:, :, 1], tmp[:, :, 1], ACT.Sqrt), m1)
            m1 = p.ve(lambda e: e.reciprocal(tmp[:, :, 1], tmp[:, :, 1]), m1)
            m1 = p.ve(lambda e: e.tensor_scalar(tmp[:, :, 2], deg[:, :], 0.0, None, ALU.is_gt), m1)
            p.ve(lambda e: e.tensor_tensor(dis1[:, :], tmp[:, :, 1], tmp[:, :, 2], ALU.mult), m1)

        def to_rows(ctx, cols, n, ROW, bank_i, lane, *waits):
            k = T * n
            tmp = sb(ctx, [k, P])
            flat = cols.rearrange("p t n -> p (t n)")
            m = p.pe(lambda e: e.transpose(PS[0:k, bank_i, 0:P], flat, ident[0:P, 0:P]), *waits)
            m = p.se(lambda e: e.activation(tmp[:, :], PS[0:k, bank_i, 0:P], ACT.Copy), m)
            return p.dma(lane, lambda e: e.dma_start(ROW[0:k, :], tmp[:, :]), m)

        def from_row(row, ROW, n, h, lane, *waits):
            src = ROW[0:T * n, :].rearrange("(t n) i -> n t i", n=n)[h]
            return p.dma(lane, lambda e: e.dma_start(
                row[:, :].rearrange("p (t i) -> p t i", i=P),
                src.unsqueeze(0).broadcast_to([P, T, P])), *waits)

        def attention(ctx, H, C, HA, SD, loops, finish):
            M = sb(ctx, [P, T, H])
            c1 = sb(ctx, [P, T, H])
            c2 = sb(ctx, [P, T, H])
            s2 = sb(ctx, [P, T, H])
            s8 = sb(ctx, [P, T, H])
            sc = sb(ctx, [P, T, H])
            with ExitStack() as c:
                SR = [sb(c, [P, N]) for _ in range(H)]
                negs = Ring([sb(c, [P, N], bf16) for _ in range(3)])
                junk = Ring([sb(c, [P, N], bf16) for _ in range(2)])
                notI = sb(c, [P, P])
                ni = p.ve(lambda e: e.tensor_scalar(notI[:, :], ident[0:P, 0:P], -1.0, 1.0, ALU.mult, ALU.add))
                m = p.ve(lambda e: e.tensor_copy(sc[:, :, :], SD[:, :, 0:H]))
                m = to_rows(c, sc[:, :, :], H, ROWS[0], 0, 11, m)
                marks = [from_row(SR[h], ROWS[0], H, h, 12 + h, m) for h in range(H)]
                for b in range(T):
                    neg, free, i = negs.take()
                    ld = p.dma(1 + i, lambda e, neg=neg, b=b: e.dma_start(neg[:, :], NEG[b]), free)
                    if loops:
                        ld = p.ve(lambda e, neg=neg, b=b: e.tensor_tensor(
                            neg[:, b * P:b * P + P], neg[:, b * P:b * P + P], notI[:, :], ALU.mult), ld, ni)
                    for h in range(H):
                        j, jfree, ji = junk.take()
                        m = p.ve(lambda e, j=j, neg=neg, h=h, b=b: e.tensor_tensor_reduce(
                            out=j[:, :], in0=neg[:, :], in1=SR[h][:, :], scale=1.0, scalar=-HUGE,
                            op0=ALU.add, op1=ALU.max, accum_out=M[:, b, h:h + 1]), ld, marks[h], jfree)
                        junk.give(ji, m)
                    negs.give(i, m)
                d = SD[:, :, H:2 * H]
                m = p.ve(lambda e: e.tensor_tensor(c1[:, :, :], M[:, :, :], d, ALU.add), m)
                m = p.ve(lambda e: e.scalar_tensor_tensor(M[:, :, :], c1[:, :, :], 0.2, c1[:, :, :],
                                                          ALU.mult, ALU.max), m)
                m = p.ve(lambda e: e.tensor_scalar(c1[:, :, :], d, 0.8, None, ALU.mult), m)
                m = p.ve(lambda e: e.tensor_scalar(s8[:, :, :], SD[:, :, 0:H], 0.8, None, ALU.mult), m)
                m = p.ve(lambda e: e.scalar_tensor_tensor(c2[:, :, :], d, 0.2, M[:, :, :],
                                                          ALU.mult, ALU.subtract), m)
                p.ve(lambda e: e.tensor_scalar(s2[:, :, :], SD[:, :, 0:H], 0.2, None, ALU.mult), m)
                r1 = to_rows(c, c1[:, :, :], H, ROWS[1], 1, 16, m)
                r2 = to_rows(c, c2[:, :, :], H, ROWS[2], 2, 17, m)
                p.hold("sync", r1, r2)
                p.flush()
            wide = C > 128
            G = min(H, 2)
            R = [[sb(ctx, [P, N]) for _ in range(2)] for _ in range(G)]
            sets = ([range(0, 7), range(7, 13), range(13, 19), range(19, 25)] if wide else
                    [range(0, 9), range(9, 17), range(17, 25)])
            most = len(sets[0])
            work = Ring([sb(ctx, [P, most * P]) for _ in range(9)])
            ads = Ring([sb(ctx, [P, most * P]) for _ in range(5 if wide else 4)])
            turned = Ring([sb(ctx, [C + 1, most * P]) for _ in range(G)]) if not wide else None
            spare = Ring((6, 7))
            whole = {}
            last = [[None, None] for _ in range(G)]
            added = [[None, None] for _ in range(G)]
            ended = [None] * G
            pending, later = [], []
            count = [0]

            def closing(g, h, tiles, mark):
                if wide:
                    for n, t in enumerate(tiles):
                        s = PS[0:P, n, 0:C + 1].unsqueeze(1)
                        ends = yield from finish(h, t, 1, s, mark)
                        ended[g] = ends
                    return
                OT, free, oi = turned.take()
                marks = []
                for b, (lo, n) in enumerate(pieces(tiles)):
                    marks.append(evacuate(OT[:, lo:lo + n], PS[0:C + 1, 3 * g + b, 0:n], mark, free))
                ended[g] = marks
                yield
                for t0 in range(0, len(tiles), 5):
                    ts = tiles[t0:t0 + 5]
                    b, bfree, bi = spare.take()

                    def go(e, b=b, t0=t0, k=len(ts)):
                        for n in range(k):
                            r = e.transpose(PS[0:P, b, n * (C + 1):(n + 1) * (C + 1)],
                                            OT[:, (t0 + n) * P:(t0 + n + 1) * P], ident[0:C + 1, 0:C + 1])
                        return r

                    m = p.pe(go, bfree, *marks)
                    turned.give(oi, m)
                    yield
                    s = PS[0:P, b, 0:len(ts) * (C + 1)].rearrange("p (t c) -> p t c", c=C + 1)
                    end = yield from finish(h, ts[0], len(ts), s, m)
                    spare.give(bi, end)
                    yield

            def pieces(tiles):
                k = 3 if len(tiles) == 9 else 4
                return [(t * P, k * P) for t in range(0, len(tiles), k)]

            def advance():
                if later and next(later[0], "end") == "end":
                    later.pop(0)

            def second(u):
                h, g, j, tiles, w, wi, ad, ai, ld, first_mark = u
                n = len(tiles) * P
                if loops and j in tiles and ld not in whole:
                    whole[ld] = p.ve(lambda e, at=(j - tiles[0]) * P: e.tensor_tensor(
                        ad[:, at:at + P], ad[:, at:at + P], ident[0:P, 0:P], ALU.add), ld)
                ld = whole.get(ld, ld)
                mk = p.se(lambda e: e.activation(w[:, 0:n], w[:, 0:n], ACT.Exp, bias=s2[:, j, h:h + 1]),
                          first_mark)
                mk = p.ve(lambda e: e.scalar_tensor_tensor(
                    w[:, 0:n], w[:, 0:n], CAP, ad[:, 0:n], ALU.min, ALU.mult), mk, ld)
                masked.setdefault(ai, []).append(mk)
                if g == G - 1:
                    ads.give(ai, masked.pop(ai))

                def go(e):
                    if wide:
                        for n in range(len(tiles)):
                            r = e.matmul(PS[0:P, n, 0:C + 1], w[:, n * P:n * P + P], HA[:, j, h, :],
                                         start=j == 0, stop=j == T - 1)
                    else:
                        for b, (lo, k) in enumerate(pieces(tiles)):
                            r = e.matmul(PS[0:C + 1, 3 * g + b, 0:k], HA[:, j, h, :], w[:, lo:lo + k],
                                         start=j == 0, stop=j == T - 1)
                    return r

                mk = p.pe(go, mk, *((ended[g] or []) if j == 0 else []))
                work.give(wi, mk)
                if j == T - 1:
                    end = closing(g, h, tiles, mk)
                    next(end, None)
                    later.append(end)
                else:
                    advance()

            masked = {}
            for h0 in range(0, H, G):
                rows = [[from_row(R[g][0], ROWS[1], H, h0 + g, 12 + 2 * g, last[g][0]),
                         from_row(R[g][1], ROWS[2], H, h0 + g, 13 + 2 * g, *added[g])] for g in range(G)]
                for tiles in sets:
                    lo, n = tiles[0] * P, len(tiles) * P
                    for j in range(T):
                        ad, free, ai = ads.take()
                        ld = p.dma(1 + ai, lambda e, ad=ad, j=j, lo=lo, n=n: e.dma_start(
                            ad[:, 0:n], adj[j][:, lo:lo + n]), *(free or []))
                        for g in range(G):
                            h = h0 + g
                            w, wfree, wi = work.take()
                            last[g][0] = p.se(lambda e, w=w, j=j, h=h, g=g, lo=lo, n=n: e.activation(
                                w[:, 0:n], R[g][0][:, lo:lo + n], ACT.Relu, bias=s8[:, j, h:h + 1]),
                                rows[g][0], wfree)
                            count[0] += 1
                            adder = p.ge if count[0] % 3 == 0 and not wide else p.ve
                            last[g][1] = adder(
                                lambda e, w=w, g=g, lo=lo, n=n: e.tensor_tensor(
                                    w[:, 0:n], w[:, 0:n], R[g][1][:, lo:lo + n], ALU.add),
                                rows[g][1], last[g][0])
                            added[g][count[0] % 3 == 0] = last[g][1]
                            pending.append((h, g, j, tiles, w, wi, ad, ai, ld, last[g][1]))
                            if len(pending) > 3:
                                second(pending.pop(0))
                    while wide and pending:
                        second(pending.pop(0))
                    while wide and later:
                        advance()
                while pending:
                    second(pending.pop(0))
            while later:
                advance()

        def gat(XTm, banks, ctx, XT, W, WN, AB, H, C, HA, SD):
            w = sb(ctx, [128, 2, D])
            wn = sb(ctx, [128, 2, D])
            ab = sb(ctx, [128, 2, 2 * H])
            wa = sb(ctx, [128, 2, 2 * H])
            l1 = p.dma(1, lambda e: e.dma_start(w[:, :, :], W.rearrange("(k p) n -> p k n", p=128)))
            l2 = p.dma(2, lambda e: e.dma_start(wn[:, :, :], WN.rearrange("(k p) n -> p k n", p=128)))
            l3 = p.dma(3, lambda e: e.dma_start(ab[:, :, :], AB.rearrange("(k p) n -> p k n", p=128)))
            b, free, i = banks.take()

            def go(e):
                for k in range(2):
                    for c in range(2):
                        r = e.matmul(PS[:, b, 64 * k:64 * k + 2 * H], wn[:, c, k * 128:k * 128 + 128],
                                     ab[:, c, :], start=c == 0, stop=c == 1)
                return r

            m = p.pe(go, l2, l3, free)
            for k in range(2):
                m2 = p.ve(lambda e, k=k: e.tensor_copy(wa[:, k, :], PS[:, b, 64 * k:64 * k + 2 * H]), m)
            banks.give(i, m2)
            b2, free, i = banks.take()
            m = small_gemm(XT, wa, 2 * H, XTm, b2, free, m2)
            m = p.ve(lambda e: e.tensor_copy(SD[:, :, :].rearrange("p t n -> p (t n)"),
                                             bank(b2, T * 2 * H, P)), m)
            banks.give(i, m)
            p.ge(lambda e: e.memset(HA[:, :, :, C:C + 1], 1.0))

            def sink(b, ts, m):
                return evacuate(HA[:, ts[0]:ts[-1] + 1, :, 0:C],
                                bank(b, len(ts) * D, P).rearrange("p (t h c) -> p t h c", h=H, c=C), m)

            rows_gemm(XT, w, XTm, banks, sink, l1)

        def reciprocals(rec, k, s, C, mark):
            m = p.ve(lambda e: e.tensor_scalar(rec[:, 0:k, :], s[:, :, C:C + 1], 1e-16, None, ALU.add), mark)
            m = p.ve(lambda e: e.reciprocal(rec[:, 0:k, :], rec[:, 0:k, :]), m)
            return rec[:, 0:k, :].broadcast_to([P, k, C]), m

        if start < 1 <= upto:
            with phase() as ctx:
                HA = sb(ctx, [P, T, 4, 65])
                SD = sb(ctx, [P, T, 8])
                with ExitStack() as c:
                    XN = sb(c, [P, T, D])
                    XT = sb(c, [128, 2, N])
                    marks = layernorm(c, X, XN)
                    banks = Ring(range(8))
                    xm = transposed(XN, XT, marks, banks)
                    gat(xm, banks, c, XT, a["L0_gnn_WT"], a["L0_gnn_W"], a["L0_gnn_AB"], 4, 64, HA, SD)
                    p.ve(lambda e: e.tensor_tensor(X[:, :, :], X[:, :, :], XN[:, :, :], ALU.add), marks[-1])
                    p.flush()
                bias = sb(ctx, [P, D])
                rec = sb(ctx, [P, 7, 1])
                o = sb(ctx, [P, 7, 64])
                o2 = sb(ctx, [P, 7, 64])
                bl = p.dma(10, lambda e: e.dma_start(bias[:, :], broadcast_row(a["L0_gnn_bias"], P)))

                def finish(h, t0, k, s, mark):
                    r, m = reciprocals(rec, k, s, 64, mark)
                    end = m = p.ve(lambda e: e.tensor_tensor(o[:, 0:k, :], s[:, :, 0:64], r, ALU.mult), m)
                    m = p.ve(lambda e: e.tensor_tensor(
                        o[:, 0:k, :], o[:, 0:k, :],
                        bias[:, 64 * h:64 * h + 64].unsqueeze(1).broadcast_to([P, k, 64]), ALU.add), m, bl)
                    m = p.ve(lambda e: e.tensor_scalar(o2[:, 0:k, :], o[:, 0:k, :], 0.0, None, ALU.min), m)
                    yield
                    m = p.se(lambda e: e.activation(o2[:, 0:k, :], o2[:, 0:k, :], ACT.Exp), m)
                    yield
                    m = p.ve(lambda e: e.scalar_tensor_tensor(o[:, 0:k, :], o[:, 0:k, :], 0.0,
                                                              o2[:, 0:k, :], ALU.max, ALU.add), m)
                    x = X[:, t0:t0 + k, 64 * h:64 * h + 64]
                    p.ve(lambda e: e.scalar_tensor_tensor(x, o[:, 0:k, :], -1.0, x, ALU.add, ALU.add), m)
                    return end

                attention(ctx, 4, 64, HA, SD, True, finish)

        def routing(ctx, XT, xm, Wr, bias, norm, banks):
            wr = sb(ctx, [128, 2, 8])
            L = sb(ctx, [P, T, 8])
            R = sb(ctx, [P, T, 8])
            O1, O2, K = sb(ctx, [P, T, 8]), sb(ctx, [P, T, 8]), sb(ctx, [P, T, 8])
            io = sb(ctx, [P, 8])
            s1 = sb(ctx, [P, T, 1])
            l1 = p.dma(14, lambda e: e.dma_start(wr[:, :, :], Wr.rearrange("(k p) n -> p k n", p=128)))
            i0 = p.ge(lambda e: e.iota(io[:, :], [[1, 8]], base=0, channel_multiplier=0,
                                       allow_small_or_imprecise_dtypes=True))
            b, free, i = banks.take()
            m = small_gemm(XT, wr, 8, xm, b, free, l1)
            lv = PS[0:P, b, 0:8 * T].rearrange("p (t n) -> p t n", n=8)
            if bias is not None:
                br = sb(ctx, [P, 8])
                l2 = p.dma(15, lambda e: e.dma_start(br[:, :], broadcast_row(bias, P)))
                m = p.ve(lambda e: e.tensor_tensor(L[:, :, :], lv, br[:, :].unsqueeze(1).broadcast_to([P, T, 8]),
                                                   ALU.add), m, l2)
            else:
                m = p.ve(lambda e: e.tensor_copy(L[:, :, :], lv), m)
            banks.give(i, m)
            sx = s1[:, :, :].broadcast_to([P, T, 8])
            iob = io[:, :].unsqueeze(1).broadcast_to([P, T, 8])

            def red(src, op, m):
                return p.ve(lambda e: e.tensor_reduce(s1[:, :, 0], src[:, :, :], AX.X, op), m)

            def tt(out, x, y, op, m, *w):
                return p.ve(lambda e: e.tensor_tensor(out[:, :, :], x[:, :, :] if x is not None else None, y, op),
                            m, *w)

            if norm is not None:
                m = red(L, ALU.max, m)
                m = tt(L, L, sx, ALU.subtract, m)
                m = p.se(lambda e: e.activation(L[:, :, :], L[:, :, :], ACT.Exp), m)
                m = red(L, ALU.add, m)
                m = p.ve(lambda e: e.reciprocal(s1[:, :, :], s1[:, :, :]), m)
                m = tt(L, L, sx, ALU.mult, m)

            def first(src, out, m):
                m = red(src, ALU.max, m)
                m = tt(K, src, sx, ALU.is_equal, m)
                m = p.ve(lambda e: e.scalar_tensor_tensor(K[:, :, :], K[:, :, :], -8.0, iob, ALU.mult, ALU.add),
                         m, i0)
                m = red(K, ALU.min, m)
                return tt(out, K, sx, ALU.is_equal, m)

            m = first(L, O1, m)
            m = p.ve(lambda e: e.scalar_tensor_tensor(R[:, :, :], O1[:, :, :], -HUGE, L[:, :, :],
                                                      ALU.mult, ALU.add), m)
            m = first(R, O2, m)
            m = tt(O1, O1, O2[:, :, :], ALU.add, m)
            if norm is not None:
                m = tt(O1, O1, L[:, :, :], ALU.mult, m)
                m = red(O1, ALU.add, m)
                if norm == "probs":
                    m = p.ve(lambda e: e.tensor_scalar(s1[:, :, :], s1[:, :, :], 1e-12, None, ALU.max), m)
                m = p.ve(lambda e: e.reciprocal(s1[:, :, :], s1[:, :, :]), m)
                m = tt(O1, O1, sx, ALU.mult, m)
            return O1, m

        def experts(ctx, XT, xm, Cw, cm, W1, b1, W2, b2, hid, scale, banks1, banks2, xready):
            nh = hid // 128
            w1s = [sb(ctx, [128, 2, hid]) for _ in range(2)]
            w2s = [sb(ctx, [128, nh, D]) for _ in range(2)]
            b1s = [sb(ctx, [128, nh]) for _ in range(2)]
            hts = Ring([sb(ctx, [128, nh, 500]) for _ in range(2)])
            xes = Ring([sb(ctx, [128, 2, 500]) for _ in range(2)]) if scale else None
            if scale:
                gb = sb(ctx, [128, 2, 8])
                bb = sb(ctx, [128, 2, 8])
                lg = p.dma(12, lambda e: e.dma_start(gb[:, :, :], scale[0].rearrange("k p n -> p k n")))
                lb = p.dma(13, lambda e: e.dma_start(bb[:, :, :], scale[1].rearrange("k p n -> p k n")))
            CT = sb(ctx, [8, N])
            b2s = sb(ctx, [8, D])
            l2 = p.dma(11, lambda e: e.dma_start(b2s[:, :], b2))
            for g in range(7):
                ts = range(4 * g, min(4 * g + 4, T))
                b, free, i = banks1.take()

                def go(e, ts=ts, b=b):
                    for n, t in enumerate(ts):
                        r = e.transpose(PS[0:8, b, n * P:n * P + P], Cw[:, t, :], ident[0:P, 0:P])
                    return r

                m = p.pe(go, free, cm)
                ct = p.se(lambda e, b=b, g=g, n=len(ts) * P: e.activation(
                    CT[:, 500 * g:500 * g + n], PS[0:8, b, 0:n], ACT.Copy), m)
                banks1.give(i, ct)
            xlast = xready
            for t0 in range(0, T, 2):
                ts = range(t0, min(t0 + 2, T))
                b, free, i = banks2.take()

                def go(e, ts=ts, b=b):
                    for n, t in enumerate(ts):
                        r = e.matmul(PS[0:P, b, n * D:n * D + D], CT[:, t * P:t * P + P], b2s[:, :],
                                     start=True, stop=True)
                    return r

                m = p.pe(go, free, ct, l2)
                xs = X[:, ts[0]:ts[-1] + 1, :].rearrange("p t d -> p (t d)")
                xlast = p.ve(lambda e, b=b, xs=xs, n=len(ts) * D: e.tensor_tensor(
                    xs, xs, bank(b, n, P), ALU.add), m, xready)
                banks2.give(i, xlast)
            used = [None, None]
            loads = {}

            def load(ex):
                i = ex % 2
                w = used[i]
                loads[ex] = [
                    p.dma(1 + 3 * i, lambda e, i=i, ex=ex: e.dma_start(
                        w1s[i][:, :, :], W1[ex].rearrange("(k p) n -> p k n", p=128)), w),
                    p.dma(2 + 3 * i, lambda e, i=i, ex=ex: e.dma_start(
                        w2s[i][:, :, :], W2[ex].rearrange("(k p) n -> p k n", p=128)), w),
                    p.dma(3 + 3 * i, lambda e, i=i, ex=ex: e.dma_start(b1s[i][:, :], b1[ex]), w)]

            def up(ex, g):
                n = min(500, N - 500 * g)
                i = ex % 2
                if scale:
                    xe, xf, xi = xes.take()
                    for k in range(2):
                        m = p.ve(lambda e, k=k: e.tensor_scalar(
                            xe[:, k, 0:n], XT[:, k, 500 * g:500 * g + n], gb[:, k, ex:ex + 1],
                            bb[:, k, ex:ex + 1], ALU.mult, ALU.add), xf, lg, lb, *[y for x in xm for y in x])
                    src, xw = (lambda k: xe[:, k, 0:n]), [m]
                else:
                    src, xw = (lambda k: XT[:, k, 500 * g:500 * g + n]), xm[g]
                ht, hf, hi = hts.take()
                last = None
                for c in range(nh):
                    b, free, bi = banks1.take()

                    def go(e, b=b, c=c):
                        for k in range(2):
                            r = e.matmul(bank(b, n), w1s[i][:, k, 128 * c:128 * c + 128], src(k),
                                         start=k == 0, stop=k == 1)
                        return r

                    m = p.pe(go, free, *loads[ex], *xw)
                    if scale:
                        xes.give(xi, m)
                    last = p.se(lambda e, b=b, c=c: e.activation(
                        ht[:, c, 0:n], bank(b, n), ACT.Gelu, bias=b1s[i][:, c:c + 1]), m, hf)
                    banks1.give(bi, last)
                return ht, hi, last

            def down(ex, g, ht, hi, ready):
                nonlocal xlast
                i = ex % 2
                ts = range(4 * g, min(4 * g + 4, T))
                for t0 in range(0, len(ts), 2):
                    pair = ts[t0:t0 + 2]
                    b, free, bi = banks2.take()

                    def go(e, b=b, pair=pair, t0=t0):
                        for n in range(len(pair)):
                            for c in range(nh):
                                r = e.matmul(PS[0:P, b, n * D:n * D + D],
                                             ht[:, c, (t0 + n) * P:(t0 + n) * P + P],
                                             w2s[i][:, c, :], start=c == 0, stop=c == nh - 1)
                        return r

                    m = p.pe(go, free, ready, *loads[ex])
                    for n, t in enumerate(pair):
                        xlast = p.ve(lambda e, b=b, n=n, t=t: e.scalar_tensor_tensor(
                            X[:, t, :], PS[0:P, b, n * D:n * D + D], Cw[:, t, ex:ex + 1], X[:, t, :],
                            ALU.mult, ALU.add), m, lastx.get(t) or xlast)
                        lastx[t] = xlast
                    banks2.give(bi, xlast)
                hts.give(hi, m)
                return m

            lastx = {}
            load(0)
            load(1)
            before = None
            for ex in range(8):
                for g in range(7):
                    now = (ex, g, *up(ex, g))
                    if before:
                        m = down(*before)
                        if before[1] == 6:
                            used[before[0] % 2] = m
                            if before[0] + 2 < 8:
                                load(before[0] + 2)
                    before = now
            down(*before)

        if start < 2 <= upto:
            with phase() as ctx:
                XT = sb(ctx, [128, 2, N])
                banks = Ring(range(4))
                with ExitStack() as c:
                    XN = sb(c, [P, T, D])
                    marks = layernorm(c, X, XN)
                    transposed(XN, XT, marks, Ring(range(8)))
                    p.ve(lambda e: e.tensor_tensor(X[:, :, :], X[:, :, :], XN[:, :, :], ALU.add), marks[-1])
                    p.flush()
                none = [()] * 7
                Cw, cm = routing(ctx, XT, none, a["L0_ffn_router_wT"], None, "probs", banks)
                experts(ctx, XT, none, Cw, cm, a["L0_ffn_w1"], a["L0_ffn_b1"], a["L0_ffn_w2"],
                        a["L0_ffn_b2"], 256, None, banks, Ring(range(4, 8)), None)

        if start < 3 <= upto:
            with phase() as ctx:
                H1 = sb(ctx, [P, T, D])
                with ExitStack() as c0:
                    HA = sb(c0, [P, T, 4, 65])
                    SD = sb(c0, [P, T, 8])
                    with ExitStack() as c:
                        XN = sb(c, [P, T, D])
                        XT = sb(c, [128, 2, N])
                        marks = layernorm(c, X, XN)
                        banks = Ring(range(8))
                        xm = transposed(XN, XT, marks, banks)
                        gat(xm, banks, c, XT, a["L1_gnn_W1T"], a["L1_gnn_W1"], a["L1_gnn_AB1"], 4, 64, HA, SD)
                        p.flush()
                    rec = sb(c0, [P, 7, 1])

                    def finish(h, t0, k, s, mark):
                        x = H1[:, t0:t0 + k, 64 * h:64 * h + 64]
                        r, m = reciprocals(rec, k, s, 64, mark)
                        end = m = p.ve(lambda e: e.tensor_tensor(x, s[:, :, 0:64], r, ALU.mult), m)
                        yield
                        p.ve(lambda e: e.tensor_scalar(x, x, 0.0, None, ALU.max), m)
                        return end

                    attention(c0, 4, 64, HA, SD, False, finish)
                    p.flush()
                with ExitStack() as c0:
                    HB = sb(c0, [P, T, 1, 257])
                    SD = sb(c0, [P, T, 2])
                    with ExitStack() as c:
                        XT = sb(c, [128, 2, N])
                        banks = Ring(range(8))
                        xm = transposed(H1, XT, [None] * T, banks)
                        gat(xm, banks, c, XT, a["L1_gnn_W2T"], a["L1_gnn_W2"], a["L1_gnn_AB2"], 1, 256, HB, SD)
                        p.flush()
                    rec = sb(c0, [P, 1, 1])
                    o = sb(c0, [P, 1, 256])

                    def finish2(h, t0, k, s, mark):
                        r, m = reciprocals(rec, 1, s, 256, mark)
                        end = m = p.ve(lambda e: e.tensor_tensor(o[:, :, :], s[:, :, 0:256], r, ALU.mult), m)
                        x = X[:, t0:t0 + 1, :]
                        p.ve(lambda e: e.tensor_tensor(x, x, o[:, :, :], ALU.add), m)
                        return [end]
                        yield

                    attention(c0, 1, 256, HB, SD, False, finish2)
                    p.flush()

        if start < 4 <= upto:
            L, NC = 25, 125
            with ExitStack() as ctx:
                XG = sb(ctx, [128, L, 6, NC])
                HS = sb(ctx, [128, L, 2, NC])
                V = sb(ctx, [128, 2, 6, 128])
                with ExitStack() as c:
                    XT = sb(c, [128, 2, N])
                    U = sb(c, [128, 2, 6, 128])
                    bg = sb(c, [128, 6])
                    XN = sb(c, [P, T, D])
                    for n, g in enumerate("ioc"):
                        lu = p.dma(1 + n, lambda e, n=n, g=g: e.dma_start(
                            U[:, :, 2 * n:2 * n + 2, :],
                            a[f"L1_ffn_U_{g}"].rearrange("(k p) (m n) -> p k m n", p=128, m=2)))
                        lv = p.dma(4 + n, lambda e, n=n, g=g: e.dma_start(
                            V[:, :, 2 * n:2 * n + 2, :],
                            a[f"L1_ffn_V_{g}"].rearrange("(k p) (m n) -> p k m n", p=128, m=2)))
                        lb = p.dma(7 + n, lambda e, n=n, g=g: e.dma_start(
                            bg[:, 2 * n:2 * n + 2], a[f"L1_ffn_b_{g}"]))
                        p.hold("sync", lu, lv, lb)
                    marks = layernorm(c, X, XN)
                    p.flush()
                    banks = Ring(range(8))
                    xm = transposed(XN, XT, marks, banks)
                    for g in range(7):
                        n = min(500, N - 500 * g)
                        for m6 in range(6):
                            b, free, i = banks.take()

                            def go(e, b=b, m6=m6, g=g, n=n):
                                for k in range(2):
                                    r = e.matmul(bank(b, n), U[:, k, m6, :], XT[:, k, 500 * g:500 * g + n],
                                                 start=k == 0, stop=k == 1)
                                return r

                            m = p.pe(go, free, *xm[g])
                            c0, c1 = 20 * g, 20 * g + n // L
                            m = p.se(lambda e, b=b, m6=m6, c0=c0, c1=c1, n=n: e.activation(
                                XG[:, :, m6, c0:c1].rearrange("p s c -> p c s"),
                                bank(b, n).rearrange("p (c s) -> p c s", s=L), ACT.Identity,
                                bias=bg[:, m6:m6 + 1]), m)
                            banks.give(i, m)
                    p.flush()
                H0, C0 = sb(ctx, [128, 2, NC]), sb(ctx, [128, 2, NC])
                Cs = sb(ctx, [128, 2, NC])
                Gt = sb(ctx, [128, 6, NC])
                t1, t2, t3 = sb(ctx, [128, 2, NC]), sb(ctx, [128, 2, NC]), sb(ctx, [128, 2, NC])
                df = sb(ctx, [128, 4])
                ft = sb(ctx, [1, 2])
                go_on = sb(ctx, [1, 1], i32)
                for t in (H0, C0):
                    p.ge(lambda e, t=t: e.memset(t[:, :, :], 0.0))
                p.ge(lambda e: e.memset(go_on[:, :], 1))
                p.flush()
                with nc.Fori(0, NC // 25):
                    more = nc.values_load(go_on[0:1, 0:1], min_val=0, max_val=1)
                    nc.all_engine_barrier(sem_only=True)
                    with nc.If(more == 1):
                        with nc.Fori(0, 25):
                            flag = nc.values_load(go_on[0:1, 0:1], min_val=0, max_val=1)
                            nc.all_engine_barrier(sem_only=True)
                            with nc.If(flag == 1):
                                q.rewind()
                                hm = cm = q.ve(lambda e: e.tensor_copy(Cs[:, :, :], C0[:, :, :]))
                                gates = ((4, 0), (0, 1), (2, 2))
                                used = [[None] * 3, [None] * 3]

                                def inputs_of(s):
                                    for g6, b in gates:
                                        def go(e, b=3 * (s % 2) + b, g6=g6):
                                            return e.matmul(
                                                PS[:, b, 0:2 * NC], ident[:, :],
                                                XG[:, s, g6:g6 + 2, :].rearrange("p g c -> p (g c)"),
                                                start=True, stop=False, skip_group_check=True)
                                        q.pe(go, used[s % 2][b])

                                inputs_of(0)
                                for s in range(L):
                                    hprev = H0[:, :, :] if s == 0 else HS[:, s - 1, :, :]
                                    acts = []
                                    for g6, b in gates:
                                        def go(e, b=3 * (s % 2) + b, g6=g6, hprev=hprev):
                                            for n in range(2):
                                                for k in range(2):
                                                    r = e.matmul(PS[:, b, n * NC:n * NC + NC], V[:, k, g6 + n, :],
                                                                 hprev[:, k, :], start=False, stop=k == 1,
                                                                 skip_group_check=True)
                                            return r
                                        m = q.pe(go, hm)
                                        acts.append((m, g6, b))
                                    if s + 1 < L:
                                        inputs_of(s + 1)
                                    m1 = q.ve(lambda e, hprev=hprev: e.tensor_tensor(
                                        t1[:, :, :], hprev, Cs[:, :, :], ALU.mult), hm, cm)
                                    am = []
                                    for m, g6, b in acts:
                                        am.append(q.se(lambda e, g6=g6, b=3 * (s % 2) + b: e.activation(
                                            Gt[:, g6:g6 + 2, :],
                                            PS[:, b, 0:2 * NC].rearrange("p (g c) -> p g c", c=NC),
                                            ACT.Tanh if g6 == 4 else ACT.Sigmoid), m, hm))
                                        used[s % 2][b] = am[-1]
                                    m2 = q.ve(lambda e: e.tensor_tensor(t2[:, :, :], Gt[:, 0:2, :], Gt[:, 4:6, :],
                                                                        ALU.mult), am[1])
                                    cm = q.ve(lambda e: e.tensor_tensor(Cs[:, :, :], t1[:, :, :], t2[:, :, :],
                                                                        ALU.add), m1, m2)
                                    m = q.se(lambda e: e.activation(t3[:, :, :], Cs[:, :, :], ACT.Tanh), cm)
                                    hm = q.ve(lambda e, s=s: e.tensor_tensor(HS[:, s, :, :], Gt[:, 2:4, :],
                                                                             t3[:, :, :], ALU.mult), m)
                                nb = NC - 1
                                new_h, new_c = HS[:, L - 1, :, 0:nb], Cs[:, :, 0:nb]
                                m = q.ve(lambda e: e.tensor_tensor(t1[:, :, 0:nb], new_h, H0[:, :, 1:NC],
                                                                   ALU.subtract), hm)
                                m = q.ve(lambda e: e.tensor_reduce(df[:, 0:1], t1[:, :, 0:nb], AX.XY, ALU.max,
                                                                   apply_absolute_value=True), m)
                                m2 = q.ve(lambda e: e.tensor_tensor(t2[:, :, 0:nb], new_c, C0[:, :, 1:NC],
                                                                    ALU.subtract), m)
                                m2 = q.ve(lambda e: e.tensor_reduce(df[:, 1:2], t2[:, :, 0:nb], AX.XY, ALU.max,
                                                                    apply_absolute_value=True), m2)
                                q.ve(lambda e: e.tensor_copy(H0[:, :, 1:NC], new_h), m)
                                q.ve(lambda e: e.tensor_copy(C0[:, :, 1:NC], new_c), m2)
                                m = q.ve(lambda e: e.tensor_tensor(df[:, 2:3], df[:, 0:1], df[:, 1:2], ALU.max), m2)
                                m = q.pe(lambda e: e.transpose(PS[0:1, 7, 0:128], df[:, 2:3], ident[:, :]), m)
                                m = q.ve(lambda e: e.tensor_reduce(ft[:, 0:1], PS[0:1, 7, 0:128], AX.X, ALU.max), m)
                                m = q.ve(lambda e: e.tensor_scalar(go_on[:, :], ft[:, 0:1], TOL, None, ALU.is_gt), m)
                                q.hold("vector", m)
                                q.flush()
                                nc.multi_engine_barrier(list(mybir.ALL_ENGINES), sems_to_clear=q.numbers())
                inorder = Ring([sb(ctx, [128, 2, 2, 5, L]) for _ in range(3)])
                banks = Ring(range(8))
                for t0 in range(0, T, 2):
                    ts = range(t0, min(t0 + 2, T))
                    b, free, i = banks.take()
                    row, rfree, ri = inorder.take()
                    for n, t in enumerate(ts):
                        for k in range(2):
                            mc = p.se(lambda e, n=n, t=t, k=k, row=row: e.activation(
                                row[:, n, k, :, :].rearrange("p c s -> p s c"),
                                HS[:, :, k, 5 * t:5 * t + 5], ACT.Copy), rfree)

                    def go(e, ts=ts, b=b, row=row):
                        for n, t in enumerate(ts):
                            for k in range(2):
                                r = e.transpose(PS[0:P, b, n * D + 128 * k:n * D + 128 * k + 128],
                                                row[:, n, k, :, :].rearrange("p c s -> p (c s)"),
                                                ident[:, :])
                        return r

                    m = p.pe(go, free, mc)
                    inorder.give(ri, m)
                    xs = X[:, ts[0]:ts[-1] + 1, :].rearrange("p t d -> p (t d)")
                    banks.give(i, p.ve(lambda e, b=b, xs=xs, n=len(ts) * D: e.tensor_tensor(
                        xs, xs, bank(b, n, P), ALU.add), m))
                p.flush()

        def convolution(ctx, banks, XT, xm, W, dis, HS, finish):
            w = sb(ctx, [128, 2, D])
            l1 = p.dma(1, lambda e: e.dma_start(w[:, :, :], W.rearrange("(k p) n -> p k n", p=128)))

            def sink(b, ts, m):
                k = len(ts)
                return p.ve(lambda e: e.tensor_tensor(
                    HS[:, ts[0]:ts[0] + k, :], bank(b, k * D, P).rearrange("p (t d) -> p t d", d=D),
                    dis[:, ts[0]:ts[0] + k].unsqueeze(2).broadcast_to([P, k, D]), ALU.mult), m)

            rows_gemm(XT, w, xm, banks, sink, l1)
            p.flush()
            half = 13
            ads = Ring([sb(ctx, [P, half * P]) for _ in range(4)])
            free_b = None
            for tiles in (range(0, half), range(half, T)):
                lo, n = tiles[0] * P, len(tiles) * P
                for j in range(T):
                    ad, free, i = ads.take()
                    ld = p.dma(2 + i, lambda e, ad=ad, j=j, lo=lo, n=n: e.dma_start(
                        ad[:, 0:n], adj[j][:, lo:lo + n]), free)

                    def go(e, ad=ad, j=j, tiles=tiles):
                        for n, t in enumerate(tiles):
                            r = e.matmul(PS[0:P, n // 2, (n % 2) * D:(n % 2) * D + D],
                                         ad[:, n * P:n * P + P], HS[:, j, :],
                                         start=(j == 0 and n % 2 == 0), stop=j == T - 1,
                                         skip_group_check=True)
                        return r

                    m = p.pe(go, ld, free_b if j == 0 else None)
                    ads.give(i, m)
                for n in range(0, len(tiles), 2):
                    ts = tiles[n:n + 2]
                    free_b = finish(ts, PS[0:P, n // 2, 0:len(ts) * D].rearrange("p (t d) -> p t d", d=D), m)

        if start < 5 <= upto:
            with phase() as ctx:
                Y = sb(ctx, [P, T, D])
                XT = sb(ctx, [128, 2, N])
                HS = sb(ctx, [P, T, D])
                with ExitStack() as c:
                    marks = layernorm(c, X, Y)
                    p.flush()
                for layer in (1, 2, 3):
                    with ExitStack() as c:
                        bias = sb(c, [P, D])
                        bl = p.dma(10, lambda e, bias=bias, layer=layer: e.dma_start(
                            bias[:, :], broadcast_row(a[f"L2_gnn_b{layer}"], P)))
                        banks = Ring(range(8))
                        xm = transposed(Y, XT, [None] * T, banks)

                        def finish(ts, s, m, layer=layer, bias=bias, bl=bl):
                            k = len(ts)
                            y, hs = Y[:, ts[0]:ts[0] + k, :], HS[:, ts[0]:ts[0] + k, :]
                            dd = dis0[:, ts[0]:ts[0] + k].unsqueeze(2).broadcast_to([P, k, D])
                            bb = bias[:, :].unsqueeze(1).broadcast_to([P, k, D])
                            m = end = p.ve(lambda e: e.tensor_tensor(y, s, hs, ALU.add), m)
                            m = p.ve(lambda e: e.tensor_tensor(y, y, dd, ALU.mult), m)
                            m = p.ve(lambda e: e.tensor_tensor(y, y, bb, ALU.add), m, bl)
                            if layer < 3:
                                p.ve(lambda e: e.tensor_scalar(y, y, 0.0, None, ALU.max), m)
                            else:
                                x = X[:, ts[0]:ts[0] + k, :]
                                p.ve(lambda e: e.tensor_tensor(x, x, y, ALU.add), m)
                            return end

                        convolution(c, banks, XT, xm, a[f"L2_gnn_W{layer}"], dis0, HS, finish)
                        p.flush()

        if start < 6 <= upto:
            with phase() as ctx:
                banks = Ring(range(4))
                XT = sb(ctx, [128, 2, N])
                Cw = sb(ctx, [P, T, 8])
                none = [()] * 7
                with ExitStack() as c0:
                    XN = sb(c0, [P, T, D])
                    with ExitStack() as c:
                        marks = layernorm(c, X, XN)
                        xm = transposed(XN, XT, marks, Ring(range(8)))
                        p.flush()
                    Cw_, cm = routing(c0, XT, none, a["L2_ffn_Wr"], a["L2_ffn_br"], "plain", banks)
                    p.flush()
                    p.ve(lambda e: e.tensor_copy(Cw[:, :, :], Cw_[:, :, :]))
                    marks = layernorm(c0, XN, XN)
                    transposed(XN, XT, marks, Ring(range(8)))
                    p.flush()
                experts(ctx, XT, none, Cw, None, a["L2_ffn_W1"], a["L2_ffn_b1"], a["L2_ffn_W2"],
                        a["L2_ffn_b2"], 1024, (a["L2_ffn_ln_g"], a["L2_ffn_ln_b"]), banks,
                        Ring(range(4, 8)), None)

        if start < 7 <= upto:
            with phase() as ctx:
                Y = sb(ctx, [P, T, D])
                XT = sb(ctx, [128, 2, N])
                HS = sb(ctx, [P, T, D])
                outs = Ring([sb(ctx, [P, 2, D]) for _ in range(2)])
                marks = layernorm(ctx, X, Y)
                banks = Ring(range(8))
                xm = transposed(Y, XT, marks, banks)

                def finish3(ts, s, m):
                    k = len(ts)
                    dd = dis1[:, ts[0]:ts[0] + k].unsqueeze(2).broadcast_to([P, k, D])
                    x = X[:, ts[0]:ts[0] + k, :]
                    o, free, i = outs.take()
                    m = end = p.ve(lambda e: e.tensor_tensor(o[:, 0:k, :], s, dd, ALU.mult), m, free)
                    outs.give(i, p.ve(lambda e: e.tensor_tensor(x, x, o[:, 0:k, :], ALU.add), m))
                    return end

                convolution(ctx, banks, XT, xm, a["L3_gnn_W"], dis1, HS, finish3)

        if start < 8 <= upto:
            with phase() as ctx:
                XT = sb(ctx, [128, 2, N])
                banks = Ring(range(4))
                with ExitStack() as c:
                    XN = sb(c, [P, T, D])
                    marks = layernorm(c, X, XN)
                    transposed(XN, XT, marks, Ring(range(8)))
                    p.flush()
                none = [()] * 7
                Cw, cm = routing(ctx, XT, none, a["L3_ffn_Wg"], a["L3_ffn_bg"], None, banks)
                experts(ctx, XT, none, Cw, cm, a["L3_ffn_W1"], a["L3_ffn_b1"], a["L3_ffn_W2"],
                        a["L3_ffn_b2"], 512, None, banks, Ring(range(4, 8)), None)

        p.hold("sync", p.dma(0, lambda e: e.dma_start(a["out"].rearrange("(t p) d -> p t d", p=P), X[:, :, :])))
        p.flush()


def laid_out(inputs):
    import numpy as np

    x = {k: np.ascontiguousarray(v) for k, v in inputs.items()}
    out = {k: x[k] for k in (
        "x", "src", "dst", "L0_gnn_W", "L0_gnn_bias", "L0_ffn_w1", "L0_ffn_w2", "L0_ffn_b2",
        "L1_gnn_W1", "L1_gnn_W2", "L2_gnn_W1", "L2_gnn_b1", "L2_gnn_W2", "L2_gnn_b2", "L2_gnn_W3",
        "L2_gnn_b3", "L2_ffn_Wr", "L2_ffn_br", "L2_ffn_W1", "L2_ffn_W2", "L2_ffn_b2", "L3_gnn_W",
        "L3_ffn_Wg", "L3_ffn_bg", "L3_ffn_W1", "L3_ffn_W2", "L3_ffn_b2")}
    for k in ("i", "o", "c"):
        out[f"L1_ffn_U_{k}"] = x[f"L1_ffn_U_{k}"]
        out[f"L1_ffn_V_{k}"] = x[f"L1_ffn_V_{k}"]
        out[f"L1_ffn_b_{k}"] = np.ascontiguousarray(x[f"L1_ffn_b_{k}"].reshape(2, 128).T)
    for name, key in (("L0_gnn_WT", "L0_gnn_W"), ("L1_gnn_W1T", "L1_gnn_W1"), ("L1_gnn_W2T", "L1_gnn_W2"),
                      ("L0_ffn_router_wT", "L0_ffn_router_w")):
        out[name] = np.ascontiguousarray(x[key].T)
    for name, s, d in (("L0_gnn_AB", "L0_gnn_att_src", "L0_gnn_att_dst"),
                       ("L1_gnn_AB1", "L1_gnn_a1_src", "L1_gnn_a1_dst"),
                       ("L1_gnn_AB2", "L1_gnn_a2_src", "L1_gnn_a2_dst")):
        h, c = x[s].shape
        block = np.zeros((256, 2 * h), x[s].dtype)
        for i in range(h):
            block[i * c:(i + 1) * c, i] = x[s][i]
            block[i * c:(i + 1) * c, h + i] = x[d][i]
        out[name] = block
    for key in ("L0_ffn_b1", "L2_ffn_b1", "L3_ffn_b1"):
        e, h = x[key].shape
        out[key] = np.ascontiguousarray(x[key].reshape(e, h // 128, 128).transpose(0, 2, 1))
    for key in ("L2_ffn_ln_g", "L2_ffn_ln_b"):
        out[key] = np.ascontiguousarray(x[key].reshape(8, 2, 128).transpose(1, 2, 0))
    return out


def kernel(**inputs):
    import concourse.bacc as _bacc
    from concourse import mybir as _mybir
    from concourse.bass_utils import run_bass_kernel_spmd as _run

    nc = _bacc.Bacc("TRN2", target_bir_lowering=False, num_devices=1)
    arrays, args = {}, {}
    for name, v in laid_out(inputs).items():
        arrays[f"in_{name}"] = v
        args[name] = nc.dram_tensor(f"in_{name}", v.shape, _mybir.dt.from_np(v.dtype), kind="ExternalInput").ap()
    args["out"] = nc.dram_tensor("out_0", (3125, 256), _mybir.dt.float32, kind="ExternalOutput").ap()
    program(nc, args)
    r = _run(nc, [arrays], core_ids=[0])
    return r.results[0]["out_0"]
```

```python
import concourse.bass as bass
from concourse import mybir
from contextlib import ExitStack, contextmanager

N, E, D = 3125, 50000, 256
P, T = 125, 25
NN = N * N
HUGE = 1.0e30
CAP = 3.0e38
TOL = 2.0 ** -18
EPS = 1e-5
W, FOLD, ROWE = 17, 782, 3070
SLOTS = 57


class Unit:

    def __init__(self, sem):
        self.sem, self.count, self.queue = sem, 0, []


class Program:

    NAMES = ("tensor", "vector", "scalar", "gpsimd", "sync")

    def __init__(self, nc, tag, lanes):
        self.nc = nc
        self.units = {n: Unit(nc.alloc_semaphore(f"{tag}_{n}")) for n in self.NAMES}
        self.lanes = [[nc.alloc_semaphore(f"{tag}_dma{i}"), 0] for i in range(lanes)]

    def add(self, name, fn, waits):
        u = self.units[name]
        u.count += 1
        u.queue.append((fn, [w for w in waits if w is not None], u.sem, 1))
        return (u.sem, u.count)

    def pe(self, fn, *waits):
        return self.add("tensor", fn, waits)

    def ve(self, fn, *waits):
        return self.add("vector", fn, waits)

    def se(self, fn, *waits):
        return self.add("scalar", fn, waits)

    def ge(self, fn, *waits):
        return self.add("gpsimd", fn, waits)

    def dma(self, lane, fn, *waits, by="sync"):
        at = self.lanes[lane]
        at[1] += 16
        self.units[by].queue.append((fn, [w for w in waits if w is not None], at[0], 16))
        return (at[0], at[1])

    def hold(self, name, *waits):
        self.units[name].queue.append((None, [w for w in waits if w is not None], None, 0))

    def flush(self):
        nc = self.nc
        with nc.Block() as block:
            for name in self.NAMES:
                queue, self.units[name].queue = self.units[name].queue, []

                def body(e, queue=queue):
                    passed = {}
                    if not queue:
                        e.nop()
                    for fn, waits, sem, by in queue:
                        for s, v in waits:
                            if passed.get(s.num, 0) < v:
                                e.wait_ge(s, v)
                                passed[s.num] = v
                        if fn is not None:
                            fn(e).then_inc(sem, by)

                block_of(block, name)(body)

    def numbers(self):
        nums = [u.sem.num for u in self.units.values()] + [s.num for s, _ in self.lanes]
        assert max(nums) - min(nums) + 1 == len(nums)
        return range(min(nums), max(nums) + 1)

    def rewind(self):
        for u in self.units.values():
            u.count = 0
        for lane in self.lanes:
            lane[1] = 0


def block_of(block, name):
    return {"tensor": block.tensor, "vector": block.vector, "scalar": block.scalar,
            "gpsimd": block.gpsimd, "sync": block.sync}[name]


class Ring:

    def __init__(self, items):
        self.items, self.free, self.at = list(items), [None] * len(items), -1

    def take(self):
        self.at = (self.at + 1) % len(self.items)
        return self.items[self.at], self.free[self.at], self.at

    def give(self, i, mark):
        self.free[i] = mark


def program(nc, a):
    f32, bf16, i32, f16 = mybir.dt.float32, mybir.dt.bfloat16, mybir.dt.int32, mybir.dt.float16
    ALU = mybir.AluOpType
    ACT = mybir.ActivationFunctionType
    AX = mybir.AxisListType
    p = Program(nc, "m", 31)
    q = Program(nc, "r", 1)
    fb = Program(nc, "f", 20)
    sp = Program(nc, "s", 31)
    top = ExitStack()
    names = [0]

    def sb(ctx, shape, dt=f32):
        names[0] += 1
        return ctx.enter_context(nc.sbuf_tensor(f"sb{names[0]}", shape, dt))

    @contextmanager
    def phase():
        with ExitStack() as ctx:
            yield ctx
            p.flush()

    A1 = nc.dram_tensor("adj", (NN + 128, 1), f32).ap()
    NEG = nc.dram_tensor("neg", (T, P, N), bf16).ap()
    ROWS = [nc.dram_tensor(f"rows{i}", (T * 4, P), f32).ap() for i in range(3)]
    HR = nc.dram_tensor("features", (N, 264), f32).ap()
    LIN = [nc.dram_tensor(f"edge_terms{i}", (128, W * 5), f32).ap() for i in range(2)]
    LISTS = [nc.dram_tensor(f"edge_lists{i}", (2 * W, 640), f32).ap() for i in range(2)]
    XS = nc.dram_tensor("slot_x", (SLOTS * P, D), f32).ap()
    YS = nc.dram_tensor("slot_y", (SLOTS * P, D), f32).ap()
    EP = nc.dram_tensor("table", (ROWE, W * 4), f32).ap()
    KD = nc.dram_tensor("keys", (P, 400), f32).ap()
    ADJ16 = nc.dram_tensor("adj16", (T, P, N), f16).ap()
    adj = A1[0:NN, :].rearrange("(t p i) o -> t p (i o)", p=P, i=N)

    with top:
        PS = top.enter_context(nc.psum_tensor("ps", [128, 8, 512], f32))
        X = sb(top, [P, T, D])
        ident = sb(top, [128, 128])
        ones = sb(top, [128, 128])
        epsc = sb(top, [128, 1])
        zeros = sb(top, [P, D])
        deg = sb(top, [P, T])
        dis0 = sb(top, [P, T])
        dis1 = sb(top, [P, T])

        def bank(i, n=512, rows=128):
            return PS[0:rows, i, 0:n]

        def use(prog):
            nonlocal p
            p = prog

        def layernorm(ctx, src, dst, *waits):
            st = sb(ctx, [P, T, 6])
            mv = sb(ctx, [P, T, 2])
            rs = sb(ctx, [P, T, 2])
            for t in range(T):
                m = p.ve(lambda e, t=t: e.bn_stats(st[:, t, :], src[:, t, :]), *waits)
            for t in range(T):
                m = p.ve(lambda e, t=t: e.bn_aggr(mv[:, t, :], st[:, t, :]), m)
            m = p.se(lambda e: e.activation(rs[:, :, 0], mv[:, :, 1], ACT.Sqrt, bias=epsc[0:P, :]), m)
            m = p.ve(lambda e: e.reciprocal(rs[:, :, 1], rs[:, :, 0]), m)
            marks = []
            for t in range(T):
                marks.append(p.ve(lambda e, t=t: e.tensor_scalar(
                    dst[:, t, :], src[:, t, :], mv[:, t, 0:1], rs[:, t, 1:2], ALU.subtract, ALU.mult), m))
            return marks

        turn = [0]

        def evacuate(out, src, *marks):
            turn[0] += 1
            if turn[0] % 2:
                return p.se(lambda e: e.activation(out, src, ACT.Copy), *marks)
            return p.ve(lambda e: e.tensor_copy(out, src), *marks)

        def transposed(src, dst, marks, banks):
            out = []
            for g in range(7):
                ts = range(4 * g, min(4 * g + 4, T))
                both = []
                for h in range(2):
                    b, free, i = banks.take()

                    def go(e, ts=ts, h=h, b=b):
                        for n, t in enumerate(ts):
                            r = e.transpose(PS[:, b, n * P:n * P + P],
                                            src[:, t, h * 128:h * 128 + 128], ident[0:P, 0:P])
                        return r

                    m = p.pe(go, free, marks[ts[-1]])
                    n = len(ts) * P
                    m = evacuate(dst[:, h, 500 * g:500 * g + n], bank(b, n), m)
                    banks.give(i, m)
                    both.append(m)
                out.append(both)
            return out

        def rows_gemm(XT, W, marks, banks, sink, *waits):
            for t0 in range(0, T, 2):
                ts = range(t0, min(t0 + 2, T))
                b, free, i = banks.take()

                def go(e, ts=ts, b=b):
                    for n, t in enumerate(ts):
                        for k in range(2):
                            r = e.matmul(PS[0:P, b, n * D:n * D + D], XT[:, k, t * P:t * P + P],
                                         W[:, k, :], start=k == 0, stop=k == 1)
                    return r

                m = p.pe(go, free, *marks[ts[-1] // 4], *marks[ts[0] // 4], *waits)
                banks.give(i, sink(b, ts, m))

        def small_gemm(XT, W, n, marks, b, free, *waits):
            def go(e):
                for t in range(T):
                    for k in range(2):
                        r = e.matmul(PS[0:P, b, t * n:t * n + n], XT[:, k, t * P:t * P + P],
                                     W[:, k, :], start=k == 0, stop=k == 1)
                return r
            return p.pe(go, free, *[m for ms in marks for m in ms], *waits)

        def broadcast_row(ap, parts):
            return ap.unsqueeze(0).broadcast_to([parts, ap.shape[0]])

        with phase() as ctx:
            z = p.ge(lambda e: e.memset(ident[:, :], 0.0))
            p.ge(lambda e: e.affine_select(out=ident[:, :], in_=ident[:, :], compare_op=ALU.not_equal,
                                           fill=1.0, base=0, pattern=[[-1, 128]], channel_multiplier=1), z)
            p.ge(lambda e: e.memset(ones[:, :], 1.0))
            p.ge(lambda e: e.memset(epsc[:, :], EPS))
            p.ge(lambda e: e.memset(zeros[:, :], 0.0))

        def edges(ctx):
            C, G = 400, 40
            se_, de = sb(ctx, [P, C], i32), sb(ctx, [P, C], i32)
            key = sb(ctx, [P, C])
            R = sb(ctx, [P, P, G])
            Q = sb(ctx, [P, G, P])
            low = sb(ctx, [P, P])
            cnt = sb(ctx, [P, C])
            dup = sb(ctx, [P, C])
            spare = sb(ctx, [P, 1])
            idx = sb(ctx, [P, C], i32)
            zero = sb(ctx, [P, N])
            z = p.ve(lambda e: e.memset(zero[:, :], 0.0))
            for t in range(T):
                zd = p.dma(3, lambda e, t=t: e.dma_start(adj[t], zero[:, :]), z)
            zd = p.dma(3, lambda e: e.dma_start(A1[NN:NN + 125, :], zero[:, 0:1]), z)
            l1 = p.dma(1, lambda e: e.dma_start(se_[:, :], a["src"].rearrange("(p c) -> p c", p=P)))
            l2 = p.dma(2, lambda e: e.dma_start(de[:, :], a["dst"].rearrange("(p c) -> p c", p=P)))
            m1 = p.ge(lambda e: e.memset(low[:, :], 1.0))
            m1 = p.ge(lambda e: e.affine_select(out=low[:, :], in_=low[:, :], compare_op=ALU.is_gt, fill=0.0,
                                                base=0, pattern=[[-1, P]], channel_multiplier=1), m1)
            m2 = p.ge(lambda e: e.iota(spare[:, :], [[0, 1]], base=NN, channel_multiplier=1,
                                       allow_small_or_imprecise_dtypes=True))
            k0 = p.ve(lambda e: e.scalar_tensor_tensor(key[:, :], se_[:, :], float(N), de[:, :],
                                                       ALU.mult, ALU.add), l1, l2)
            kd = p.dma(4, lambda e: e.dma_start(KD, key[:, :]), k0)
            flat = KD.rearrange("p c -> (p c)").unsqueeze(0).broadcast_to([P, P * C])\
                .rearrange("q (f c) -> q f c", c=C)
            read, done = None, None
            for g in range(C // G):
                s = slice(g * G, g * G + G)
                ld = p.dma(5, lambda e, s=s: e.dma_start(R[:, :, :], flat[:, :, s]), kd, read)
                m = p.ve(lambda e, s=s: e.tensor_tensor(
                    Q[:, :, :], R[:, :, :].rearrange("p f c -> p c f"),
                    key[:, s].unsqueeze(2).broadcast_to([P, G, P]), ALU.is_equal), ld, done)
                read = m
                m = p.ve(lambda e, s=s: e.tensor_reduce(cnt[:, s], Q[:, :, :], AX.X, ALU.add), m)
                m = p.ve(lambda e, s=s: e.tensor_tensor(
                    Q[:, :, :], Q[:, :, :], low[:, :].unsqueeze(1).broadcast_to([P, G, P]), ALU.mult), m, m1)
                m = p.ve(lambda e, s=s: e.tensor_reduce(dup[:, s], Q[:, :, :], AX.X, ALU.max), m)
                done = m
            m = p.ve(lambda e: e.tensor_scalar(zero[:, 0:C], key[:, :], spare[:, 0:1], None, ALU.subtract),
                     m, m2, zd)
            m = p.ve(lambda e: e.tensor_scalar(dup[:, :], dup[:, :], -1.0, 1.0, ALU.mult, ALU.add), m)
            m = p.ve(lambda e: e.tensor_tensor(zero[:, 0:C], zero[:, 0:C], dup[:, :], ALU.mult), m)
            m = p.ve(lambda e: e.tensor_scalar(idx[:, :], zero[:, 0:C], spare[:, 0:1], None, ALU.add), m)
            last = zd
            for c in range(C):
                last = p.dma(-1, lambda e, c=c: e.indirect_dma_start(
                    A1, bass.IndirectOffsetOnAxis(idx[:, c:c + 1], 0), cnt[:, c:c + 1], None,
                    compute_op=ALU.add), m, last, by="gpsimd")
            p.hold("gpsimd", last)

        def masks(ctx):
            tiles = Ring([sb(ctx, [P, T, P]) for _ in range(2)])
            outs = Ring([sb(ctx, [P, N], bf16) for _ in range(2)])
            banks = Ring(range(8))
            cols = A1[0:NN, :].rearrange("(t p i) o -> p t (i o)", p=P, i=N)
            dp = sb(ctx, [P, T, 7])
            z = p.ve(lambda e: e.memset(dp[:, :, :], 0.0))
            for bk in range(T):
                tile, free, i = tiles.take()
                ld = p.dma(1 + i, lambda e, tile=tile, bk=bk: e.dma_start(
                    tile[:, :, :], cols[:, :, bk * P:bk * P + P]), free)
                o, ofree, oi = outs.take()
                for g in range(7):
                    js = range(4 * g, min(4 * g + 4, T))
                    b, bfree, bi = banks.take()

                    def go(e, js=js, b=b, tile=tile):
                        for n, j in enumerate(js):
                            r = e.transpose(PS[0:P, b, n * P:n * P + P], tile[:, j, :], ident[0:P, 0:P])
                        return r

                    n = len(js) * P
                    last = p.pe(go, ld, bfree)
                    m = p.ve(lambda e, b=b, n=n, g=g, bk=bk: e.tensor_reduce(
                        dp[:, bk, g:g + 1], bank(b, n, P), AX.X, ALU.add), last, z)
                    m = p.ve(lambda e, b=b, n=n, g=g, o=o: e.tensor_scalar(
                        o[:, 500 * g:500 * g + n], bank(b, n, P), 0.0, -HUGE, ALU.is_equal, ALU.mult),
                        ofree)
                    banks.give(bi, m)
                tiles.give(i, last)
                outs.give(oi, p.dma(3 + oi, lambda e, o=o, bk=bk: e.dma_start(NEG[bk], o[:, :]), m, by="scalar"))
            p.hold("scalar", *outs.free)
            p.ve(lambda e: e.tensor_reduce(deg[:, :], dp[:, :, :], AX.X, ALU.add), m)

        redo = sb(top, [1, 1], i32)
        at = sb(top, [128, T], i32)
        first = sb(top, [128, T])
        lists = sb(top, [P, T], i32)
        flat = EP.rearrange("r c -> (r c)")
        cols = ADJ16.rearrange("t p i -> p t i")
        with ExitStack() as ctx:
            ioN = sb(ctx, [128, N])
            ioF = sb(ctx, [128, FOLD], f16)
            S = [sb(ctx, [128, FOLD + 2], bf16) for _ in range(8)]
            with ExitStack() as c:
                se_, de = sb(c, [P, 400], i32), sb(c, [P, 400], i32)
                rec = sb(c, [P, 400, 4])
                sf, df_ = sb(c, [P, 400]), sb(c, [P, 400])
                ge_ = [sb(c, [P, 400]) for _ in range(3)]
                below = sb(c, [P, T, 400])
                cnt = sb(c, [P, T])
                af = sb(c, [128, T])
                part = sb(c, [128, 1])
                pad = sb(c, [8, 1095])
                l1 = p.dma(1, lambda e: e.dma_start(se_[:, :], a["src"].rearrange("(p c) -> p c", p=P)))
                l2 = p.dma(2, lambda e: e.dma_start(de[:, :], a["dst"].rearrange("(p c) -> p c", p=P)))
                g0 = p.ge(lambda e: e.iota(ioN[:, :], [[1, N]], base=0, channel_multiplier=0,
                                           allow_small_or_imprecise_dtypes=True))
                g1 = p.ge(lambda e: e.iota(part[:, :], [[0, 1]], base=0, channel_multiplier=1,
                                           allow_small_or_imprecise_dtypes=True))
                m = p.ve(lambda e: e.memset(pad[:, :], -1.0))
                zd = p.dma(3, lambda e: e.dma_start(
                    flat[4 * E:ROWE * W * 4].rearrange("(p c) -> p c", p=8), pad[:, :]), m)
                for t in S:
                    m = p.ve(lambda e, t=t: e.memset(t[:, FOLD:FOLD + 1], 1.0))
                    m = p.ve(lambda e, t=t: e.memset(t[:, FOLD + 1:FOLD + 2], 0.0))
                ms = p.ve(lambda e: e.tensor_copy(sf[:, :], se_[:, :]), l1)
                m0 = p.ve(lambda e: e.tensor_copy(rec[:, :, 3], se_[:, :]), l1)
                md = p.ve(lambda e: e.tensor_copy(df_[:, :], de[:, :]), l2)
                mg = [p.ve(lambda e, k=k: e.tensor_scalar(ge_[k][:, :], sf[:, :], float(FOLD * (k + 1)), None,
                                                          ALU.is_ge), ms) for k in range(3)]
                m = ms
                for k in range(3):
                    m = p.ve(lambda e, k=k: e.scalar_tensor_tensor(
                        sf[:, :], ge_[k][:, :], -float(FOLD), sf[:, :], ALU.mult, ALU.add), m, mg[2])
                w1 = p.ve(lambda e: e.tensor_copy(rec[:, :, 1], sf[:, :]), m)
                m = p.ve(lambda e: e.tensor_scalar(sf[:, :], ge_[0][:, :], 63.0, 1.0, ALU.mult, ALU.add), w1)
                m = p.ve(lambda e: e.scalar_tensor_tensor(sf[:, :], ge_[1][:, :], 4032.0, sf[:, :],
                                                          ALU.mult, ALU.add), m)
                w2 = p.ve(lambda e: e.scalar_tensor_tensor(rec[:, :, 2], ge_[2][:, :], 258048.0, sf[:, :],
                                                           ALU.mult, ALU.add), m)
                w0 = p.ve(lambda e: e.tensor_copy(rec[:, :, 0], df_[:, :]), md)
                wd = p.dma(4, lambda e: e.dma_start(
                    flat[0:4 * E].rearrange("(p c) -> p c", p=P),
                    rec[:, :, :].rearrange("p c k -> p (c k)")), m0, w0, w1, w2)
                m = p.ve(lambda e: e.tensor_tensor(
                    below[:, :, :], df_[:, :].unsqueeze(1).broadcast_to([P, T, 400]),
                    ioN[0:P, 0:T * P].rearrange("p (t i) -> p t i", i=P)[:, :, 0:1].broadcast_to([P, T, 400]),
                    ALU.is_lt), md, g0)
                m = p.ve(lambda e: e.tensor_reduce(cnt[:, :], below[:, :, :], AX.X, ALU.add), m)
                m = p.pe(lambda e: e.matmul(PS[:, 0, 0:T], ones[0:P, :], cnt[:, :], start=True, stop=True), m)
                m = p.ve(lambda e: e.tensor_scalar(af[:, :], PS[:, 0, 0:T], 1.0 / W, -0.55, ALU.mult, ALU.add), m)
                m = p.ve(lambda e: e.tensor_scalar(af[:, :], af[:, :], 0.0, None, ALU.max), m)
                m = p.ve(lambda e: e.tensor_copy(at[:, :], af[:, :]), m)
                m = p.ve(lambda e: e.tensor_copy(af[:, :], at[:, :]), m)
                m = p.ve(lambda e: e.tensor_copy(first[:, :], af[:, :]), m)
                m = p.ve(lambda e: e.tensor_scalar(af[:, :], af[:, :], part[:, 0:1], None, ALU.add), m, g1)
                p.ve(lambda e: e.tensor_copy(at[:, :], af[:, :]), m)
                p.ve(lambda e: e.tensor_copy(ioF[:, :], ioN[:, 0:FOLD]), g0)
                p.hold("sync", zd, wd)
                lx = p.dma(20, lambda e: e.dma_start(X[:, :, :], a["x"].rearrange("(t p) d -> p t d", p=P)))
                lz = p.dma(21, lambda e: e.dma_start(XS.rearrange("(i p) d -> p i d", p=P),
                                                     zeros[:, :].unsqueeze(1).broadcast_to([P, SLOTS, D])))
                p.flush()
            egs = Ring([sb(ctx, [128, W, 4]) for _ in range(3)])
            dts = Ring([sb(ctx, [128, W, P], bf16) for _ in range(2)])
            hots = Ring(S)
            sums = Ring((0, 2))
            vis = Ring([sb(ctx, [P, 2, 392], i32) for _ in range(2)])
            qis = Ring([sb(ctx, [P, FOLD], i32) for _ in range(3)])
            ats = Ring([sb(ctx, [P, 4 * FOLD]) for _ in range(2)])
            outs = Ring([sb(ctx, [P, N], bf16) for _ in range(2)])
            oas = Ring([sb(ctx, [P, T, P], f16) for _ in range(2)])
            banks = Ring(range(4, 8))

            fetched = {}

            def fetch(b):
                eg, free, ei = egs.take()
                ld = p.dma(-1 - ei, lambda e: e.indirect_dma_start(
                    eg[:, :, :].rearrange("p w k -> p (w k)"), None, EP,
                    bass.IndirectOffsetOnAxis(at[:, b:b + 1], 0)), *(free or []), by="gpsimd")
                fetched[b] = eg, ei, ld

            def front(b):
                if b + 1 < T:
                    fetch(b + 1)
                eg, ei, ld = fetched.pop(b)
                dt, free, di = dts.take()
                for w in range(W):
                    md = p.ge(lambda e, w=w: e.tensor_scalar(
                        dt[:, w, :], ioN[:, b * P:b * P + P], eg[:, w, 0:1], None, ALU.is_equal), ld, free)
                bank2, bfree, bi = sums.take()
                for w in range(W):
                    hot, hfree, hi = hots.take()
                    ms = p.ve(lambda e, w=w, hot=hot: e.tensor_scalar(
                        hot[:, 0:FOLD], ioF[:, :], eg[:, w, 1:2], eg[:, w, 2:3], ALU.is_equal, ALU.mult),
                        ld, hfree)

                    def go(e, w=w, hot=hot):
                        for k in range(2):
                            r = e.matmul(PS[0:P, bank2 + k, 0:392], dt[:, w, :], hot[:, 392 * k:392 * k + 392],
                                         start=w == 0, stop=w == W - 1)
                        return r

                    m = p.pe(go, ms, md, *((bfree or []) if w == 0 else []))
                    hots.give(hi, m)
                egs.give(ei, [ms, md])
                dts.give(di, m)
                return b, bank2, bi, m

            def back(b, bank2, bi, mark):
                vi, free, vv = vis.take()
                m1 = p.se(lambda e: e.activation(vi[:, :, :], PS[0:P, bank2:bank2 + 2, 0:392], ACT.Copy),
                          mark, free)
                p.ve(lambda e: e.tensor_copy(deg[:, b:b + 1], vi[:, 1, FOLD - 392:FOLD - 391]), m1)
                sums.give(bi, [m1])
                A, afree, ai = ats.take()
                flat_v = vi[:, :, :].rearrange("p a c -> p (a c)")
                for k in range(4):
                    qi, free, qq = qis.take()
                    m = p.ve(lambda e, k=k, qi=qi: e.tensor_scalar(
                        qi[:, :], flat_v[:, 0:FOLD], 6 * k, 63, ALU.logical_shift_right, ALU.bitwise_and),
                        m1, free)
                    mc = p.se(lambda e, k=k, qi=qi: e.activation(
                        A[:, FOLD * k:FOLD * k + FOLD], qi[:, :], ACT.Copy), m, *(afree or []))
                    qis.give(qq, mc)
                vis.give(vv, m)
                o, free, oi = outs.take()
                mn = p.ve(lambda e: e.tensor_scalar(o[:, :], A[:, 0:N], 0.0, -HUGE, ALU.is_equal, ALU.mult),
                          mc, free)
                outs.give(oi, p.dma(1 + oi, lambda e: e.dma_start(NEG[b], o[:, :]), mn, by="sync"))
                oa, ofree, ii = oas.take()
                for g in range(7):
                    js = range(4 * g, min(4 * g + 4, T))
                    bk, bfree, bki = banks.take()

                    def go(e, js=js, bk=bk):
                        for n, j in enumerate(js):
                            r = e.transpose(PS[0:P, bk, n * P:n * P + P], A[:, j * P:j * P + P],
                                            ident[0:P, 0:P])
                        return r

                    mt = p.pe(go, mc, bfree)
                    m = p.se(lambda e, js=js, bk=bk: e.activation(
                        oa[:, js[0]:js[-1] + 1, :].rearrange("p t i -> p (t i)"),
                        bank(bk, len(js) * P, P), ACT.Copy), mt, ofree)
                    banks.give(bki, m)
                ats.give(ai, [mn, mt])
                oas.give(ii, p.dma(3 + ii, lambda e: e.dma_start(cols[:, :, b * P:b * P + P], oa[:, :, :]), m,
                                   by="sync"))

            before = None
            fetch(0)
            for b in range(T):
                now = front(b)
                if before:
                    back(*before)
                before = now
            back(*before)
            p.hold("sync", *outs.free, *oas.free, lx, lz)
            p.flush()
            rd = sb(ctx, [P, 2])
            rr = sb(ctx, [1, 4])
            m = p.ve(lambda e: e.tensor_reduce(rd[:, 0:1], deg[:, :], AX.X, ALU.add))
            m = p.ve(lambda e: e.tensor_reduce(rd[:, 1:2], deg[:, :], AX.X, ALU.max), m)

            def go(e):
                e.matmul(PS[0:1, 0, 0:2], ones[0:P, 0:1], rd[:, :], start=True, stop=True)
                return e.transpose(PS[0:1, 1, 0:P], rd[:, 1:2], ident[0:P, 0:P])

            m = p.pe(go, m)
            m1 = p.ve(lambda e: e.tensor_scalar(rr[:, 0:1], PS[0:1, 0, 0:1], float(E), None, ALU.not_equal), m)
            m2 = p.ve(lambda e: e.tensor_reduce(rr[:, 1:2], PS[0:1, 1, 0:P], AX.X, ALU.max), m)
            m2 = p.ve(lambda e: e.tensor_scalar(rr[:, 2:3], rr[:, 1:2], 63.0, None, ALU.is_gt), m2)
            p.ve(lambda e: e.tensor_tensor(redo[:, :], rr[:, 0:1], rr[:, 2:3], ALU.max), m1, m2)
            tri = sb(ctx, [P, P])
            run = sb(ctx, [P, T])
            steps = sb(ctx, [P, 2 * W])
            cmp_ = sb(ctx, [P, T, 2 * W])
            t0 = p.ge(lambda e: e.memset(tri[:, :], 1.0))
            t0 = p.ge(lambda e: e.affine_select(out=tri[:, :], in_=tri[:, :], compare_op=ALU.is_gt, fill=0.0,
                                                base=0, pattern=[[1, P]], channel_multiplier=-1), t0)
            t1 = p.ge(lambda e: e.iota(steps[:, :], [[64, 2 * W]], base=64, channel_multiplier=0,
                                       allow_small_or_imprecise_dtypes=True))

            def go(e):
                e.matmul(PS[0:P, 4, 0:T], tri[:, :], deg[:, :], start=True, stop=True)
                return e.matmul(PS[0:P, 5, 0:T], ones[0:P, 0:P], deg[:, :], start=True, stop=True)

            mm = p.pe(go, t0)
            m = p.ve(lambda e: e.memset(run[:, 0:1], 0.0), mm)
            for t in range(T - 1):
                m = p.ve(lambda e, t=t: e.tensor_tensor(run[:, t + 1:t + 2], run[:, t:t + 1],
                                                        PS[0:P, 5, t:t + 1], ALU.add), m)
            m = p.ve(lambda e: e.tensor_tensor(run[:, :], run[:, :], PS[0:P, 4, 0:T], ALU.add), m)
            m = p.ve(lambda e: e.scalar_tensor_tensor(run[:, :], first[0:P, :], -float(W), run[:, :],
                                                      ALU.mult, ALU.add), m)
            m = p.ve(lambda e: e.tensor_tensor(
                cmp_[:, :, :], run[:, :].unsqueeze(2).broadcast_to([P, T, 2 * W]),
                steps[:, :].unsqueeze(1).broadcast_to([P, T, 2 * W]), ALU.is_ge), m, t1)
            m = p.ve(lambda e: e.tensor_reduce(run[:, :], cmp_[:, :, :], AX.X, ALU.add), m)
            m = p.ve(lambda e: e.tensor_scalar(run[:, :], run[:, :], 2.0 * W - 1, None, ALU.min), m)
            p.ve(lambda e: e.tensor_copy(lists[:, :], run[:, :]), m)
            for LI in LISTS:
                p.hold("sync", p.dma(6, lambda e, LI=LI: e.dma_start(
                    LI[2 * W - 1:2 * W, 320:640].rearrange("r (k c) -> (r k) c", k=5), ioN[0:5, 0:64]), t1))
            p.flush()
        flag = nc.values_load(redo[0:1, 0:1], min_val=0, max_val=1)
        nc.all_engine_barrier(sem_only=True)
        with nc.If(flag == 1):
            main = p
            use(fb)
            with phase() as ctx:
                edges(ctx)
            with phase() as ctx:
                masks(ctx)
            use(main)

        with phase() as ctx:
            m = None
            tmp = sb(ctx, [P, T, 3])
            m1 = p.ve(lambda e: e.tensor_scalar(tmp[:, :, 0], deg[:, :], 1.0, None, ALU.add), m)
            m1 = p.se(lambda e: e.activation(tmp[:, :, 0], tmp[:, :, 0], ACT.Sqrt), m1)
            m1 = p.ve(lambda e: e.reciprocal(dis0[:, :], tmp[:, :, 0]), m1)
            m1 = p.ve(lambda e: e.tensor_scalar(tmp[:, :, 1], deg[:, :], 1.0, None, ALU.max), m1)
            m1 = p.se(lambda e: e.activation(tmp[:, :, 1], tmp[:, :, 1], ACT.Sqrt), m1)
            m1 = p.ve(lambda e: e.reciprocal(tmp[:, :, 1], tmp[:, :, 1]), m1)
            m1 = p.ve(lambda e: e.tensor_scalar(tmp[:, :, 2], deg[:, :], 0.0, None, ALU.is_gt), m1)
            p.ve(lambda e: e.tensor_tensor(dis1[:, :], tmp[:, :, 1], tmp[:, :, 2], ALU.mult), m1)

        def to_rows(ctx, cols, n, ROW, bank_i, lane, *waits):
            k = T * n
            tmp = sb(ctx, [k, P])
            flat = cols.rearrange("p t n -> p (t n)")
            m = p.pe(lambda e: e.transpose(PS[0:k, bank_i, 0:P], flat, ident[0:P, 0:P]), *waits)
            m = p.se(lambda e: e.activation(tmp[:, :], PS[0:k, bank_i, 0:P], ACT.Copy), m)
            return p.dma(lane, lambda e: e.dma_start(ROW[0:k, :], tmp[:, :]), m)

        def from_row(row, ROW, n, h, lane, *waits):
            src = ROW[0:T * n, :].rearrange("(t n) i -> n t i", n=n)[h]
            return p.dma(lane, lambda e: e.dma_start(
                row[:, :].rearrange("p (t i) -> p t i", i=P),
                src.unsqueeze(0).broadcast_to([P, T, P])), *waits)

        def attention(ctx, H, C, HA, SD, loops, finish, A=adj, dt=f32):
            M = sb(ctx, [P, T, H])
            c1 = sb(ctx, [P, T, H])
            c2 = sb(ctx, [P, T, H])
            s2 = sb(ctx, [P, T, H])
            s8 = sb(ctx, [P, T, H])
            sc = sb(ctx, [P, T, H])
            with ExitStack() as c:
                SR = [sb(c, [P, N]) for _ in range(H)]
                negs = Ring([sb(c, [P, N], bf16) for _ in range(3)])
                junk = Ring([sb(c, [P, N], bf16) for _ in range(2)])
                notI = sb(c, [P, P])
                ni = p.ve(lambda e: e.tensor_scalar(notI[:, :], ident[0:P, 0:P], -1.0, 1.0, ALU.mult, ALU.add))
                m = p.ve(lambda e: e.tensor_copy(sc[:, :, :], SD[:, :, 0:H]))
                m = to_rows(c, sc[:, :, :], H, ROWS[0], 0, 11, m)
                marks = [from_row(SR[h], ROWS[0], H, h, 12 + h, m) for h in range(H)]
                for b in range(T):
                    neg, free, i = negs.take()
                    ld = p.dma(1 + i, lambda e, neg=neg, b=b: e.dma_start(neg[:, :], NEG[b]), free)
                    if loops:
                        ld = p.ve(lambda e, neg=neg, b=b: e.tensor_tensor(
                            neg[:, b * P:b * P + P], neg[:, b * P:b * P + P], notI[:, :], ALU.mult), ld, ni)
                    for h in range(H):
                        j, jfree, ji = junk.take()
                        m = p.ve(lambda e, j=j, neg=neg, h=h, b=b: e.tensor_tensor_reduce(
                            out=j[:, :], in0=neg[:, :], in1=SR[h][:, :], scale=1.0, scalar=-HUGE,
                            op0=ALU.add, op1=ALU.max, accum_out=M[:, b, h:h + 1]), ld, marks[h], jfree)
                        junk.give(ji, m)
                    negs.give(i, m)
                d = SD[:, :, H:2 * H]
                m = p.ve(lambda e: e.tensor_tensor(c1[:, :, :], M[:, :, :], d, ALU.add), m)
                m = p.ve(lambda e: e.scalar_tensor_tensor(M[:, :, :], c1[:, :, :], 0.2, c1[:, :, :],
                                                          ALU.mult, ALU.max), m)
                m = p.ve(lambda e: e.tensor_scalar(c1[:, :, :], d, 0.8, None, ALU.mult), m)
                m = p.ve(lambda e: e.tensor_scalar(s8[:, :, :], SD[:, :, 0:H], 0.8, None, ALU.mult), m)
                m = p.ve(lambda e: e.scalar_tensor_tensor(c2[:, :, :], d, 0.2, M[:, :, :],
                                                          ALU.mult, ALU.subtract), m)
                p.ve(lambda e: e.tensor_scalar(s2[:, :, :], SD[:, :, 0:H], 0.2, None, ALU.mult), m)
                r1 = to_rows(c, c1[:, :, :], H, ROWS[1], 1, 16, m)
                r2 = to_rows(c, c2[:, :, :], H, ROWS[2], 2, 17, m)
                p.hold("sync", r1, r2)
                p.flush()
            wide = C > 128
            G = min(H, 2)
            R = [[sb(ctx, [P, N]) for _ in range(2)] for _ in range(G)]
            sets = ([range(0, 7), range(7, 13), range(13, 19), range(19, 25)] if wide else
                    [range(0, 9), range(9, 17), range(17, 25)])
            most = len(sets[0])
            work = Ring([sb(ctx, [P, most * P]) for _ in range(9)])
            ads = Ring([sb(ctx, [P, most * P], dt) for _ in range(5 if wide else 4)])
            turned = Ring([sb(ctx, [C + 1, most * P]) for _ in range(G)]) if not wide else None
            spare = Ring((6, 7))
            whole = {}
            last = [[None, None] for _ in range(G)]
            added = [[None, None] for _ in range(G)]
            ended = [None] * G
            pending, later = [], []
            count = [0]

            def closing(g, h, tiles, mark):
                if wide:
                    for n, t in enumerate(tiles):
                        s = PS[0:P, n, 0:C + 1].unsqueeze(1)
                        ends = yield from finish(h, t, 1, s, mark)
                        ended[g] = ends
                    return
                OT, free, oi = turned.take()
                marks = []
                for b, (lo, n) in enumerate(pieces(tiles)):
                    marks.append(evacuate(OT[:, lo:lo + n], PS[0:C + 1, 3 * g + b, 0:n], mark, free))
                ended[g] = marks
                yield
                for t0 in range(0, len(tiles), 5):
                    ts = tiles[t0:t0 + 5]
                    b, bfree, bi = spare.take()

                    def go(e, b=b, t0=t0, k=len(ts)):
                        for n in range(k):
                            r = e.transpose(PS[0:P, b, n * (C + 1):(n + 1) * (C + 1)],
                                            OT[:, (t0 + n) * P:(t0 + n + 1) * P], ident[0:C + 1, 0:C + 1])
                        return r

                    m = p.pe(go, bfree, *marks)
                    turned.give(oi, m)
                    yield
                    s = PS[0:P, b, 0:len(ts) * (C + 1)].rearrange("p (t c) -> p t c", c=C + 1)
                    end = yield from finish(h, ts[0], len(ts), s, m)
                    spare.give(bi, end)
                    yield

            def pieces(tiles):
                k = 3 if len(tiles) == 9 else 4
                return [(t * P, k * P) for t in range(0, len(tiles), k)]

            def advance():
                if later and next(later[0], "end") == "end":
                    later.pop(0)

            def second(u):
                h, g, j, tiles, w, wi, ad, ai, ld, first_mark = u
                n = len(tiles) * P
                if loops and j in tiles and ld not in whole:
                    whole[ld] = p.ve(lambda e, at=(j - tiles[0]) * P: e.tensor_tensor(
                        ad[:, at:at + P], ad[:, at:at + P], ident[0:P, 0:P], ALU.add), ld)
                ld = whole.get(ld, ld)
                mk = p.se(lambda e: e.activation(w[:, 0:n], w[:, 0:n], ACT.Exp, bias=s2[:, j, h:h + 1]),
                          first_mark)
                mk = p.ve(lambda e: e.scalar_tensor_tensor(
                    w[:, 0:n], w[:, 0:n], CAP, ad[:, 0:n], ALU.min, ALU.mult), mk, ld)
                masked.setdefault(ai, []).append(mk)
                if g == G - 1:
                    ads.give(ai, masked.pop(ai))

                def go(e):
                    if wide:
                        for n in range(len(tiles)):
                            r = e.matmul(PS[0:P, n, 0:C + 1], w[:, n * P:n * P + P], HA[:, j, h, :],
                                         start=j == 0, stop=j == T - 1)
                    else:
                        for b, (lo, k) in enumerate(pieces(tiles)):
                            r = e.matmul(PS[0:C + 1, 3 * g + b, 0:k], HA[:, j, h, :], w[:, lo:lo + k],
                                         start=j == 0, stop=j == T - 1)
                    return r

                mk = p.pe(go, mk, *((ended[g] or []) if j == 0 else []))
                work.give(wi, mk)
                if j == T - 1:
                    end = closing(g, h, tiles, mk)
                    next(end, None)
                    later.append(end)
                else:
                    advance()

            masked = {}
            for h0 in range(0, H, G):
                rows = [[from_row(R[g][0], ROWS[1], H, h0 + g, 12 + 2 * g, last[g][0]),
                         from_row(R[g][1], ROWS[2], H, h0 + g, 13 + 2 * g, *added[g])] for g in range(G)]
                for tiles in sets:
                    lo, n = tiles[0] * P, len(tiles) * P
                    for j in range(T):
                        ad, free, ai = ads.take()
                        ld = p.dma(1 + ai, lambda e, ad=ad, j=j, lo=lo, n=n: e.dma_start(
                            ad[:, 0:n], A[j][:, lo:lo + n]), *(free or []))
                        for g in range(G):
                            h = h0 + g
                            w, wfree, wi = work.take()
                            last[g][0] = p.se(lambda e, w=w, j=j, h=h, g=g, lo=lo, n=n: e.activation(
                                w[:, 0:n], R[g][0][:, lo:lo + n], ACT.Relu, bias=s8[:, j, h:h + 1]),
                                rows[g][0], wfree)
                            count[0] += 1
                            adder = p.ge if count[0] % 3 == 0 and not wide else p.ve
                            last[g][1] = adder(
                                lambda e, w=w, g=g, lo=lo, n=n: e.tensor_tensor(
                                    w[:, 0:n], w[:, 0:n], R[g][1][:, lo:lo + n], ALU.add),
                                rows[g][1], last[g][0])
                            added[g][count[0] % 3 == 0] = last[g][1]
                            pending.append((h, g, j, tiles, w, wi, ad, ai, ld, last[g][1]))
                            if len(pending) > 3:
                                second(pending.pop(0))
                    while wide and pending:
                        second(pending.pop(0))
                    while wide and later:
                        advance()
                while pending:
                    second(pending.pop(0))
            while later:
                advance()

        def either(listed, plain):
            main = p
            for value, prog, fn in ((0, sp, listed), (1, fb, plain)):
                flag = nc.values_load(redo[0:1, 0:1], min_val=0, max_val=1)
                nc.all_engine_barrier(sem_only=True)
                with nc.If(flag == value):
                    use(prog)
                    fn()
                    use(main)

        def by_edges(ctx, HA, SD, loops, finish):
            ioP = sb(ctx, [128, P])
            rel = sb(ctx, [128, W, 1])
            g0 = p.ge(lambda e: e.iota(ioP[:, :], [[1, P]], base=0, channel_multiplier=0,
                                       allow_small_or_imprecise_dtypes=True))
            part = sb(ctx, [128, T])
            g1 = p.ge(lambda e: e.iota(part[:, :], [[P, T]], base=0, channel_multiplier=1,
                                       allow_small_or_imprecise_dtypes=True))
            HV = HR.rearrange("(t p) c -> p t c", p=P)
            w1 = p.dma(0, lambda e: e.dma_start(HV[:, :, 0:260], HA[:, :, :, :].rearrange("p t h c -> p t (h c)")))
            w2 = p.dma(1, lambda e: e.dma_start(HV[:, :, 260:264], SD[:, :, 0:4]))
            p.hold("sync", w1, w2)
            p.flush()
            egs = Ring([sb(ctx, [128, W, 4]) for _ in range(4)])
            ids = Ring([sb(ctx, [128, W], i32) for _ in range(3)])
            hgs = Ring([sb(ctx, [128, W, 264]) for _ in range(4)])
            dts = Ring([sb(ctx, [128, W, P]) for _ in range(3)])
            turned = Ring([sb(ctx, [P, W, 128]) for _ in range(2)])
            sls = Ring([sb(ctx, [128, W, 5]) for _ in range(2)])
            lins = Ring([0, 1])
            lls = Ring([sb(ctx, [P, 128, 5]) for _ in range(2)])
            neg = sb(ctx, [P, 128])
            mx = sb(ctx, [P, 4, 128])
            M = sb(ctx, [P, 4])
            DMs = Ring([sb(ctx, [P, 9]) for _ in range(2)])
            selfs = Ring([sb(ctx, [P, 4]) for _ in range(3)])
            lg = sb(ctx, [128, W, 4])
            lg2 = sb(ctx, [128, W, 4])
            spt = Ring((0, 1, 2, 3))
            spe = Ring((4,))
            spo = Ring((6, 7))
            ev, st = {}, {}

            def fetch(b):
                eg, free, ei = egs.take()
                ld = p.dma(-9 - ei, lambda e: e.indirect_dma_start(
                    eg[:, :, :].rearrange("p w k -> p (w k)"), None, EP,
                    bass.IndirectOffsetOnAxis(at[:, b:b + 1], 0)), *(free or []), by="gpsimd")
                st[b] = dict(eg=eg, ei=ei, ld=ld)

            def indices(b):
                u = st[b]
                eg = u["eg"]
                ix, free, ii = ids.take()
                mi = p.ve(lambda e: e.tensor_scalar(ix[:, :], eg[:, :, 3], 0.0, None, ALU.max), u["ld"], free)
                u.update(ix=ix, ii=ii, mi=mi)

            def hot(b):
                u = st[b]
                eg = u["eg"]
                dt, free, di = dts.take()
                md = p.ve(lambda e: e.tensor_scalar(rel[:, :, :], eg[:, :, 0:1], float(b * P), None,
                                                    ALU.subtract), u["ld"])
                md = p.ve(lambda e: e.tensor_tensor(
                    dt[:, :, :], rel[:, :, :].broadcast_to([128, W, P]),
                    ioP[:, :].unsqueeze(1).broadcast_to([128, W, P]), ALU.is_equal), md, free, g0)
                egs.give(u["ei"], [md])
                u.update(dt=dt, di=di, md=md)

            def gather(b):
                u = st[b]
                hg, free, hi = hgs.take()
                for w in range(W):
                    m = p.dma(-3 - hi, lambda e, w=w: e.indirect_dma_start(
                        hg[:, w, :], None, HR, bass.IndirectOffsetOnAxis(u["ix"][:, w:w + 1], 0)),
                        u["mi"], free, by="gpsimd")
                ids.give(u["ii"], m)
                u.update(hg=hg, hi=hi, mg=m)

            def spread(b):
                u = st[b]
                sl, free, si = sls.take()
                m1 = p.ve(lambda e: e.tensor_copy(sl[:, :, 0:4], u["hg"][:, :, 260:264]), u["mg"], free)
                m2 = p.ve(lambda e: e.tensor_copy(sl[:, :, 4:5], u["eg"][:, :, 0:1]), u["ld"], free)
                k, lfree, ki = lins.take()
                lin = LIN[k].rearrange("p c -> (p c)")
                m = p.dma(0, lambda e: e.dma_start(LIN[k], sl[:, :, :].rearrange("p w c -> p (w c)")),
                          m1, m2, lfree)
                sls.give(si, m)
                ma = p.dma(1, lambda e: e.dma_start(LISTS[k][:, 0:320], lin.rearrange("(r c) -> r c", c=320)), m)
                mb = p.dma(2, lambda e: e.dma_start(
                    LISTS[k][0:2 * W - 1, 320:640], lin[320:2 * W * 320].rearrange("(r c) -> r c", c=320)), m)
                u.update(k=k, ki=ki, ma=ma, mb=mb)

            def turn(b):
                u = st[b]
                DT, dfree, dti = turned.take()
                for w0 in range(0, W, 4):
                    n = min(4, W - w0)
                    bk, bfree, bi = spt.take()

                    def go(e, w0=w0, n=n, bk=bk):
                        for x in range(n):
                            r = e.transpose(PS[0:P, bk, x * 128:x * 128 + 128], u["dt"][:, w0 + x, :],
                                            ident[:, :])
                        return r

                    m = p.pe(go, u["md"], bfree)
                    m = p.se(lambda e, w0=w0, n=n, bk=bk: e.activation(
                        DT[:, w0:w0 + n, :].rearrange("p w c -> p (w c)"), bank(bk, n * 128, P), ACT.Copy),
                        m, dfree)
                    spt.give(bi, m)
                u.update(DT=DT, dti=dti, mt=m)

            def listing(b):
                u = st[b]
                ll, free, li = lls.take()
                ml = p.dma(-7 - li, lambda e: e.indirect_dma_start(
                    ll[:, :, :].rearrange("p e c -> p (e c)"), None, LISTS[u["k"]],
                    bass.IndirectOffsetOnAxis(lists[:, b:b + 1], 0)), u["ma"], u["mb"], free, by="gpsimd")
                lins.give(u["ki"], ml)
                u.update(ll=ll, li=li, ml=ml)

            def maxima(b):
                u = st[b]
                ll = u["ll"]
                dm, free, dmi = DMs.take()
                m = p.ve(lambda e: e.tensor_scalar(neg[:, :], ll[:, :, 4], part[0:P, b:b + 1], -HUGE,
                                                   ALU.not_equal, ALU.mult), u["ml"], g1)
                m = p.ve(lambda e: e.tensor_tensor(
                    mx[:, :, :], ll[:, :, 0:4].rearrange("p e h -> p h e"),
                    neg[:, :].unsqueeze(1).broadcast_to([P, 4, 128]), ALU.add), m)
                lls.give(u["li"], m)
                m = p.ve(lambda e: e.tensor_reduce(M[:, :], mx[:, :, :], AX.X, ALU.max), m)
                d, s4 = SD[:, b, 4:8], SD[:, b, 0:4]
                if loops:
                    m = p.ve(lambda e: e.tensor_tensor(M[:, :], M[:, :], s4, ALU.max), m)
                m = p.ve(lambda e: e.tensor_tensor(M[:, :], M[:, :], d, ALU.add), m)
                m = p.ve(lambda e: e.scalar_tensor_tensor(dm[:, 4:8], M[:, :], 0.2, M[:, :], ALU.mult, ALU.max),
                         m, free)
                m2 = p.ve(lambda e: e.tensor_copy(dm[:, 0:4], d), free)
                m3 = p.ve(lambda e: e.memset(dm[:, 8:9], 1.0), free)
                u.update(dm=dm, dmi=dmi, mm=[m, m2, m3])
                if loops:
                    se_, free, sei = selfs.take()
                    m = p.ve(lambda e: e.tensor_tensor(se_[:, :], s4, d, ALU.add), m, free)
                    m = p.ve(lambda e: e.scalar_tensor_tensor(se_[:, :], se_[:, :], 0.2, se_[:, :],
                                                              ALU.mult, ALU.max), m)
                    m = p.ve(lambda e: e.tensor_tensor(se_[:, :], se_[:, :], dm[:, 4:8], ALU.subtract), m)
                    m = p.se(lambda e: e.activation(se_[:, :], se_[:, :], ACT.Exp), m)
                    u.update(se=se_, sei=sei, mse=m)

            def expand(b):
                u = st[b]
                bk, bfree, bi = spe.take()

                def go(e):
                    for w in range(W):
                        r = e.matmul(PS[:, bk, w * 9:w * 9 + 9], u["DT"][:, w, :], u["dm"][:, :],
                                     start=True, stop=True)
                    return r

                m = p.pe(go, u["mt"], bfree, *u["mm"])
                turned.give(u["dti"], m)
                DMs.give(u["dmi"], m)
                u.update(eb=bk, ebi=bi, me=m)

            def weigh(b):
                u = st[b]
                E_ = PS[:, u["eb"], 0:9 * W].rearrange("p (w c) -> p w c", c=9)
                hg = u["hg"]
                m = p.ve(lambda e: e.tensor_tensor(lg[:, :, :], hg[:, :, 260:264], E_[:, :, 0:4], ALU.add),
                         u["me"], last[0])
                m = p.ve(lambda e: e.scalar_tensor_tensor(lg[:, :, :], lg[:, :, :], 0.2, lg[:, :, :],
                                                          ALU.mult, ALU.max), m)
                m = p.ve(lambda e: e.tensor_tensor(lg[:, :, :], lg[:, :, :], E_[:, :, 4:8], ALU.subtract), m)
                m = p.se(lambda e: e.activation(lg2[:, :, :], lg[:, :, :], ACT.Exp), m, last[1])
                m = p.ve(lambda e: e.scalar_tensor_tensor(
                    lg2[:, :, :], lg2[:, :, :], CAP, E_[:, :, 8:9].broadcast_to([128, W, 4]),
                    ALU.min, ALU.mult), m)
                spe.give(u["ebi"], m)
                last[0] = m
                u["scaled"] = []
                for w0 in range(0, W, 6):
                    ms = []
                    for w in range(w0, min(w0 + 6, W)):
                        v = hg[:, w, 0:260].rearrange("p (h c) -> p h c", c=65)
                        ms.append(p.ve(lambda e, w=w, v=v: e.tensor_tensor(
                            v, v, lg2[:, w, :].unsqueeze(2).broadcast_to([128, 4, 65]), ALU.mult), m))
                    u["scaled"].append(ms[-1])
                last[1] = ms[-1]

            last = [None, None]

            def add_up(b):
                u = st[b]
                bk, bfree, bi = spo.take()
                for n, w0 in enumerate(range(0, W, 6)):
                    def go(e, w0=w0):
                        for w in range(w0, min(w0 + 6, W)):
                            r = e.matmul(PS[0:P, bk, 0:260], u["dt"][:, w, :], u["hg"][:, w, 0:260],
                                         start=w == 0, stop=w == W - 1)
                        return r

                    m = p.pe(go, u["scaled"][n], bfree)
                hgs.give(u["hi"], m)
                dts.give(u["di"], m)
                u.update(ob=bk, obi=bi, mo=m)

            acc = sb(ctx, [P, 4, 65])

            def close(b):
                u = st.pop(b)
                s = PS[0:P, u["ob"], 0:260].rearrange("p (h c) -> p h c", c=65)
                if loops:
                    m = p.ve(lambda e: e.tensor_tensor(
                        acc[:, :, :], HA[:, b, :, :], u["se"][:, :].unsqueeze(2).broadcast_to([P, 4, 65]),
                        ALU.mult), u["mse"], u["mo"])
                    selfs.give(u["sei"], m)
                    m = p.ve(lambda e: e.tensor_tensor(acc[:, :, :], acc[:, :, :], s, ALU.add), m)
                else:
                    m = p.ve(lambda e: e.tensor_copy(acc[:, :, :], s), u["mo"])
                spo.give(u["obi"], m)
                finish(b, acc, m)

            fetch(0)
            fetch(1)
            indices(0)
            for i in range(T + 3):
                if i >= 2 and i - 2 < T:
                    maxima(i - 2)
                    expand(i - 2)
                if i + 2 < T:
                    fetch(i + 2)
                if i < T:
                    gather(i)
                if i + 1 < T:
                    indices(i + 1)
                if 1 <= i <= T:
                    spread(i - 1)
                    listing(i - 1)
                    hot(i - 1)
                    turn(i - 1)
                if i >= 3:
                    close(i - 3)
                if i >= 2 and i - 2 < T:
                    weigh(i - 2)
                    add_up(i - 2)

        def gat(XTm, banks, ctx, XT, W, WN, AB, H, C, HA, SD):
            w = sb(ctx, [128, 2, D])
            wn = sb(ctx, [128, 2, D])
            ab = sb(ctx, [128, 2, 2 * H])
            wa = sb(ctx, [128, 2, 2 * H])
            l1 = p.dma(1, lambda e: e.dma_start(w[:, :, :], W.rearrange("(k p) n -> p k n", p=128)))
            l2 = p.dma(2, lambda e: e.dma_start(wn[:, :, :], WN.rearrange("(k p) n -> p k n", p=128)))
            l3 = p.dma(3, lambda e: e.dma_start(ab[:, :, :], AB.rearrange("(k p) n -> p k n", p=128)))
            b, free, i = banks.take()

            def go(e):
                for k in range(2):
                    for c in range(2):
                        r = e.matmul(PS[:, b, 64 * k:64 * k + 2 * H], wn[:, c, k * 128:k * 128 + 128],
                                     ab[:, c, :], start=c == 0, stop=c == 1)
                return r

            m = p.pe(go, l2, l3, free)
            for k in range(2):
                m2 = p.ve(lambda e, k=k: e.tensor_copy(wa[:, k, :], PS[:, b, 64 * k:64 * k + 2 * H]), m)
            banks.give(i, m2)
            b2, free, i = banks.take()
            m = small_gemm(XT, wa, 2 * H, XTm, b2, free, m2)
            m = p.ve(lambda e: e.tensor_copy(SD[:, :, :].rearrange("p t n -> p (t n)"),
                                             bank(b2, T * 2 * H, P)), m)
            banks.give(i, m)
            p.ge(lambda e: e.memset(HA[:, :, :, C:C + 1], 1.0))

            def sink(b, ts, m):
                return evacuate(HA[:, ts[0]:ts[-1] + 1, :, 0:C],
                                bank(b, len(ts) * D, P).rearrange("p (t h c) -> p t h c", h=H, c=C), m)

            rows_gemm(XT, w, XTm, banks, sink, l1)

        def reciprocals(rec, k, s, C, mark):
            m = p.ve(lambda e: e.tensor_scalar(rec[:, 0:k, :], s[:, :, C:C + 1], 1e-16, None, ALU.add), mark)
            m = p.ve(lambda e: e.reciprocal(rec[:, 0:k, :], rec[:, 0:k, :]), m)
            return rec[:, 0:k, :].broadcast_to([P, k, C]), m

        with phase() as ctx:
            HA = sb(ctx, [P, T, 4, 65])
            SD = sb(ctx, [P, T, 8])
            with ExitStack() as c:
                XN = sb(c, [P, T, D])
                XT = sb(c, [128, 2, N])
                marks = layernorm(c, X, XN)
                banks = Ring(range(8))
                xm = transposed(XN, XT, marks, banks)
                gat(xm, banks, c, XT, a["L0_gnn_WT"], a["L0_gnn_W"], a["L0_gnn_AB"], 4, 64, HA, SD)
                p.ve(lambda e: e.tensor_tensor(X[:, :, :], X[:, :, :], XN[:, :, :], ALU.add), marks[-1])
                p.flush()
            bias = sb(ctx, [P, D])
            rec = sb(ctx, [P, 7, 1])
            o = sb(ctx, [P, 7, 64])
            o2 = sb(ctx, [P, 7, 64])
            bl = None
            p.hold("sync", p.dma(10, lambda e: e.dma_start(bias[:, :], broadcast_row(a["L0_gnn_bias"], P))))
            p.flush()

            def finish(h, t0, k, s, mark):
                r, m = reciprocals(rec, k, s, 64, mark)
                end = m = p.ve(lambda e: e.tensor_tensor(o[:, 0:k, :], s[:, :, 0:64], r, ALU.mult), m)
                m = p.ve(lambda e: e.tensor_tensor(
                    o[:, 0:k, :], o[:, 0:k, :],
                    bias[:, 64 * h:64 * h + 64].unsqueeze(1).broadcast_to([P, k, 64]), ALU.add), m, bl)
                m = p.ve(lambda e: e.tensor_scalar(o2[:, 0:k, :], o[:, 0:k, :], 0.0, None, ALU.min), m)
                yield
                m = p.se(lambda e: e.activation(o2[:, 0:k, :], o2[:, 0:k, :], ACT.Exp), m)
                yield
                m = p.ve(lambda e: e.scalar_tensor_tensor(o[:, 0:k, :], o[:, 0:k, :], 0.0,
                                                          o2[:, 0:k, :], ALU.max, ALU.add), m)
                x = X[:, t0:t0 + k, 64 * h:64 * h + 64]
                p.ve(lambda e: e.scalar_tensor_tensor(x, o[:, 0:k, :], -1.0, x, ALU.add, ALU.add), m)
                return end

            def finish_block(b, acc, m):
                m = p.ve(lambda e: e.tensor_scalar(rec[:, 0:4, :], acc[:, :, 64:65], 1e-16, None, ALU.add), m)
                m = p.ve(lambda e: e.reciprocal(rec[:, 0:4, :], rec[:, 0:4, :]), m)
                m = p.ve(lambda e: e.tensor_tensor(o[:, 0:4, :], acc[:, :, 0:64],
                                                   rec[:, 0:4, :].broadcast_to([P, 4, 64]), ALU.mult), m)
                m = p.ve(lambda e: e.tensor_tensor(
                    o[:, 0:4, :], o[:, 0:4, :], bias[:, :].rearrange("p (h c) -> p h c", c=64), ALU.add), m)
                m = p.ve(lambda e: e.tensor_scalar(o2[:, 0:4, :], o[:, 0:4, :], 0.0, None, ALU.min), m)
                m = p.se(lambda e: e.activation(o2[:, 0:4, :], o2[:, 0:4, :], ACT.Exp), m)
                m = p.ve(lambda e: e.scalar_tensor_tensor(o[:, 0:4, :], o[:, 0:4, :], 0.0,
                                                          o2[:, 0:4, :], ALU.max, ALU.add), m)
                x = X[:, b, :].rearrange("p (h c) -> p h c", c=64)
                p.ve(lambda e: e.scalar_tensor_tensor(x, o[:, 0:4, :], -1.0, x, ALU.add, ALU.add), m)

            def listed():
                with ExitStack() as c:
                    by_edges(c, HA, SD, True, finish_block)
                    p.flush()

            def plain():
                with ExitStack() as c:
                    attention(c, 4, 64, HA, SD, True, finish)
                    p.flush()

            either(listed, plain)

        def routing(ctx, XT, xm, Wr, bias, norm, banks, outer=None):
            wr = sb(ctx, [128, 2, 8])
            L = sb(ctx, [P, T, 8])
            R = sb(ctx, [P, T, 8])
            O1, O2 = outer or (sb(ctx, [P, T, 8]), sb(ctx, [P, T, 8]))
            K = sb(ctx, [P, T, 8])
            io = sb(ctx, [P, 8])
            s1 = sb(ctx, [P, T, 1])
            l1 = p.dma(14, lambda e: e.dma_start(wr[:, :, :], Wr.rearrange("(k p) n -> p k n", p=128)))
            i0 = p.ge(lambda e: e.iota(io[:, :], [[1, 8]], base=0, channel_multiplier=0,
                                       allow_small_or_imprecise_dtypes=True))
            b, free, i = banks.take()
            m = small_gemm(XT, wr, 8, xm, b, free, l1)
            lv = PS[0:P, b, 0:8 * T].rearrange("p (t n) -> p t n", n=8)
            if bias is not None:
                br = sb(ctx, [P, 8])
                l2 = p.dma(15, lambda e: e.dma_start(br[:, :], broadcast_row(bias, P)))
                m = p.ve(lambda e: e.tensor_tensor(L[:, :, :], lv, br[:, :].unsqueeze(1).broadcast_to([P, T, 8]),
                                                   ALU.add), m, l2)
            else:
                m = p.ve(lambda e: e.tensor_copy(L[:, :, :], lv), m)
            banks.give(i, m)
            sx = s1[:, :, :].broadcast_to([P, T, 8])
            iob = io[:, :].unsqueeze(1).broadcast_to([P, T, 8])

            def red(src, op, m):
                return p.ve(lambda e: e.tensor_reduce(s1[:, :, 0], src[:, :, :], AX.X, op), m)

            def tt(out, x, y, op, m, *w):
                return p.ve(lambda e: e.tensor_tensor(out[:, :, :], x[:, :, :] if x is not None else None, y, op),
                            m, *w)

            if norm is not None:
                m = red(L, ALU.max, m)
                m = tt(L, L, sx, ALU.subtract, m)
                m = p.se(lambda e: e.activation(L[:, :, :], L[:, :, :], ACT.Exp), m)
                m = red(L, ALU.add, m)
                m = p.ve(lambda e: e.reciprocal(s1[:, :, :], s1[:, :, :]), m)
                m = tt(L, L, sx, ALU.mult, m)

            def first(src, out, m):
                m = red(src, ALU.max, m)
                m = tt(K, src, sx, ALU.is_equal, m)
                m = p.ve(lambda e: e.scalar_tensor_tensor(K[:, :, :], K[:, :, :], -8.0, iob, ALU.mult, ALU.add),
                         m, i0)
                m = red(K, ALU.min, m)
                return tt(out, K, sx, ALU.is_equal, m)

            m = first(L, O1, m)
            m = p.ve(lambda e: e.scalar_tensor_tensor(R[:, :, :], O1[:, :, :], -HUGE, L[:, :, :],
                                                      ALU.mult, ALU.add), m)
            m = first(R, O2, m)
            m = tt(K, O1, O2[:, :, :], ALU.add, m)
            if norm is not None:
                m = tt(K, K, L[:, :, :], ALU.mult, m)
                m = red(K, ALU.add, m)
                if norm == "probs":
                    m = p.ve(lambda e: e.tensor_scalar(s1[:, :, :], s1[:, :, :], 1e-12, None, ALU.max), m)
                m = p.ve(lambda e: e.reciprocal(s1[:, :, :], s1[:, :, :]), m)
                m = tt(K, K, sx, ALU.mult, m)
            return O1, O2, K, m

        def placed(keep, ctx, O1, O2, Cw, cm, XN, *waits):
            sel = sb(ctx, [P, T, 8])
            tri = sb(ctx, [P, P])
            tot = sb(ctx, [128, T, 8])
            run = sb(ctx, [128, T + 1, 8])
            steps = sb(ctx, [128, T])
            order = sb(ctx, [128, SLOTS])
            part = sb(ctx, [128, 1])
            cmp_ = sb(ctx, [128, 8, T])
            nt = sb(ctx, [128, 8])
            bt = sb(ctx, [128, 9])
            slot = sb(ctx, [P, T, 8])
            tmp = sb(ctx, [P, T, 8])
            cmp2 = sb(ctx, [128, SLOTS, 8])
            te = sb(ctx, [128, SLOTS])
            sf = sb(ctx, [P, T])
            t0 = p.ge(lambda e: e.memset(tri[:, :], 1.0))
            t0 = p.ge(lambda e: e.affine_select(out=tri[:, :], in_=tri[:, :], compare_op=ALU.is_gt, fill=0.0,
                                                base=0, pattern=[[1, P]], channel_multiplier=-1), t0)
            t1 = p.ge(lambda e: e.iota(steps[:, :], [[P, T]], base=0, channel_multiplier=0,
                                       allow_small_or_imprecise_dtypes=True))
            t1 = p.ge(lambda e: e.iota(order[:, :], [[1, SLOTS]], base=0, channel_multiplier=0,
                                       allow_small_or_imprecise_dtypes=True))
            t1 = p.ge(lambda e: e.iota(part[:, :], [[0, 1]], base=0, channel_multiplier=1,
                                       allow_small_or_imprecise_dtypes=True))
            m = p.ve(lambda e: e.tensor_tensor(sel[:, :, :], O1[:, :, :], O2[:, :, :], ALU.add), cm)
            flat = sel[:, :, :].rearrange("p t n -> p (t n)")

            def go(e):
                e.matmul(PS[0:P, 4, 0:8 * T], tri[:, :], flat, start=True, stop=True)
                return e.matmul(PS[:, 5, 0:8 * T], ones[0:P, :], flat, start=True, stop=True)

            mm = p.pe(go, m, t0)
            m = p.ve(lambda e: e.tensor_copy(tot[:, :, :].rearrange("p t n -> p (t n)"), PS[:, 5, 0:8 * T]), mm)
            m2 = p.ve(lambda e: e.memset(run[:, 0, :], 0.0))
            for t in range(T):
                m2 = p.ve(lambda e, t=t: e.tensor_tensor(run[:, t + 1, :], run[:, t, :], tot[:, t, :], ALU.add),
                          m, m2)
            m = p.ve(lambda e: e.tensor_tensor(
                cmp_[:, :, :], run[:, T, :].unsqueeze(2).broadcast_to([128, 8, T]),
                steps[:, :].unsqueeze(1).broadcast_to([128, 8, T]), ALU.is_gt), m2, t1)
            m = p.ve(lambda e: e.tensor_reduce(nt[:, :], cmp_[:, :, :], AX.X, ALU.add), m)
            mb = p.ve(lambda e: e.memset(bt[:, 0:1], 0.0))
            for x in range(8):
                mb = p.ve(lambda e, x=x: e.tensor_tensor(bt[:, x + 1:x + 2], bt[:, x:x + 1], nt[:, x:x + 1],
                                                         ALU.add), m, mb)
            m = p.ve(lambda e: e.tensor_tensor(
                cmp2[:, :, :], bt[:, 1:9].unsqueeze(1).broadcast_to([128, SLOTS, 8]),
                order[:, :].unsqueeze(2).broadcast_to([128, SLOTS, 8]), ALU.is_le), mb)
            m = p.ve(lambda e: e.tensor_reduce(te[:, :], cmp2[:, :, :], AX.X, ALU.add), m)
            m = p.ve(lambda e: e.tensor_scalar(te[:, :], te[:, :], 7.0, None, ALU.min), m)
            mi = p.ve(lambda e: e.tensor_copy(keep.expert[:, :], te[:, :]), m)
            m = p.ve(lambda e: e.tensor_scalar(te[:, :], te[:, :], 128.0, part[:, 0:1], ALU.mult, ALU.add), mi)
            p.ve(lambda e: e.tensor_copy(keep.rows[:, :], te[:, :]), m)
            m = p.ve(lambda e: e.tensor_tensor(slot[:, :, :], run[0:P, 0:T, :],
                                               PS[0:P, 4, 0:8 * T].rearrange("p (t n) -> p t n", n=8),
                                               ALU.add), m2)
            mb = p.ve(lambda e: e.tensor_scalar(bt[:, :], bt[:, :], float(P), None, ALU.mult), mb)
            m = p.ve(lambda e: e.tensor_tensor(slot[:, :, :], slot[:, :, :],
                                               bt[0:P, 0:8].unsqueeze(1).broadcast_to([P, T, 8]), ALU.add), m, mb)
            dep = m
            for O, idx, w in ((O1, keep.slot[0], keep.weight[0]), (O2, keep.slot[1], keep.weight[1])):
                m = p.ve(lambda e, O=O: e.tensor_tensor(tmp[:, :, :], slot[:, :, :], O[:, :, :], ALU.mult), dep)
                m = p.ve(lambda e: e.tensor_reduce(sf[:, :], tmp[:, :, :], AX.X, ALU.add), m)
                mi = p.ve(lambda e, idx=idx: e.tensor_copy(idx[:, :], sf[:, :]), m)
                m = p.ve(lambda e, O=O: e.tensor_tensor(tmp[:, :, :], Cw[:, :, :], O[:, :, :], ALU.mult), mi)
                dep = p.ve(lambda e, w=w: e.tensor_reduce(w[:, :], tmp[:, :, :], AX.X, ALU.add), m)
            last = None
            for t in range(T):
                for idx in keep.slot:
                    last = p.dma(-1, lambda e, t=t, idx=idx: e.indirect_dma_start(
                        XS, bass.IndirectOffsetOnAxis(idx[:, t:t + 1], 0), XN[:, t, :], None), dep, *waits,
                        by="gpsimd")
            p.hold("gpsimd", last)
            return dep

        class Keep:

            def __init__(self, ctx, hid, W1):
                self.expert, self.rows = sb(ctx, [128, SLOTS], i32), sb(ctx, [128, SLOTS], i32)
                self.slot = [sb(ctx, [P, T], i32) for _ in range(2)]
                self.weight = [sb(ctx, [P, T]) for _ in range(2)]
                self.w1 = sb(ctx, [128, 8, 2, hid])
                self.loads = [p.dma(16 + x % 4, lambda e, x=x: e.dma_start(
                    self.w1[:, x, :, :], W1[x].rearrange("(k p) n -> p k n", p=128)), by="scalar")
                    for x in range(8)]
                p.hold("scalar", *self.loads)

        def output_biases(ctx, Cw, cm, b2, xready):
            CT = sb(ctx, [8, N])
            b2s = sb(ctx, [8, D])
            l2 = p.dma(11, lambda e: e.dma_start(b2s[:, :], b2))
            banks = Ring(range(8))
            for g in range(7):
                ts = range(4 * g, min(4 * g + 4, T))
                b, free, i = banks.take()

                def go(e, ts=ts, b=b):
                    for n, t in enumerate(ts):
                        r = e.transpose(PS[0:8, b, n * P:n * P + P], Cw[:, t, :], ident[0:P, 0:P])
                    return r

                m = p.pe(go, free, cm)
                ct = p.ve(lambda e, b=b, g=g, n=len(ts) * P: e.tensor_copy(
                    CT[:, 500 * g:500 * g + n], PS[0:8, b, 0:n]), m)
                banks.give(i, ct)
            for t0 in range(0, T, 2):
                ts = range(t0, min(t0 + 2, T))
                b, free, i = banks.take()

                def go(e, ts=ts, b=b):
                    for n, t in enumerate(ts):
                        r = e.matmul(PS[0:P, b, n * D:n * D + D], CT[:, t * P:t * P + P], b2s[:, :],
                                     start=True, stop=True)
                    return r

                m = p.pe(go, free, ct, l2)
                xs = X[:, ts[0]:ts[-1] + 1, :].rearrange("p t d -> p (t d)")
                biased = p.ve(lambda e, b=b, xs=xs, n=len(ts) * D: e.tensor_tensor(
                    xs, xs, bank(b, n, P), ALU.add), m, xready)
                banks.give(i, biased)

        def experts(ctx, keep, hid, CC, W2, scale):
            nh, nb = hid // 128, (hid + 511) // 512
            width = nh + (4 if scale else 0)
            w2 = sb(ctx, [128, 8, nh, D])
            lw = [p.dma(16 + x % 4, lambda e, x=x: e.dma_start(
                w2[:, x, :, :], W2[x].rearrange("(k p) n -> p k n", p=128)), by="scalar") for x in range(8)]
            lw = lw[4:]
            w1f = keep.w1[:, :, :, :].rearrange("p e k n -> p (e k n)")
            w2f = w2[:, :, :, :].rearrange("p e k n -> p (e k n)")
            rows = Ring([sb(ctx, [P, D]) for _ in range(4)])
            consts = Ring([sb(ctx, [128, width]) for _ in range(7)])
            xts = Ring([sb(ctx, [128, 2, P]) for _ in range(2)])
            hs = Ring([sb(ctx, [P, hid]) for _ in range(2)])
            hts = Ring([sb(ctx, [128, nh, P]) for _ in range(2)])
            ys = Ring([sb(ctx, [P, D]) for _ in range(3)])
            tx, g1 = Ring((0, 7)), Ring((1, 2) if nb == 1 else (1,))
            th, g2 = Ring((3, 4) if nb == 1 else (3,)), Ring((5, 6))
            state, value = {}, {}

            def fetch(i):
                row, rf, ri = rows.take()
                l1 = p.dma(ri, lambda e: e.dma_start(row[:, :], XS[i * P:i * P + P, :]), rf)
                con, cf, ci = consts.take()
                lc = p.dma(-2 - ci, lambda e: e.indirect_dma_start(
                    con[:, :], None, CC, bass.IndirectOffsetOnAxis(keep.rows[:, i:i + 1], 0)), cf, by="gpsimd")
                state[i] = row, ri, l1, con, ci, lc

            def turn_in(i):
                row, ri, l1, con, ci, lc = state[i]
                b, bf, bi = tx.take()
                xt, xf, xi = xts.take()

                def go(e):
                    for k in range(2):
                        r = e.transpose(PS[:, b, k * P:k * P + P], row[:, k * 128:k * 128 + 128],
                                        ident[0:P, 0:P])
                    return r

                m = p.pe(go, l1, bf)
                rows.give(ri, m)
                if scale:
                    for k in range(2):
                        m1 = p.ve(lambda e, k=k: e.tensor_scalar(
                            xt[:, k, :], PS[:, b, k * P:k * P + P], con[:, nh + k:nh + k + 1],
                            con[:, nh + 2 + k:nh + 3 + k], ALU.mult, ALU.add), m, lc, xf)
                else:
                    m1 = p.ve(lambda e: e.tensor_copy(xt[:, :, :].rearrange("p k n -> p (k n)"),
                                                      PS[:, b, 0:2 * P]), m, xf)
                tx.give(bi, m1)
                state[i] = (con, ci, lc, xt, xi, m1)

            def up(i):
                con, ci, lc, xt, xi, ready = state[i]
                b, bf, bi = g1.take()
                h, hf, hi = hs.take()
                cols = min(512, hid)

                def go(e):
                    value[i] = v = nc.values_load(
                        keep.expert[0:1, i:i + 1], engines=[mybir.EngineType.PE], min_val=0, max_val=7,
                        skip_runtime_bounds_check_because="a count of at most 7, by a minimum")
                    for c in range(nb):
                        for k in range(2):
                            r = e.matmul(PS[0:P, b + c, 0:cols], xt[:, k, :],
                                         w1f[:, bass.ds(v * (2 * hid) + (k * hid + c * 512), cols)],
                                         start=k == 0, stop=k == 1)
                    return r

                m = p.pe(go, ready, bf)
                xts.give(xi, m)
                m = p.ve(lambda e: e.tensor_copy(h[:, :].rearrange("p (b n) -> p b n", b=nb),
                                                 PS[0:P, b:b + nb, 0:cols]), m, hf)
                g1.give(bi, m)
                state[i] = (con, ci, lc, h, hi, m)

            def middle(i):
                con, ci, lc, h, hi, ready = state[i]
                b, bf, bi = th.take()
                ht, hf, ti = hts.take()

                def go(e):
                    for c in range(nh):
                        r = e.transpose(PS[:, b + c // 4, (c % 4) * P:(c % 4) * P + P],
                                        h[:, c * 128:c * 128 + 128], ident[0:P, 0:P])
                    return r

                m = p.pe(go, ready, bf)
                hs.give(hi, m)
                for c in range(nh):
                    m1 = p.se(lambda e, c=c: e.activation(
                        ht[:, c, :], PS[:, b + c // 4, (c % 4) * P:(c % 4) * P + P], ACT.Gelu,
                        bias=con[:, c:c + 1]), m, lc, hf)
                th.give(bi, m1)
                consts.give(ci, m1)
                state[i] = (ht, ti, m1)

            def down(i):
                ht, ti, ready = state.pop(i)
                b, bf, bi = g2.take()
                y, yf, yi = ys.take()

                def go(e):
                    for c in range(nh):
                        r = e.matmul(PS[0:P, b, 0:D], ht[:, c, :],
                                     w2f[:, bass.ds(value[i] * (nh * D) + c * D, D)],
                                     start=c == 0, stop=c == nh - 1)
                    return r

                m = p.pe(go, ready, bf, *lw)
                hts.give(ti, m)
                m = p.ve(lambda e: e.tensor_copy(y[:, :], PS[0:P, b, 0:D]), m, yf)
                g2.give(bi, m)
                ys.give(yi, p.dma(5 + yi, lambda e: e.dma_start(YS[i * P:i * P + P, :], y[:, :]), m))

            for i in range(-3, SLOTS + 3):
                if i + 3 < SLOTS:
                    fetch(i + 3)
                if 0 <= i < SLOTS:
                    turn_in(i)
                if 0 <= i - 1 < SLOTS:
                    up(i - 1)
                if 0 <= i - 2 < SLOTS:
                    middle(i - 2)
                if 0 <= i - 3 < SLOTS:
                    down(i - 3)
            p.hold("gpsimd", *ys.free)
            got = Ring([sb(ctx, [P, D]) for _ in range(6)])
            m = None
            for t in range(T):
                for c in range(2):
                    y, yf, yi = got.take()
                    ld = p.dma(-2 - yi, lambda e, y=y, c=c, t=t: e.indirect_dma_start(
                        y[:, :], None, YS, bass.IndirectOffsetOnAxis(keep.slot[c][:, t:t + 1], 0)), yf,
                        by="gpsimd")
                    m = p.ve(lambda e, y=y, c=c, t=t: e.scalar_tensor_tensor(
                        X[:, t, :], y[:, :], keep.weight[c][:, t:t + 1], X[:, t, :], ALU.mult, ALU.add),
                        ld, m if c else None)
                    got.give(yi, m)

        with phase() as ctx:
            keep = Keep(ctx, 256, a["L0_ffn_w1"])
            with ExitStack() as c:
                XN = sb(c, [P, T, D])
                XT = sb(c, [128, 2, N])
                marks = layernorm(c, X, XN)
                xm = transposed(XN, XT, marks, Ring(range(8)))
                p.ve(lambda e: e.tensor_tensor(X[:, :, :], X[:, :, :], XN[:, :, :], ALU.add), marks[-1])
                p.flush()
                O1, O2, Cw, cm = routing(c, XT, xm, a["L0_ffn_router_wT"], None, "probs", Ring(range(4)))
                dep = placed(keep, c, O1, O2, Cw, cm, XN, marks[-1])
                output_biases(c, Cw, dep, a["L0_ffn_b2"], None)
                p.flush()
            experts(ctx, keep, 256, a["L0_ffn_C"], a["L0_ffn_w2"], False)

        with phase() as ctx:
            H1 = sb(ctx, [P, T, D])
            with ExitStack() as c0:
                HA = sb(c0, [P, T, 4, 65])
                SD = sb(c0, [P, T, 8])
                with ExitStack() as c:
                    XN = sb(c, [P, T, D])
                    XT = sb(c, [128, 2, N])
                    marks = layernorm(c, X, XN)
                    banks = Ring(range(8))
                    xm = transposed(XN, XT, marks, banks)
                    gat(xm, banks, c, XT, a["L1_gnn_W1T"], a["L1_gnn_W1"], a["L1_gnn_AB1"], 4, 64, HA, SD)
                    p.flush()
                rec = sb(c0, [P, 7, 1])

                def finish(h, t0, k, s, mark):
                    x = H1[:, t0:t0 + k, 64 * h:64 * h + 64]
                    r, m = reciprocals(rec, k, s, 64, mark)
                    end = m = p.ve(lambda e: e.tensor_tensor(x, s[:, :, 0:64], r, ALU.mult), m)
                    yield
                    p.ve(lambda e: e.tensor_scalar(x, x, 0.0, None, ALU.max), m)
                    return end

                def finish_block(b, acc, m):
                    m = p.ve(lambda e: e.tensor_scalar(rec[:, 0:4, :], acc[:, :, 64:65], 1e-16, None,
                                                       ALU.add), m)
                    m = p.ve(lambda e: e.reciprocal(rec[:, 0:4, :], rec[:, 0:4, :]), m)
                    x = H1[:, b, :].rearrange("p (h c) -> p h c", c=64)
                    m = p.ve(lambda e: e.tensor_tensor(x, acc[:, :, 0:64],
                                                       rec[:, 0:4, :].broadcast_to([P, 4, 64]), ALU.mult), m)
                    p.ve(lambda e: e.tensor_scalar(x, x, 0.0, None, ALU.max), m)

                def listed():
                    with ExitStack() as c:
                        by_edges(c, HA, SD, False, finish_block)
                        p.flush()

                def plain():
                    with ExitStack() as c:
                        attention(c, 4, 64, HA, SD, False, finish)
                        p.flush()

                either(listed, plain)
            with ExitStack() as c0:
                HB = sb(c0, [P, T, 1, 257])
                SD = sb(c0, [P, T, 2])
                with ExitStack() as c:
                    XT = sb(c, [128, 2, N])
                    banks = Ring(range(8))
                    xm = transposed(H1, XT, [None] * T, banks)
                    gat(xm, banks, c, XT, a["L1_gnn_W2T"], a["L1_gnn_W2"], a["L1_gnn_AB2"], 1, 256, HB, SD)
                    p.flush()
                rec = sb(c0, [P, 1, 1])
                o = sb(c0, [P, 1, 256])

                def finish2(h, t0, k, s, mark):
                    r, m = reciprocals(rec, 1, s, 256, mark)
                    end = m = p.ve(lambda e: e.tensor_tensor(o[:, :, :], s[:, :, 0:256], r, ALU.mult), m)
                    x = X[:, t0:t0 + 1, :]
                    p.ve(lambda e: e.tensor_tensor(x, x, o[:, :, :], ALU.add), m)
                    return [end]
                    yield

                def listed():
                    with ExitStack() as c:
                        attention(c, 1, 256, HB, SD, False, finish2, ADJ16, f16)
                        p.flush()

                def plain():
                    with ExitStack() as c:
                        attention(c, 1, 256, HB, SD, False, finish2)
                        p.flush()

                either(listed, plain)

        L, NC = 25, 125
        with ExitStack() as ctx:
            XH, XL = sb(ctx, [128, L, 6, NC], f16), sb(ctx, [128, L, 6, NC], f16)
            id16 = sb(ctx, [128, 128], f16)
            i16 = p.ve(lambda e: e.tensor_copy(id16[:, :], ident[:, :]))
            HS = sb(ctx, [128, L, 2, NC])
            V = sb(ctx, [128, 2, 6, 128])
            with ExitStack() as c:
                XT = sb(c, [128, 2, N])
                U = sb(c, [128, 2, 6, 128])
                bg = sb(c, [128, 6])
                XN = sb(c, [P, T, D])
                loads = []
                raw = Ring([sb(c, [128, 500]) for _ in range(3)])
                for n, g in enumerate("ioc"):
                    lu = p.dma(1 + n, lambda e, n=n, g=g: e.dma_start(
                        U[:, :, 2 * n:2 * n + 2, :],
                        a[f"L1_ffn_U_{g}"].rearrange("(k p) (m n) -> p k m n", p=128, m=2)))
                    lv = p.dma(4 + n, lambda e, n=n, g=g: e.dma_start(
                        V[:, :, 2 * n:2 * n + 2, :],
                        a[f"L1_ffn_V_{g}"].rearrange("(k p) (m n) -> p k m n", p=128, m=2)))
                    lb = p.dma(7 + n, lambda e, n=n, g=g: e.dma_start(
                        bg[:, 2 * n:2 * n + 2], a[f"L1_ffn_b_{g}"]))
                    loads += [lu, lv, lb]
                marks = layernorm(c, X, XN)
                banks = Ring(range(8))
                xm = transposed(XN, XT, marks, banks)
                for g in range(7):
                    n = min(500, N - 500 * g)
                    for m6 in range(6):
                        b, free, i = banks.take()

                        def go(e, b=b, m6=m6, g=g, n=n):
                            for k in range(2):
                                r = e.matmul(bank(b, n), U[:, k, m6, :], XT[:, k, 500 * g:500 * g + n],
                                             start=k == 0, stop=k == 1)
                            return r

                        m = p.pe(go, free, *xm[g], *loads)
                        c0, c1 = 20 * g, 20 * g + n // L
                        x, xfree, xi = raw.take()
                        m = p.se(lambda e, b=b, m6=m6, n=n, x=x: e.activation(
                            x[:, 0:n], bank(b, n), ACT.Identity, bias=bg[:, m6:m6 + 1]), m, xfree, *loads)
                        banks.give(i, m)
                        m = p.ve(lambda e, n=n, x=x: e.tensor_scalar(
                            x[:, 0:n], x[:, 0:n], 60000.0, -60000.0, ALU.min, ALU.max), m)
                        v = x[:, 0:n].rearrange("p (c s) -> p c s", s=L)
                        h = XH[:, :, m6, c0:c1].rearrange("p s c -> p c s")
                        l = XL[:, :, m6, c0:c1].rearrange("p s c -> p c s")
                        m = p.se(lambda e, v=v, h=h: e.activation(h, v, ACT.Copy), m)
                        raw.give(xi, p.ve(lambda e, v=v, h=h, l=l: e.tensor_tensor(l, v, h, ALU.subtract), m))
                p.flush()
            H0, C0 = sb(ctx, [128, 2, NC]), sb(ctx, [128, 2, NC])
            Cs = sb(ctx, [128, 2, NC])
            Gt = sb(ctx, [128, 6, NC])
            t1, t2, t3 = sb(ctx, [128, 2, NC]), sb(ctx, [128, 2, NC]), sb(ctx, [128, 2, NC])
            df = sb(ctx, [128, 4])
            ft = sb(ctx, [1, 2])
            go_on = sb(ctx, [1, 1], i32)
            for t in (H0, C0):
                p.ge(lambda e, t=t: e.memset(t[:, :, :], 0.0))
            p.ge(lambda e: e.memset(go_on[:, :], 1))
            p.flush()
            with nc.Fori(0, NC // 25):
                more = nc.values_load(go_on[0:1, 0:1], min_val=0, max_val=1)
                nc.all_engine_barrier(sem_only=True)
                with nc.If(more == 1):
                    with nc.Fori(0, 25):
                        flag = nc.values_load(go_on[0:1, 0:1], min_val=0, max_val=1)
                        nc.all_engine_barrier(sem_only=True)
                        with nc.If(flag == 1):
                            q.rewind()
                            m = q.ve(lambda e: e.tensor_copy(Cs[:, :, :], C0[:, :, :]))
                            hm = cm = [m, m]
                            gates = ((4, 2, 0), (0, 1, 1), (1, 1, 2), (2, 2, 3))
                            used = [[None] * 4, [None] * 4]

                            def inputs_of(s):
                                for g6, w, b in gates:
                                    def go(e, b=4 * (s % 2) + b, g6=g6, w=w):
                                        for part in (XH, XL):
                                            r = e.matmul(
                                                PS[:, b, 0:w * NC], id16[:, :],
                                                part[:, s, g6:g6 + w, :].rearrange("p g c -> p (g c)"),
                                                start=part is XH, stop=False, skip_group_check=True)
                                        return r
                                    q.pe(go, used[s % 2][b])

                            inputs_of(0)
                            for s in range(L):
                                hprev = H0[:, :, :] if s == 0 else HS[:, s - 1, :, :]
                                acts = []

                                def part_of(g6, w, b, ks):
                                    def go(e, b=4 * (s % 2) + b, g6=g6, w=w, hprev=hprev, ks=ks):
                                        for k in ks:
                                            for n in range(w):
                                                r = e.matmul(PS[:, b, n * NC:n * NC + NC], V[:, k, g6 + n, :],
                                                             hprev[:, k, :], start=False, stop=k == 1,
                                                             skip_group_check=True)
                                        return r
                                    return q.pe(go, *[hm[k] for k in ks])

                                for gate in gates:
                                    part_of(*gate, (0,))
                                    acts.append((part_of(*gate, (1,)), *gate))
                                if s + 1 < L:
                                    inputs_of(s + 1)
                                m1 = [q.ve(lambda e, hprev=hprev, k=k: e.tensor_tensor(
                                    t1[:, k, :], hprev[:, k, :], Cs[:, k, :], ALU.mult), hm[k], cm[k])
                                    for k in range(2)]
                                am = []

                                def gated(m, g6, w, b):
                                    am.append(q.se(lambda e, b=4 * (s % 2) + b: e.activation(
                                        Gt[:, g6:g6 + w, :],
                                        PS[:, b, 0:w * NC].rearrange("p (g c) -> p g c", c=NC),
                                        ACT.Tanh if g6 == 4 else ACT.Sigmoid), m, *hm))
                                    used[s % 2][b] = am[-1]

                                for x in acts[0:3]:
                                    gated(*x)
                                cm, ms = list(cm), []
                                for k in range(2):
                                    m = q.ve(lambda e, k=k: e.tensor_tensor(
                                        t2[:, k, :], Gt[:, k, :], Gt[:, 4 + k, :], ALU.mult), am[1 + k])
                                    cm[k] = q.ve(lambda e, k=k: e.tensor_tensor(
                                        Cs[:, k, :], t1[:, k, :], t2[:, k, :], ALU.add), m1[k], m)
                                    ms.append(q.se(lambda e, k=k: e.activation(t3[:, k, :], Cs[:, k, :],
                                                                               ACT.Tanh), cm[k]))
                                    if k == 0:
                                        gated(*acts[3])
                                ms = [am[3], ms[1]]
                                hm = [q.ve(lambda e, s=s, k=k: e.tensor_tensor(
                                    HS[:, s, k, :], Gt[:, 2 + k, :], t3[:, k, :], ALU.mult), ms[k])
                                    for k in range(2)]
                            nb = NC - 1
                            new_h, new_c = HS[:, L - 1, :, 0:nb], Cs[:, :, 0:nb]
                            m = q.ve(lambda e: e.tensor_tensor(t1[:, :, 0:nb], new_h, H0[:, :, 1:NC],
                                                               ALU.subtract), *hm)
                            m = q.ve(lambda e: e.tensor_reduce(df[:, 0:1], t1[:, :, 0:nb], AX.XY, ALU.max,
                                                               apply_absolute_value=True), m)
                            m2 = q.ve(lambda e: e.tensor_tensor(t2[:, :, 0:nb], new_c, C0[:, :, 1:NC],
                                                                ALU.subtract), m)
                            m2 = q.ve(lambda e: e.tensor_reduce(df[:, 1:2], t2[:, :, 0:nb], AX.XY, ALU.max,
                                                                apply_absolute_value=True), m2)
                            q.ve(lambda e: e.tensor_copy(H0[:, :, 1:NC], new_h), m)
                            q.ve(lambda e: e.tensor_copy(C0[:, :, 1:NC], new_c), m2)
                            m = q.ve(lambda e: e.tensor_tensor(df[:, 2:3], df[:, 0:1], df[:, 1:2], ALU.max), m2)
                            m = q.pe(lambda e: e.transpose(PS[0:1, 7, 0:128], df[:, 2:3], ident[:, :]), m)
                            m = q.ve(lambda e: e.tensor_reduce(ft[:, 0:1], PS[0:1, 7, 0:128], AX.X, ALU.max), m)
                            m = q.ve(lambda e: e.tensor_scalar(go_on[:, :], ft[:, 0:1], TOL, None, ALU.is_gt), m)
                            q.hold("vector", m)
                            q.flush()
                            nc.multi_engine_barrier(list(mybir.ALL_ENGINES), sems_to_clear=q.numbers())
            inorder = Ring([sb(ctx, [128, 2, 2, 5, L]) for _ in range(3)])
            banks = Ring(range(8))
            for t0 in range(0, T, 2):
                ts = range(t0, min(t0 + 2, T))
                b, free, i = banks.take()
                row, rfree, ri = inorder.take()
                for n, t in enumerate(ts):
                    for k in range(2):
                        mc = p.se(lambda e, n=n, t=t, k=k, row=row: e.activation(
                            row[:, n, k, :, :].rearrange("p c s -> p s c"),
                            HS[:, :, k, 5 * t:5 * t + 5], ACT.Copy), rfree)

                def go(e, ts=ts, b=b, row=row):
                    for n, t in enumerate(ts):
                        for k in range(2):
                            r = e.transpose(PS[0:P, b, n * D + 128 * k:n * D + 128 * k + 128],
                                            row[:, n, k, :, :].rearrange("p c s -> p (c s)"),
                                            ident[:, :])
                    return r

                m = p.pe(go, free, mc)
                inorder.give(ri, m)
                xs = X[:, ts[0]:ts[-1] + 1, :].rearrange("p t d -> p (t d)")
                banks.give(i, p.ve(lambda e, b=b, xs=xs, n=len(ts) * D: e.tensor_tensor(
                    xs, xs, bank(b, n, P), ALU.add), m))
            p.flush()

        def convolution(ctx, banks, XT, xm, W, dis, HS, finish_of):
            w = sb(ctx, [128, 2, D])
            l1 = p.dma(1, lambda e: e.dma_start(w[:, :, :], W.rearrange("(k p) n -> p k n", p=128)))

            def sink(b, ts, m):
                k = len(ts)
                return p.ve(lambda e: e.tensor_tensor(
                    HS[:, ts[0]:ts[0] + k, :], bank(b, k * D, P).rearrange("p (t d) -> p t d", d=D),
                    dis[:, ts[0]:ts[0] + k].unsqueeze(2).broadcast_to([P, k, D]), ALU.mult), m)

            rows_gemm(XT, w, xm, banks, sink, l1)
            p.flush()

            def products(c, A, dt, operands, finish):
                half = 13
                ads = Ring([sb(c, [P, half * P], dt) for _ in range(4)])
                frees = [None] * 7
                for tiles in (range(0, half), range(half, T)):
                    lo, n = tiles[0] * P, len(tiles) * P
                    for j in range(T):
                        ad, free, i = ads.take()
                        ld = p.dma(2 + i, lambda e, ad=ad, j=j, lo=lo, n=n: e.dma_start(
                            ad[:, 0:n], A[j][:, lo:lo + n]), free)
                        parts, ready = operands(j)

                        for n0 in range(0, len(tiles), 2):
                            def go(e, ad=ad, j=j, n0=n0, tiles=tiles, parts=parts):
                                for n in range(n0, min(n0 + 2, len(tiles))):
                                    for x, part in enumerate(parts):
                                        r = e.matmul(PS[0:P, n // 2, (n % 2) * D:(n % 2) * D + D],
                                                     ad[:, n * P:n * P + P], part,
                                                     start=(j == 0 and n % 2 == 0 and x == 0),
                                                     stop=j == T - 1 and x == len(parts) - 1,
                                                     skip_group_check=True)
                                return r

                            m = p.pe(go, ld, ready, frees[n0 // 2] if j == 0 else None)
                        ads.give(i, m)
                    ends = [finish(tiles[n:n + 2],
                                   PS[0:P, n // 2, 0:len(tiles[n:n + 2]) * D].rearrange(
                                       "p (t d) -> p t d", d=D), m)
                            for n in range(0, len(tiles), 2)]
                    frees = [next(x) for x in ends]
                    for x in ends:
                        next(x, None)

            def plain():
                with ExitStack() as c:
                    products(c, adj, f32, lambda j: ([HS[:, j, :]], None), finish_of(c, None))
                    p.flush()

            def split():
                with ExitStack() as c:
                    hi, lo = sb(c, [P, T, D], f16), sb(c, [P, T, D], f16)
                    mx = sb(c, [P, 1])
                    one = sb(c, [1, 1])
                    big = sb(c, [P, 1])
                    eb = sb(c, [P, 1], i32)
                    sb_ = sb(c, [P, 1], i32)
                    sc = sb(c, [P, 2])
                    m = p.ve(lambda e: e.tensor_reduce(mx[:, :], HS[:, :, :], AX.XY, ALU.max,
                                                       apply_absolute_value=True))
                    m = p.pe(lambda e: e.transpose(PS[0:1, 0, 0:P], mx[:, :], ident[0:P, 0:P]), m)
                    m = p.ve(lambda e: e.tensor_reduce(one[:, :], PS[0:1, 0, 0:P], AX.X, ALU.max), m)
                    m = p.pe(lambda e: e.matmul(PS[0:P, 1, 0:1], ones[0:1, 0:P], one[:, :],
                                                start=True, stop=True), m)
                    m = p.ve(lambda e: e.tensor_scalar(big[:, :], PS[0:P, 1, 0:1], 2.0 ** -90, None, ALU.max), m)
                    m = p.ve(lambda e: e.tensor_scalar(eb[:, :], big[:, :].bitcast(i32), 0x7F800000, None,
                                                       ALU.bitwise_and), m)
                    m1 = p.ve(lambda e: e.tensor_scalar(sb_[:, :], eb[:, :], -1.0, float(254 << 23),
                                                        ALU.mult, ALU.add), m)
                    m1 = p.ve(lambda e: e.tensor_scalar(sc[:, 0:1], sb_[:, :].bitcast(f32), 2.0 ** 14, None,
                                                        ALU.mult), m1)
                    m2 = p.ve(lambda e: e.tensor_scalar(sc[:, 1:2], eb[:, :].bitcast(f32), 2.0 ** -14, None,
                                                        ALU.mult), m1)
                    marks = []
                    for t0 in range(0, T, 5):
                        m = p.se(lambda e, t0=t0: e.activation(hi[:, t0:t0 + 5, :], HS[:, t0:t0 + 5, :],
                                                               ACT.Copy, scale=sc[:, 0:1]), m1)
                        marks.append(p.ve(lambda e, t0=t0: e.scalar_tensor_tensor(
                            lo[:, t0:t0 + 5, :], HS[:, t0:t0 + 5, :], sc[:, 0:1], hi[:, t0:t0 + 5, :],
                            ALU.mult, ALU.subtract), m, m2))
                    products(c, ADJ16, f16, lambda j: ([hi[:, j, :], lo[:, j, :]], marks[j // 5]),
                             finish_of(c, sc[:, 1:2]))
                    p.flush()

            either(split, plain)

        with phase() as ctx:
            Y = sb(ctx, [P, T, D])
            XT = sb(ctx, [128, 2, N])
            HS = sb(ctx, [P, T, D])
            marks = layernorm(ctx, X, Y)
            for layer in (1, 2, 3):
                with ExitStack() as c:
                    bias = sb(c, [P, D])
                    p.hold("sync", p.dma(10, lambda e, bias=bias, layer=layer: e.dma_start(
                        bias[:, :], broadcast_row(a[f"L2_gnn_b{layer}"], P))))
                    banks = Ring(range(8))
                    xm = transposed(Y, XT, marks if layer == 1 else [None] * T, banks)

                    def finish_of(c, scale, layer=layer, bias=bias):
                        def finish(ts, s, m):
                            k = len(ts)
                            y, hs = Y[:, ts[0]:ts[0] + k, :], HS[:, ts[0]:ts[0] + k, :]
                            dd = dis0[:, ts[0]:ts[0] + k].unsqueeze(2).broadcast_to([P, k, D])
                            bb = bias[:, :].unsqueeze(1).broadcast_to([P, k, D])
                            if scale is None:
                                m = end = p.ve(lambda e: e.tensor_tensor(y, s, hs, ALU.add), m)
                            else:
                                m = end = p.ve(lambda e: e.scalar_tensor_tensor(y, s, scale, hs,
                                                                                ALU.mult, ALU.add), m)
                            yield end
                            m = p.ve(lambda e: e.tensor_tensor(y, y, dd, ALU.mult), m)
                            m = p.ve(lambda e: e.tensor_tensor(y, y, bb, ALU.add), m)
                            if layer < 3:
                                p.ve(lambda e: e.tensor_scalar(y, y, 0.0, None, ALU.max), m)
                            else:
                                x = X[:, ts[0]:ts[0] + k, :]
                                p.ve(lambda e: e.tensor_tensor(x, x, y, ALU.add), m)
                        return finish

                    convolution(c, banks, XT, xm, a[f"L2_gnn_W{layer}"], dis0, HS, finish_of)
                    p.flush()

        with phase() as ctx:
            keep = Keep(ctx, 1024, a["L2_ffn_W1"])
            with ExitStack() as c0:
                XN = sb(c0, [P, T, D])
                both = sb(c0, [P, T, 8]), sb(c0, [P, T, 8])
                weights = sb(c0, [P, T, 8])
                with ExitStack() as c:
                    XT = sb(c, [128, 2, N])
                    marks = layernorm(c, X, XN)
                    xm = transposed(XN, XT, marks, Ring(range(8)))
                    O1, O2, Cw, cm = routing(c, XT, xm, a["L2_ffn_Wr"], a["L2_ffn_br"], "plain",
                                             Ring(range(4)), both)
                    p.ve(lambda e: e.tensor_copy(weights[:, :, :], Cw[:, :, :]), cm)
                    p.flush()
                marks = layernorm(c0, XN, XN)
                dep = placed(keep, c0, O1, O2, weights, None, XN, marks[-1])
                output_biases(c0, weights, dep, a["L2_ffn_b2"], None)
                p.flush()
            experts(ctx, keep, 1024, a["L2_ffn_C"], a["L2_ffn_W2"], True)

        with phase() as ctx:
            Y = sb(ctx, [P, T, D])
            XT = sb(ctx, [128, 2, N])
            HS = sb(ctx, [P, T, D])
            marks = layernorm(ctx, X, Y)
            banks = Ring(range(8))
            xm = transposed(Y, XT, marks, banks)

            def finish_of(c, scale):
                outs = Ring([sb(c, [P, 2, D]) for _ in range(7)])

                def finish(ts, s, m):
                    k = len(ts)
                    dd = dis1[:, ts[0]:ts[0] + k].unsqueeze(2).broadcast_to([P, k, D])
                    x = X[:, ts[0]:ts[0] + k, :]
                    o, free, i = outs.take()
                    if scale is None:
                        m = end = p.ve(lambda e: e.tensor_tensor(o[:, 0:k, :], s, dd, ALU.mult), m, free)
                    else:
                        m = end = p.ve(lambda e: e.scalar_tensor_tensor(o[:, 0:k, :], s, scale, dd,
                                                                        ALU.mult, ALU.mult), m, free)
                    yield end
                    outs.give(i, p.ve(lambda e: e.tensor_tensor(x, x, o[:, 0:k, :], ALU.add), m))
                return finish

            convolution(ctx, banks, XT, xm, a["L3_gnn_W"], dis1, HS, finish_of)

        with phase() as ctx:
            keep = Keep(ctx, 512, a["L3_ffn_W1"])
            with ExitStack() as c:
                XN = sb(c, [P, T, D])
                XT = sb(c, [128, 2, N])
                marks = layernorm(c, X, XN)
                xm = transposed(XN, XT, marks, Ring(range(8)))
                O1, O2, Cw, cm = routing(c, XT, xm, a["L3_ffn_Wg"], a["L3_ffn_bg"], None, Ring(range(4)))
                dep = placed(keep, c, O1, O2, Cw, cm, XN, marks[-1])
                output_biases(c, Cw, dep, a["L3_ffn_b2"], None)
                p.flush()
            experts(ctx, keep, 512, a["L3_ffn_C"], a["L3_ffn_W2"], False)

        p.hold("sync", p.dma(0, lambda e: e.dma_start(a["out"].rearrange("(t p) d -> p t d", p=P), X[:, :, :])))
        p.flush()


def laid_out(inputs):
    import numpy as np

    x = {k: np.ascontiguousarray(v) for k, v in inputs.items()}
    out = {k: x[k] for k in (
        "x", "src", "dst", "L0_gnn_W", "L0_gnn_bias", "L0_ffn_w1", "L0_ffn_w2", "L0_ffn_b2",
        "L1_gnn_W1", "L1_gnn_W2", "L2_gnn_W1", "L2_gnn_b1", "L2_gnn_W2", "L2_gnn_b2", "L2_gnn_W3",
        "L2_gnn_b3", "L2_ffn_Wr", "L2_ffn_br", "L2_ffn_W1", "L2_ffn_W2", "L2_ffn_b2", "L3_gnn_W",
        "L3_ffn_Wg", "L3_ffn_bg", "L3_ffn_W1", "L3_ffn_W2", "L3_ffn_b2")}
    for k in ("i", "o", "c"):
        out[f"L1_ffn_U_{k}"] = x[f"L1_ffn_U_{k}"]
        out[f"L1_ffn_V_{k}"] = x[f"L1_ffn_V_{k}"]
        out[f"L1_ffn_b_{k}"] = np.ascontiguousarray(x[f"L1_ffn_b_{k}"].reshape(2, 128).T)
    for name, key in (("L0_gnn_WT", "L0_gnn_W"), ("L1_gnn_W1T", "L1_gnn_W1"), ("L1_gnn_W2T", "L1_gnn_W2"),
                      ("L0_ffn_router_wT", "L0_ffn_router_w")):
        out[name] = np.ascontiguousarray(x[key].T)
    for name, s, d in (("L0_gnn_AB", "L0_gnn_att_src", "L0_gnn_att_dst"),
                       ("L1_gnn_AB1", "L1_gnn_a1_src", "L1_gnn_a1_dst"),
                       ("L1_gnn_AB2", "L1_gnn_a2_src", "L1_gnn_a2_dst")):
        h, c = x[s].shape
        block = np.zeros((256, 2 * h), x[s].dtype)
        for i in range(h):
            block[i * c:(i + 1) * c, i] = x[s][i]
            block[i * c:(i + 1) * c, h + i] = x[d][i]
        out[name] = block
    for name, keys in (("L0_ffn_C", ("L0_ffn_b1",)), ("L2_ffn_C", ("L2_ffn_b1", "L2_ffn_ln_g", "L2_ffn_ln_b")),
                       ("L3_ffn_C", ("L3_ffn_b1",))):
        parts = [x[k].reshape(8, -1, 128).transpose(0, 2, 1) for k in keys]
        both = np.concatenate(parts, axis=2)
        out[name] = np.ascontiguousarray(both.reshape(8 * 128, both.shape[2]))
    return out


def kernel(**inputs):
    import concourse.bacc as _bacc
    from concourse import mybir as _mybir
    from concourse.bass_utils import run_bass_kernel_spmd as _run

    nc = _bacc.Bacc("TRN2", target_bir_lowering=False, num_devices=1)
    arrays, args = {}, {}
    for name, v in laid_out(inputs).items():
        arrays[f"in_{name}"] = v
        args[name] = nc.dram_tensor(f"in_{name}", v.shape, _mybir.dt.from_np(v.dtype), kind="ExternalInput").ap()
    args["out"] = nc.dram_tensor("out_0", (3125, 256), _mybir.dt.float32, kind="ExternalOutput").ap()
    program(nc, args)
    r = _run(nc, [arrays], core_ids=[0])
    return r.results[0]["out_0"]
```
